# Optimizing a Trainium2 kernel written in Bass

```python
import numpy as np
import jax
import jax.numpy as jnp

def _softmax(x, axis=-1):
    return jax.nn.softmax(x, axis=axis)

def _gelu(x):
    return jax.nn.gelu(x, approximate=True)

def _silu(x):
    return jax.nn.silu(x)

def _sigmoid(x):
    return jax.nn.sigmoid(x)

def _layernorm(x, axis=-1, eps=1e-05):
    m = jnp.mean(x, axis=axis, keepdims=True)
    v = jnp.var(x, axis=axis, keepdims=True)
    return (x - m) / jnp.sqrt(v + eps)

def _scatter_add(tgt, idx, src, axis=0):
    return tgt.at[idx].add(src)

def _segment_sum(src, seg, n):
    return jax.ops.segment_sum(src, seg, n)
kernel_name = 'mk_vit_tower_d1_tok_img512_r4_0ab9c4'

def setup_inputs(seed: int=0):
    np.random.seed(seed)
    _w = jnp.asarray

    def _rec_inputs():
        import jax
        import jax.numpy as jnp
        _rk = jax.random.key(seed)
        x = -0.000147625 + 0.999875 * jax.random.normal(jax.random.fold_in(_rk, 1), (128, 3, 224, 224), jnp.float32)
        return x
    x = _rec_inputs()

    def _L0_tok_setup():
        import jax, jax.numpy as jnp
        import numpy as np
        N_PATCHES = 8
        PATCH = 28
        C = 3
        IN_D = C * PATCH * PATCH
        HID = 128
        SEQ = N_PATCHES * N_PATCHES + 1

        def _positional_embedding(seq_len, dim):
            i = np.arange(seq_len)[:, None].astype(np.float32)
            j = np.arange(dim)[None, :].astype(np.float32)
            ang = i / np.power(100000.0, j / dim)
            pe = np.where(j % 2 == 0, np.sin(ang), np.cos(ang))
            return jnp.asarray(pe, dtype=jnp.float32)
        key = jax.random.key(seed)
        k1, k2, k3, k4 = jax.random.split(key, 4)
        B = 64
        X = jax.random.normal(k1, (B, C, 224, 224), dtype=jnp.float32)
        bound = 1.0 / np.sqrt(IN_D)
        W = jax.random.uniform(k2, (HID, IN_D), minval=-bound, maxval=bound, dtype=jnp.float32)
        b = jax.random.uniform(k3, (HID,), minval=-bound, maxval=bound, dtype=jnp.float32)
        class_token = jax.random.uniform(k4, (1, HID), dtype=jnp.float32)
        pos_embed = _positional_embedding(SEQ, HID)
        return {'X': X, 'W': W, 'b': b, 'class_token': class_token, 'pos_embed': pos_embed}
    _L0_tok_all = _L0_tok_setup()
    _L0_tok_in = {k: v for k, v in _L0_tok_all.items() if k in ('W', 'b', 'class_token', 'pos_embed')}
    del _L0_tok_all

    def _L0_attn_setup():
        import jax, jax.numpy as jnp
        import numpy as np
        ATT_WINDOW = 64
        key = jax.random.key(seed)
        k1, k2 = jax.random.split(key)
        x = jax.random.normal(k1, (4, 512, 128), dtype=jnp.float32)
        W_c = jax.random.uniform(k2, (256, 128), minval=-0.05, maxval=0.05, dtype=jnp.float32)
        return {'x': x, 'W_c': W_c}
    _L0_attn_all = _L0_attn_setup()
    _L0_attn_in = {k: v for k, v in _L0_attn_all.items() if k in ('W_c',)}
    del _L0_attn_all

    def _L0_ffn_setup():
        import jax, jax.numpy as jnp
        import numpy as np
        B, S, D = (4, 256, 128)
        E = 16
        DH = 4 * D
        DS = 2 * D
        TOP_K = 2
        TEMP = 0.7
        SHARED_SCALE = 0.25
        EPS = 1e-05

        def layer_norm(x, g, b):
            mu = jnp.mean(x, axis=-1, keepdims=True)
            var = jnp.mean(jnp.square(x - mu), axis=-1, keepdims=True)
            return (x - mu) * jax.lax.rsqrt(var + EPS) * g + b
        key = jax.random.key(seed)
        ks = jax.random.split(key, 12)
        s = 0.02
        return {'x': jax.random.normal(ks[0], (B, S, D), jnp.float32), 'ln_in_g': jnp.ones((D,), jnp.float32), 'ln_in_b': jnp.zeros((D,), jnp.float32), 'router_w': jax.random.normal(ks[1], (D, E), jnp.float32) * s, 'router_b': jnp.zeros((E,), jnp.float32), 'ew1': jax.random.normal(ks[2], (E, D, DH), jnp.float32) * s, 'eb1': jnp.zeros((E, DH), jnp.float32), 'ew2': jax.random.normal(ks[3], (E, DH, D), jnp.float32) * s, 'eb2': jnp.zeros((E, D), jnp.float32), 'sw1': jax.random.normal(ks[4], (D, DS), jnp.float32) * s, 'sb1': jnp.zeros((DS,), jnp.float32), 'sw2': jax.random.normal(ks[5], (DS, D), jnp.float32) * s, 'sb2': jnp.zeros((D,), jnp.float32), 'ff_ln_g': jnp.ones((D,), jnp.float32), 'ff_ln_b': jnp.zeros((D,), jnp.float32), 'ff_w1': jax.random.normal(ks[6], (D, DH), jnp.float32) * s, 'ff_b1': jnp.zeros((DH,), jnp.float32), 'ff_w2': jax.random.normal(ks[7], (DH, D), jnp.float32) * s, 'ff_b2': jnp.zeros((D,), jnp.float32)}
    _L0_ffn_all = _L0_ffn_setup()
    _L0_ffn_in = {k: v for k, v in _L0_ffn_all.items() if k in ('ln_in_g', 'ln_in_b', 'router_w', 'router_b', 'ew1', 'eb1', 'ew2', 'eb2', 'sw1', 'sb1', 'sw2', 'sb2', 'ff_ln_g', 'ff_ln_b', 'ff_w1', 'ff_b1', 'ff_w2', 'ff_b2')}
    del _L0_ffn_all
    return {'x': x, 'L0_tok_W': _L0_tok_in['W'], 'L0_tok_b': _L0_tok_in['b'], 'L0_tok_class_token': _L0_tok_in['class_token'], 'L0_tok_pos_embed': _L0_tok_in['pos_embed'], 'L0_attn_W_c': _L0_attn_in['W_c'], 'L0_ffn_ln_in_g': _L0_ffn_in['ln_in_g'], 'L0_ffn_ln_in_b': _L0_ffn_in['ln_in_b'], 'L0_ffn_router_w': _L0_ffn_in['router_w'], 'L0_ffn_router_b': _L0_ffn_in['router_b'], 'L0_ffn_ew1': _L0_ffn_in['ew1'], 'L0_ffn_eb1': _L0_ffn_in['eb1'], 'L0_ffn_ew2': _L0_ffn_in['ew2'], 'L0_ffn_eb2': _L0_ffn_in['eb2'], 'L0_ffn_sw1': _L0_ffn_in['sw1'], 'L0_ffn_sb1': _L0_ffn_in['sb1'], 'L0_ffn_sw2': _L0_ffn_in['sw2'], 'L0_ffn_sb2': _L0_ffn_in['sb2'], 'L0_ffn_ff_ln_g': _L0_ffn_in['ff_ln_g'], 'L0_ffn_ff_ln_b': _L0_ffn_in['ff_ln_b'], 'L0_ffn_ff_w1': _L0_ffn_in['ff_w1'], 'L0_ffn_ff_b1': _L0_ffn_in['ff_b1'], 'L0_ffn_ff_w2': _L0_ffn_in['ff_w2'], 'L0_ffn_ff_b2': _L0_ffn_in['ff_b2']}

def reference(x, L0_tok_W, L0_tok_b, L0_tok_class_token, L0_tok_pos_embed, L0_attn_W_c, L0_ffn_ln_in_g, L0_ffn_ln_in_b, L0_ffn_router_w, L0_ffn_router_b, L0_ffn_ew1, L0_ffn_eb1, L0_ffn_ew2, L0_ffn_eb2, L0_ffn_sw1, L0_ffn_sb1, L0_ffn_sw2, L0_ffn_sb2, L0_ffn_ff_ln_g, L0_ffn_ff_ln_b, L0_ffn_ff_w1, L0_ffn_ff_b1, L0_ffn_ff_w2, L0_ffn_ff_b2):
    import jax
    import jax.numpy as jnp

    def _L0_tok_ref(X, W, b, class_token, pos_embed):
        import jax, jax.numpy as jnp
        import numpy as np
        N_PATCHES = 8
        PATCH = 28
        C = 3
        IN_D = C * PATCH * PATCH
        HID = 128
        SEQ = N_PATCHES * N_PATCHES + 1

        def _positional_embedding(seq_len, dim):
            i = np.arange(seq_len)[:, None].astype(np.float32)
            j = np.arange(dim)[None, :].astype(np.float32)
            ang = i / np.power(100000.0, j / dim)
            pe = np.where(j % 2 == 0, np.sin(ang), np.cos(ang))
            return jnp.asarray(pe, dtype=jnp.float32)
        B = X.shape[0]
        patches = X.reshape(B, C, N_PATCHES, PATCH, N_PATCHES, PATCH)
        patches = patches.transpose(0, 2, 4, 1, 3, 5).reshape(B, N_PATCHES * N_PATCHES, IN_D)
        tokens = jnp.einsum('bpi,hi->bph', patches, W) + b
        cls = jnp.broadcast_to(class_token[None, :, :], (B, 1, HID))
        tokens = jnp.concatenate([cls, tokens], axis=1)
        return tokens * pos_embed[None, :, :]

    def _L0_attn_ref(x, W_c):
        import jax, jax.numpy as jnp
        import numpy as np
        ATT_WINDOW = 64
        'Sliding-window (strictly-causal, left W steps) dot attention + output head.\n\n            Faithful to the original per-timestep loop: for step t, the window is the\n            W padded positions preceding the current one (zero-padded at the start),\n            score = <h_t, h_s>, softmax over window (padding zeros included, as in TF),\n            context c_t, then sigmoid(concat([c_t, h_t]) @ W_c).\n            '
        W = ATT_WINDOW
        B, S, D = x.shape
        h = jnp.pad(x, ((0, 0), (W, 0), (0, 0)))
        idx = jnp.arange(S)[:, None] + jnp.arange(W)[None, :]
        h_s = h[:, idx]
        scores = jnp.einsum('bsd,bswd->bsw', x, h_s)
        alpha = jax.nn.softmax(scores, axis=-1)
        c = jnp.einsum('bsw,bswd->bsd', alpha, h_s)
        concat_vec = jnp.concatenate([c, x], axis=-1)
        out = jax.nn.sigmoid(jnp.einsum('bsf,fo->bso', concat_vec, W_c))
        return out

    def _L0_ffn_ref(x, ln_in_g, ln_in_b, router_w, router_b, ew1, eb1, ew2, eb2, sw1, sb1, sw2, sb2, ff_ln_g, ff_ln_b, ff_w1, ff_b1, ff_w2, ff_b2):
        import jax, jax.numpy as jnp
        import numpy as np
        B, S, D = (4, 256, 128)
        E = 16
        DH = 4 * D
        DS = 2 * D
        TOP_K = 2
        TEMP = 0.7
        SHARED_SCALE = 0.25
        EPS = 1e-05

        def layer_norm(x, g, b):
            mu = jnp.mean(x, axis=-1, keepdims=True)
            var = jnp.mean(jnp.square(x - mu), axis=-1, keepdims=True)
            return (x - mu) * jax.lax.rsqrt(var + EPS) * g + b
        h = layer_norm(x, ln_in_g, ln_in_b)
        gate = jax.nn.softmax((h @ router_w + router_b) / TEMP, axis=-1)
        vals, idx = jax.lax.top_k(gate, TOP_K)
        comb = jnp.sum(jax.nn.one_hot(idx, E, dtype=h.dtype) * vals[..., None], axis=-2)
        eh = jax.nn.silu(jnp.einsum('bsd,edh->ebsh', h, ew1) + eb1[:, None, None, :])
        ey = jnp.einsum('ebsh,ehd->ebsd', eh, ew2) + eb2[:, None, None, :]
        mix = jnp.einsum('bse,ebsd->bsd', comb, ey)
        shared = (jax.nn.silu(h @ sw1 + sb1) @ sw2 + sb2) * SHARED_SCALE
        moe_out = mix + shared
        fh = layer_norm(moe_out, ff_ln_g, ff_ln_b)
        ff_out = jax.nn.silu(fh @ ff_w1 + ff_b1) @ ff_w2 + ff_b2
        return x + moe_out + ff_out
    h = _L0_tok_ref(x, L0_tok_W, L0_tok_b, L0_tok_class_token, L0_tok_pos_embed)
    h = h + _L0_attn_ref(_layernorm(h, axis=-1), L0_attn_W_c)
    h = h + _L0_ffn_ref(_layernorm(h, axis=-1), L0_ffn_ln_in_g, L0_ffn_ln_in_b, L0_ffn_router_w, L0_ffn_router_b, L0_ffn_ew1, L0_ffn_eb1, L0_ffn_ew2, L0_ffn_eb2, L0_ffn_sw1, L0_ffn_sb1, L0_ffn_sw2, L0_ffn_sb2, L0_ffn_ff_ln_g, L0_ffn_ff_ln_b, L0_ffn_ff_w1, L0_ffn_ff_b1, L0_ffn_ff_w2, L0_ffn_ff_b2)
    return h

_drawn_inputs = setup_inputs


def setup_inputs(seed=0):
    import zlib

    import numpy as np

    out = dict(_drawn_inputs(seed))
    spreads = {'L0_ffn_ln_in_g': (1.0, 0.6),
     'L0_ffn_ln_in_b': (0.0, 0.8),
     'L0_ffn_router_b': (0.0, 0.598),
     'L0_ffn_eb1': (0.0, 0.8),
     'L0_ffn_eb2': (0.0, 0.451),
     'L0_ffn_sb1': (0.0, 0.8),
     'L0_ffn_sb2': (0.0, 0.65),
     'L0_ffn_ff_ln_g': (1.0, 0.6),
     'L0_ffn_ff_ln_b': (0.0, 2.0),
     'L0_ffn_ff_b1': (0.0, 0.576),
     'L0_ffn_ff_b2': (0.0, 0.1)}
    factors = {'L0_ffn_router_w': 2.927,
     'L0_ffn_ew1': 5.601,
     'L0_ffn_ew2': 5.153,
     'L0_ffn_sw1': 4.889,
     'L0_ffn_sw2': 4.436}
    for name, (base, spread) in spreads.items():
        noise = np.random.default_rng([zlib.crc32(name.encode()), seed]).standard_normal(out[name].shape)
        drawn = base * np.exp(spread * noise) if base else spread * noise
        out[name] = jnp.asarray(drawn.astype(out[name].dtype))
    for name, factor in factors.items():
        out[name] = (out[name] * factor).astype(out[name].dtype)
    return out
```

```python
from contextlib import ExitStack

import numpy as np

import concourse.bass as bass
from concourse import mybir

F32 = mybir.dt.float32
BF16 = mybir.dt.bfloat16
U32 = mybir.dt.uint32
I32 = mybir.dt.int32
ALU = mybir.AluOpType
ACT = mybir.ActivationFunctionType
AX = mybir.AxisListType

P = 128
D = 128
BATCH, CH, IMG, PATCH = 128, 3, 224, 28
NP = IMG // PATCH
SEQ = NP * NP
KROWS = CH * PATCH
PATCH_TILES = BATCH * SEQ // P
TILES = PATCH_TILES + 1
GT = 4
GTOK = GT * P
GIMG = GTOK // SEQ
GROUPS = PATCH_TILES // GT
TOKENS = TILES * P
E, DH, DS = 16, 512, 256
EC, SC = DH // P, DS // P
TOPK = 2
TEMP = 0.7
SHARED = 0.25
EPS = 1e-5
EROWS = 256
EH = EROWS // P
CAP = -(-TOKENS // EROWS) * EROWS + EROWS
EXPERT_TILES = (TOKENS * TOPK + E * (EROWS - 1)) // EROWS
SPARE_TILES = EXPERT_TILES - TOKENS * TOPK // EROWS
ZROWS = E * CAP + SPARE_TILES * EROWS
XLOADS = GIMG * CH
N_LOADS = 19

C_ID, C_MASK, C_CLS, C_KEEP, C_IOTA, C_PREF, C_BASE, C_TILE = 0, 128, 192, 193, 194, 210, 338, 354
C_END = C_TILE + EXPERT_TILES

V_EB1, V_EB2 = 0, E * EC
V_SB1 = V_EB2 + E
V_SB2 = V_SB1 + SC
V_FB1 = V_SB2 + 1
V_FB2 = V_FB1 + EC
V_LG, V_LB, V_FG, V_FB, V_TB = V_FB2 + 1, V_FB2 + 2, V_FB2 + 3, V_FB2 + 4, V_FB2 + 5
V_END = V_TB + 1


def constants():
    c = np.zeros((P, C_END), np.float32)
    c[:, C_ID:C_ID + P] = np.eye(P)
    row = np.arange(P) % SEQ
    c[:, C_MASK:C_MASK + SEQ] = np.arange(SEQ)[None] < row[:, None]
    c[:, C_MASK + SEQ - 1] = 1
    c[:, C_CLS] = row == SEQ - 1
    c[:, C_KEEP] = row != SEQ - 1
    c[:, C_IOTA:C_IOTA + E] = np.arange(E)
    c[:, C_PREF:C_PREF + P] = np.arange(P)[:, None] < np.arange(P)[None]
    c[:, C_BASE:C_BASE + E] = np.arange(E) * CAP
    c[:, C_TILE:] = np.arange(EXPERT_TILES)
    return c


def build(nc, consts, x, tok_w, tok_b, cls_tok, pos, w_c, ln_g, ln_b, r_w, r_b, ew1, eb1, ew2, eb2,
          sw1, sb1, sw2, sb2, f_g, f_b, fw1, fb1, fw2, fb2, out):
    with ExitStack() as ctx:
        def sb(name, shape, dt=F32):
            return ctx.enter_context(nc.sbuf_tensor(name, shape, dt))

        def sem(name):
            return ctx.enter_context(nc.semaphore(name))

        def dram(name, shape, dt=F32):
            return nc.dram_tensor(name, shape, dt, kind="Internal").ap()

        z_rows = dram("z_rows", [ZROWS, D])
        y_rows = dram("y_rows", [EXPERT_TILES * EROWS, D])
        r_dram = dram("r_dram", [P, TILES, D])
        ht_dram = dram("ht_dram", [P, TILES, P])

        cst = sb("cst", [P, C_END])
        ident = cst[:, C_ID:C_ID + P]
        mask = cst[:, C_MASK:C_MASK + SEQ]
        iota = cst[:, C_IOTA:C_IOTA + E]
        pref = sb("pref", [P, P], BF16)
        ones = sb("ones", [P, P], BF16)
        neghalf = sb("neghalf", [P, 2 * GT])
        vecs = sb("vecs", [V_END, D])
        cols = sb("cols", [P, V_END])
        sb2q = sb("sb2q", [P, 1])
        wnat = sb("wnat", [P, CH, PATCH, PATCH])[:, :, :, :]
        pos_t = sb("pos_t", [P, D])
        wp = sb("wp", [KROWS, PATCH, D])
        wc = sb("wc", [P, 2, D])
        rw = sb("rw", [P, E])
        rb = sb("rb", [P, E])
        hcls = sb("hcls", [P, D])
        pos0 = sb("pos0", [P, D])
        xcls = sb("xcls", [P, D])
        xclsT = sb("xclsT", [P, P])
        vcls = sb("vcls", [P, D])
        pos_all = sb("pos_all", [P, TILES * TOPK])
        w_all = sb("w_all", [P, TILES * TOPK])
        shift = sb("shift", [P, TILES * TOPK])
        base = sb("base", [P, E])

        XCOLS = GIMG * NP * IMG
        region = sb("region", [P, 2 * XCOLS])
        xb = [region[0:KROWS, u * XCOLS:(u + 1) * XCOLS] for u in range(2)]
        carved = [0]

        def carve(n):
            carved[0] += n
            assert carved[0] <= 2 * XCOLS
            return region[:, carved[0] - n:carved[0]]

        W = EC * P
        w1b = [carve(W) for _ in range(4)]
        w2b = [carve(W).rearrange("p (c d) -> p c d", c=EC) for _ in range(4)]
        zin = [carve(EH * D).rearrange("p (h d) -> p h d", h=EH) for _ in range(4)]
        h2T = [carve(EROWS) for _ in range(2)]
        ehT = [carve(EC * EROWS).rearrange("p (c r) -> p c r", c=EC) for _ in range(2)]
        eyT = [carve(EROWS) for _ in range(2)]
        yout = [carve(EH * D).rearrange("p (h d) -> p h d", h=EH) for _ in range(2)]
        sw1_t = carve(DS)
        sw2_t = carve(SC * D).rearrange("p (c d) -> p c d", c=SC)
        fw1_t = carve(DH)
        fw2_t = carve(EC * D).rearrange("p (c d) -> p c d", c=EC)
        gat = [carve(GT * TOPK * D).rearrange("p (t k d) -> p t k d", t=GT, k=TOPK) for _ in range(2)]
        shs = carve(SC * GTOK).rearrange("p (c r) -> p c r", c=SC)
        shF = carve(GTOK)
        moe = carve(GT * D).rearrange("p (t d) -> p t d", t=GT)
        z4 = carve(GT * D).rearrange("p (t d) -> p t d", t=GT)
        h4T = carve(GTOK)
        ffs = carve(EC * GTOK).rearrange("p (c r) -> p c r", c=EC)
        oF = carve(GTOK)
        ht3 = [carve(GTOK) for _ in range(2)]
        r_res = carve(TILES * D)

        def tm(name):
            return sb(name, [P, GT, D])

        hF = sb("hF", [P, GTOK])
        h = tm("h")
        xh = tm("xh")
        vp = tm("vp")
        xT = sb("xT", [P, GTOK])
        s_t = sb("s_t", [P, GT, SEQ])
        e_t = sb("e_t", [P, GT, SEQ])
        a_bd = tm("a_bd")
        aT = sb("aT", [P, GTOK])
        cT = sb("cT", [P, GTOK])
        th = sb("th", [P, GTOK])
        h2 = tm("h2")
        z = [tm(f"z{u}") for u in range(2)]
        rr = [tm(f"rr{u}") for u in range(2)]
        hT = [sb(f"hT{u}", [P, GTOK]) for u in range(2)]
        st = sb("st", [P, GT, 6])
        mv = sb("mv", [P, GT, 2])
        var1 = sb("var1", [P, GT])
        rstd1 = sb("rstd1", [P, GT])
        var2 = sb("var2", [P, 2 * GT])
        rstd2 = sb("rstd2", [P, 2 * GT])
        rs1 = sb("rs1", [P, GT])
        rs2 = sb("rs2", [P, GT])
        mx = sb("mx", [P, GT])
        sm = sb("sm", [P, GT])
        rsm = sb("rsm", [P, GT])
        lg = sb("lg", [P, GT, E])
        m8 = sb("m8", [P, GT, 8])
        i8 = sb("i8", [P, GT, 8], U32)
        i2 = sb("i2", [P, GT * TOPK])
        d18 = sb("d18", [P, GT, E + TOPK])
        oh = sb("oh", [P, GT * TOPK, E])
        m2 = sb("m2", [P, GT, E], BF16)
        pp = sb("pp", [P, GT, TOPK, E])
        posf = sb("posf", [P, GT * TOPK])
        posg = [sb(f"posg{u}", [P, GT * TOPK], U32) for u in range(2)]
        gidx = [sb(f"gidx{u}", [P, GT * TOPK], U32) for u in range(2)]
        cnt = sb("cnt", [P, E])
        cnti = sb("cnti", [P, E], I32)
        nt = sb("nt", [P, E])
        nti = sb("nti", [P, E], I32)
        dsh = sb("dsh", [P, E])
        one_e = sb("one_e", [1, E])
        cum = sb("cum", [1, E])
        cmp = sb("cmp", [1, EXPERT_TILES, E])
        ej = sb("ej", [1, EXPERT_TILES])
        tj = sb("tj", [1, EXPERT_TILES])
        ejc = sb("ejc", [1, EXPERT_TILES], I32)
        rowj = sb("rowj", [1, EXPERT_TILES], I32)
        tail = sb("tail", [1, E], I32)
        zeros = sb("zeros", [P, EH * D])
        zsrc = zeros[:, :].rearrange("p (h d) -> p h d", h=EH)

        bank = [ctx.enter_context(nc.psum_tensor(f"bank{i}", [P, 512], F32)) for i in range(8)]

        def tiles_of(b, w=D):
            return bank[b][:, 0:GT * w].rearrange("p (t d) -> p t d", t=GT)

        pa = [bank[0], bank[1]]
        t1, t2, s_ps, t3 = tiles_of(2), bank[3], tiles_of(4, SEQ), bank[5]
        c_ps, w_ps, t4, t5 = bank[2], bank[3], tiles_of(4), bank[5]
        l_ps = bank[6][:, 0:GT * E].rearrange("p (t e) -> p t e", t=GT)
        p_ps = bank[7][:, 0:(GT + 1) * E].rearrange("p (t e) -> p t e", t=GT + 1)

        ld_const, ld_w = sem("ld_const"), sem("ld_w")
        memset_done, dve_setup = sem("memset_done"), sem("dve_setup")
        cls_var, cls_rstd, xcls_ready = sem("cls_var"), sem("cls_rstd"), sem("xcls_ready")
        setup_t, wp_t = sem("setup_t"), sem("wp_t")
        cols_ready, xclsT_ready, wp_ready = sem("cols_ready"), sem("xclsT_ready"), sem("wp_ready")
        x_loaded = [sem(f"x_loaded{u}") for u in range(2)]
        patch_done, hF_ready, t1_done, h_ready = sem("patch_done"), sem("hF_ready"), sem("t1_done"), sem("h_ready")
        var1_ready, rstd1_ready, xh_ready, vp_ready = sem("var1_ready"), sem("rstd1_ready"), sem("xh_ready"), sem("vp_ready")
        t2_done, xT_ready, s_done, smax_ready = sem("t2_done"), sem("xT_ready"), sem("s_done"), sem("smax_ready")
        e_ready, a_ready, t3_done, aT_ready = sem("e_ready"), sem("a_ready"), sem("t3_done"), sem("aT_ready")
        c_done, cT_ready, w_done, th_ready = sem("c_done"), sem("cT_ready"), sem("w_done"), sem("th_ready")
        t4_done, var2_ready, rstd2_ready, z_ready = sem("t4_done"), sem("var2_ready"), sem("rstd2_ready"), sem("z_ready")
        r_ready, t5_done, hT_ready, l_done = sem("r_ready"), sem("t5_done"), sem("hT_ready"), sem("l_done")
        gate_ready, gexp_ready, m2_ready, p_done, pos_ready = (
            sem("gate_ready"), sem("gexp_ready"), sem("m2_ready"), sem("p_done"), sem("pos_ready"))
        dve_step = sem("dve_step")
        r_free = [sem(f"r_free{u}") for u in range(2)]
        hT_free = [sem(f"hT_free{u}") for u in range(2)]
        z_free = [sem(f"z_free{u}") for u in range(2)]
        tab_step, tab_ready, spare_zeroed, tails_zeroed = sem("tab_step"), sem("tab_ready"), sem("spare_zeroed"), sem("tails_zeroed")
        ew_loaded = [sem(f"ew_loaded{u}") for u in range(4)]
        zin_loaded = [sem(f"zin_loaded{u}") for u in range(4)]
        tin_done, h2T_ready, up_done, eh_ready = sem("tin_done"), sem("h2T_ready"), sem("up_done"), sem("eh_ready")
        down_done, eyT_ready, tout_done, yout_ready = sem("down_done"), sem("eyT_ready"), sem("tout_done"), sem("yout_ready")
        y_free = [sem(f"y_free{u}") for u in range(2)]
        w3_loaded, r_loaded = sem("w3_loaded"), sem("r_loaded")
        ht_loaded = [sem(f"ht_loaded{u}") for u in range(2)]
        idx_ready, sb2q_ready = sem("idx_ready"), sem("sb2q_ready")
        gathered = [sem(f"gathered{u}") for u in range(2)]
        u_done, u_used = sem("u_done"), sem("u_used")
        shd_done, shF_ready, tsh_done, mix_done = sem("shd_done"), sem("shF_ready"), sem("tsh_done"), sem("mix_done")
        var4_ready, rstd4_ready, z4_ready, tz_done, h4T_ready = (
            sem("var4_ready"), sem("rstd4_ready"), sem("z4_ready"), sem("tz_done"), sem("h4T_ready"))
        ffd_done, oF_ready, tout3_done, out_ready, out_stored = (
            sem("ffd_done"), sem("oF_ready"), sem("tout3_done"), sem("out_ready"), sem("out_stored"))
        wait_carried = sem("wait_carried")
        dve_step3 = sem("dve_step3")
        DVE_STEPS, DVE_STEPS3 = 24, 4

        def bc(ap, shape):
            return ap.to_broadcast(shape)

        def groups(eng, first, last, body):
            assert (last - first) % 2 == 0
            with eng.Fori(0, (last - first) // 2) as i:
                for j in range(first, first + 2):
                    body(i * 2 + j, j % 2, i + j // 2)

        def one(body, g):
            body(g, g % 2, g // 2)

        def plain(eng):
            eng.sem_inc(wait_carried, 1)

        def col(n):
            return cols[:, n:n + 1]

        block = ctx.enter_context(nc.Block())

        @block.sync
        def _(sp):
            loads = [(cst[:, :], consts), (vecs[V_EB1:V_EB2], eb1.rearrange("e (c p) -> (e c) p", p=P)),
                     (vecs[V_EB2:V_SB1], eb2), (vecs[V_SB1:V_SB2], sb1.rearrange("(c p) -> c p", p=P)),
                     (vecs[V_SB2:V_FB1], sb2.unsqueeze(0)), (vecs[V_FB1:V_FB2], fb1.rearrange("(c p) -> c p", p=P)),
                     (vecs[V_FB2:V_LG], fb2.unsqueeze(0)), (vecs[V_LG:V_LB], ln_g.unsqueeze(0)),
                     (vecs[V_LB:V_FG], ln_b.unsqueeze(0)), (vecs[V_FG:V_FB], f_g.unsqueeze(0)),
                     (vecs[V_FB:V_TB], f_b.unsqueeze(0)), (vecs[V_TB:V_END], tok_b.unsqueeze(0)),
                     (pos_t[0:SEQ], pos[1:SEQ + 1]), (pos_t[SEQ:P], pos[1:SEQ + 1]),
                     (hcls[:, :], cls_tok[0].partition_broadcast(P)), (pos0[:, :], pos[0].partition_broadcast(P)),
                     (wc[:, :, :], w_c.rearrange("(k f) o -> f k o", k=2)), (rw[:, :], r_w),
                     (rb[:, :], r_b.partition_broadcast(P))]
            assert len(loads) == N_LOADS

            def load_x(g, k, h):
                dst = xb[k].rearrange("p (b n w) -> p b n w", b=GIMG, n=NP)
                for c in range(CH):
                    for b in range(GIMG):
                        src = x[bass.ds(g * GIMG + b, 1), c].rearrange("o (n y) w -> y (o n) w", y=PATCH)
                        sp.dma_start(dst[c * PATCH:(c + 1) * PATCH, b], src).then_inc(x_loaded[k], 16)

            def reload_x(g, k, h):
                sp.wait_ge(patch_done, g - 1)
                load_x(g, k, h)

            def stores(g, k, h, nt=GT):
                sp.wait_ge(r_ready, g + 1)
                sp.dma_start(r_dram[:, bass.ds(g * GT, nt)], rr[k][:, 0:nt]).then_inc(r_free[k], 16)
                sp.wait_ge(hT_ready, g + 1)
                sp.dma_start(ht_dram[:, bass.ds(g * GT, nt)],
                             hT[k][:, 0:nt * P].rearrange("p (t c) -> p t c", t=nt)).then_inc(hT_free[k], 16)

            sp.dma_start(wnat, tok_w.rearrange("h (c y x) -> h c y x", c=CH, y=PATCH)).then_inc(ld_w, 16)
            load_x(0, 0, 0)
            for dst, src in loads:
                sp.dma_start(dst, src).then_inc(ld_const, 16)
            load_x(1, 1, 0)
            for k in range(2):
                sp.sem_inc(r_free[k], 16)
                sp.sem_inc(hT_free[k], 16)
            sp.wait_ge(memset_done, 2)
            for s in range(2, SPARE_TILES):
                at = E * CAP + s * EROWS
                sp.dma_start(z_rows[at:at + EROWS].rearrange("(h p) d -> p h d", p=P), zsrc).then_inc(spare_zeroed, 16)

            def step(g, k, h):
                reload_x(g + 2, k, h + 1)
                stores(g, k, h)

            groups(sp, 0, GROUPS - 2, step)
            one(stores, GROUPS - 2)
            one(stores, GROUPS - 1)
            stores(GROUPS, 0, GROUPS // 2, 1)

            sp.wait_ge(tab_ready, 1)
            with sp.Fori(0, E) as e:
                row = sp.value_load(tail[0:1, bass.ds(e, 1)], min_val=0, max_val=ZROWS - EROWS)
                sp.dma_start(z_rows[bass.ds(row, EROWS)].rearrange("(h p) d -> p h d", p=P), zsrc)\
                  .then_inc(tails_zeroed, 16)
            sp.wait_ge(z_free[0], 16 + 16 * TOPK * (GT * GROUPS // 2 + 1))
            sp.wait_ge(z_free[1], 16 + 16 * TOPK * GT * GROUPS // 2)
            sp.wait_ge(tails_zeroed, 16 * E)
            sp.wait_ge(spare_zeroed, 16 * (SPARE_TILES - 2))
            sp.wait_ge(patch_done, GROUPS)

            def expert_loads(j, n):
                ex = sp.value_load(ejc[0:1, bass.ds(j, 1)], min_val=0, max_val=E - 1)
                row = sp.value_load(rowj[0:1, bass.ds(j, 1)], min_val=0, max_val=ZROWS - EROWS)
                sp.wait_ge(down_done, j - 3) if n >= 4 else None
                sp.dma_start(zin[n % 4], z_rows[bass.ds(row, EROWS)].rearrange("(h p) d -> p h d", p=P))\
                  .then_inc(zin_loaded[n % 4], 16)
                sp.dma_start(w1b[n % 4], ew1[bass.ds(ex, 1)].rearrange("o d h -> d (o h)")).then_inc(ew_loaded[n % 4], 16)
                sp.dma_start(w2b[n % 4], ew2[bass.ds(ex, 1)].rearrange("o (c p) d -> p (o c) d", p=P))\
                  .then_inc(ew_loaded[n % 4], 16)

            for j in range(4):
                expert_loads(j, j)
            for k in range(2):
                sp.wait_ge(r_free[k], 16 + 16 * (GROUPS // 2 + 1 - k))
                sp.wait_ge(hT_free[k], 16 + 16 * (GROUPS // 2 + 1 - k))
            for dst, src in ((sw1_t, sw1), (sw2_t, sw2.rearrange("(c p) d -> p c d", p=P)), (fw1_t, fw1),
                             (fw2_t, fw2.rearrange("(c p) d -> p c d", p=P))):
                sp.dma_start(dst, src).then_inc(w3_loaded, 16)
            sp.dma_start(r_res, r_dram.rearrange("p t d -> p (t d)")).then_inc(r_loaded, 16)
            for q in range(2):
                sp.dma_start(ht3[q], ht_dram[:, q * GT:(q + 1) * GT].rearrange("p t c -> p (t c)")).then_inc(ht_loaded[q], 16)
            with sp.Fori(1, EXPERT_TILES // 4) as i:
                for n in range(4):
                    expert_loads(i * 4 + n, 4 + n)

            def load_ht(q, k, n, nt=GT):
                sp.wait_ge(u_done, n)
                sp.dma_start(ht3[k][:, 0:nt * P].rearrange("p (t c) -> p t c", t=nt),
                             ht_dram[:, bass.ds(q * GT, nt)]).then_inc(ht_loaded[k], 16)

            def store_out(q, nt=GT):
                sp.wait_ge(out_ready, q + 2)
                res = r_res.rearrange("p (t d) -> p t d", d=D)
                for t in range(nt):
                    if nt == GT:
                        dst = out[bass.ds(q * GIMG + 2 * t, 2), 1:SEQ + 1]
                    else:
                        dst = out[:, 0]
                    sp.dma_start(dst, res[:, bass.ds(q * GT + t, 1)].rearrange("p o d -> p (o d)"))\
                      .then_inc(out_stored, 16)

            def step3(q, k, h):
                store_out(q)
                load_ht(q + 5, (k + 5) % 2, q * 6 + 12)

            for q in range(2, 5):
                load_ht(q, q % 2, SC * (q - 1))
            groups(sp, 0, GROUPS - 6, step3)
            one(step3, GROUPS - 6)
            store_out(GROUPS - 5)
            load_ht(GROUPS, 0, (GROUPS - 5) * 6 + 12, 1)
            for q in range(GROUPS - 4, GROUPS):
                store_out(q)
            store_out(GROUPS, 1)
            sp.wait_ge(out_stored, 16 * TILES)

        @block.scalar
        def _(act):
            act.wait_ge(setup_t, 1)
            act.activation(cols[:, :], bank[7][:, 0:V_END], ACT.Copy).then_inc(cols_ready, 1)
            for b in range(PATCH // 4):
                act.wait_ge(wp_t, b + 1)
                act.activation(wp[:, 4 * b:4 * b + 4].rearrange("p x h -> p (x h)"), bank[b][0:KROWS, :], ACT.Copy)\
                   .then_inc(wp_ready, 1)
            act.wait_ge(setup_t, 2)
            act.activation(xclsT[:, :], bank[7][:, P:2 * P], ACT.Copy).then_inc(xclsT_ready, 1)
            act.wait_ge(cols_ready, 1)

            def tail_of(g, k, h, nt):
                act.wait_ge(w_done, g + 1)
                act.activation(th[:, 0:nt * P], w_ps[:, 0:nt * P], ACT.Tanh, scale=0.5).then_inc(th_ready, 1)
                act.wait_ge(hT_free[k], h * 16 + 16)
                act.wait_ge(t5_done, g + 1)
                act.activation(hT[k][:, 0:nt * P], t5[:, 0:nt * P], ACT.Identity, scale=col(V_LG), bias=col(V_LB))\
                   .then_inc(hT_ready, 1)
                act.wait_ge(gate_ready, g + 1)
                act.activation(d18[:, 0:nt], d18[:, 0:nt], ACT.Exp, scale=1.0 / TEMP).then_inc(gexp_ready, 1)

            def group(g, k, h):
                act.wait_ge(patch_done, g + 1)
                act.activation(hF[:, :], pa[k][:, :], ACT.Identity, bias=col(V_TB)).then_inc(hF_ready, 1)
                act.wait_ge(t2_done, g + 1)
                act.activation(xT[:, :], t2[:, :], ACT.Copy).then_inc(xT_ready, 1)
                act.wait_ge(smax_ready, g + 1)
                act.activation(e_t[:, :, :], s_t[:, :, :], ACT.Exp).then_inc(e_ready, 1)
                act.wait_ge(t3_done, g + 1)
                act.activation(aT[:, :], t3[:, :], ACT.Copy).then_inc(aT_ready, 1)
                act.wait_ge(c_done, g + 1)
                act.activation(cT[:, :], c_ps[:, :], ACT.Copy).then_inc(cT_ready, 1)
                tail_of(g, k, h, GT)

            groups(act, 0, GROUPS, group)
            tail_of(GROUPS, 0, GROUPS // 2, 1)

            def take_in(j, n):
                act.wait_ge(tin_done, j + 1)
                act.activation(h2T[n % 2], bank[0][:, 0:EROWS], ACT.Identity, scale=col(V_LG), bias=col(V_LB))\
                   .then_inc(h2T_ready, 1)

            def silus(j, n):
                ex = act.value_load(ejc[0:1, bass.ds(j, 1)], min_val=0, max_val=E - 1)
                bias = [cols[:, bass.ds(ex * EC + c, 1)] for c in range(EC)]
                for c in range(EC):
                    act.wait_ge(up_done, j * EC + c + 1)
                    act.activation(ehT[n % 2][:, c], bank[1 + c][:, 0:EROWS], ACT.Silu, bias=bias[c])\
                       .then_inc(eh_ready, 1)

            act.wait_ge(tab_ready, 1)
            take_in(0, 0)
            with act.Fori(0, EXPERT_TILES // 4 - 1) as i:
                for n in range(4):
                    take_in(i * 4 + n + 1, n + 1)
                    silus(i * 4 + n, n)
            for j in range(EXPERT_TILES - 4, EXPERT_TILES):
                if j + 1 < EXPERT_TILES:
                    take_in(j + 1, j + 1)
                silus(j, j)

            def silu3(n, b, dst, bias, w):
                act.wait_ge(u_done, n + 1)
                act.activation(dst[:, 0:w], bank[b][:, 0:w], ACT.Silu, bias=bias).then_inc(u_used, 1)

            def sh_silu(q, n, nt=GT):
                for c in range(SC):
                    silu3(n + c, (4 + c) % 3, shs[:, c], col(V_SB1 + c), nt * P)

            def sh_out(q, nt=GT):
                act.wait_ge(shd_done, q + 1)
                act.activation(shF[:, 0:nt * P], bank[3][:, 0:nt * P], ACT.Identity, scale=SHARED, bias=sb2q[:, 0:1])\
                   .then_inc(shF_ready, 1)

            def z_in(q, nt=GT):
                act.wait_ge(tz_done, q + 1)
                act.activation(h4T[:, 0:nt * P], bank[5][:, 0:nt * P], ACT.Identity, scale=col(V_FG), bias=col(V_FB))\
                   .then_inc(h4T_ready, 1)

            def ff_silu(q, n, nt=GT):
                for c in range(EC):
                    silu3(n + c, c % 3, ffs[:, c], col(V_FB1 + c), nt * P)

            def ff_out(q, nt=GT):
                act.wait_ge(ffd_done, q + 1)
                act.activation(oF[:, 0:nt * P], bank[4][:, 0:nt * P], ACT.Identity, bias=col(V_FB2)).then_inc(oF_ready, 1)

            act.wait_ge(sb2q_ready, 1)
            for q in range(3):
                sh_silu(q, 2 * q)
                if q < 2:
                    sh_out(q)
            z_in(0)

            def step3(q, sh3=GT, sh2=GT, z1=GT, now=GT, n=None):
                n = q * 6 + 6 if n is None else n
                ff_silu(q, n, now)
                if sh2:
                    sh_out(q + 2, sh2)
                if z1:
                    z_in(q + 1, z1)
                ff_out(q, now)
                if sh3:
                    sh_silu(q + 3, n + 4, sh3)

            with act.Fori(0, GROUPS - 3) as q:
                step3(q)
            step3(GROUPS - 3, sh3=1)
            last = (GROUPS - 3) * 6 + 12
            step3(GROUPS - 2, sh3=0, sh2=1, n=last)
            step3(GROUPS - 1, sh3=0, sh2=0, z1=1, n=last + EC)
            step3(GROUPS, sh3=0, sh2=0, z1=0, now=1, n=last + 2 * EC)

        @block.gpsimd
        def _(pool):
            pool.memset(neghalf[:, :], -0.5).then_inc(memset_done, 1)
            def rstd(var_ready, n, dst, var, ready):
                pool.wait_ge(var_ready, n)
                pool.tensor_tensor(dst, var, neghalf[:, 0:var.shape[1]], ALU.pow).then_inc(ready, 1)

            pool.wait_ge(memset_done, 2)
            for u in range(2):
                at = E * CAP + u * EROWS
                pool.dma_start(z_rows[at:at + EROWS].rearrange("(h p) d -> p h d", p=P), zsrc).then_inc(z_free[u], 16)
            rstd(cls_var, 1, rstd1[:, 0:1], var1[:, 0:1], cls_rstd)

            def scatter(g, k, nt=GT):
                pool.wait_ge(z_ready, g + 1)
                pool.wait_ge(pos_ready, g + 1)
                plain(pool)
                for t in range(nt):
                    for s in range(TOPK):
                        n = t * TOPK + s
                        pool.indirect_dma_start(z_rows, bass.IndirectOffsetOnAxis(posg[k][:, n:n + 1], 0),
                                                z[k][:, t], None).then_inc(z_free[k], 16)

            def norms(g):
                rstd(var2_ready, g + 1, rstd2[:, :], var2[:, :], rstd2_ready)

            def step(g, k, h):
                rstd(var1_ready, g + 1, rstd1[:, :], var1[:, :], rstd1_ready)
                scatter(g - 1, (k + 1) % 2)
                norms(g)

            rstd(var1_ready, 1, rstd1[:, :], var1[:, :], rstd1_ready)
            norms(0)
            groups(pool, 1, GROUPS - 1, step)
            one(step, GROUPS - 1)
            scatter(GROUPS - 1, 1)
            norms(GROUPS)
            scatter(GROUPS, 0, 1)


            def store_y(j, k, h):
                pool.wait_ge(yout_ready, j + 1)
                plain(pool)
                pool.dma_start(y_rows[bass.ds(j * EROWS, EROWS)].rearrange("(h p) d -> p h d", p=P), yout[k])\
                    .then_inc(y_free[k], 16)

            groups(pool, 0, EXPERT_TILES, store_y)
            for k in range(2):
                pool.wait_ge(y_free[k], 16 * (EXPERT_TILES // 2))

            def gather(q, k, nt=GT):
                pool.wait_ge(idx_ready, q + 1)
                plain(pool)
                for t in range(nt):
                    for s in range(TOPK):
                        n = t * TOPK + s
                        pool.indirect_dma_start(gat[k][:, t, s], None, y_rows,
                                                bass.IndirectOffsetOnAxis(gidx[k][:, n:n + 1], 0))\
                            .then_inc(gathered[k], 16)

            def norms3(q):
                rstd(var4_ready, q + 1, rstd1[:, :], var1[:, :], rstd4_ready)

            def step3(q, k, h):
                gather(q + 3, (k + 3) % 2)
                norms3(q + 2)

            gather(0, 0)
            gather(1, 1)
            norms3(0)
            gather(2, 0)
            norms3(1)
            groups(pool, 0, GROUPS - 4, step3)
            one(step3, GROUPS - 4)
            gather(GROUPS, 0, 1)
            for q in range(GROUPS - 1, GROUPS + 1):
                norms3(q)

        @block.vector
        def _(dve):
            dve.memset(ones[:, :], 1.0)
            dve.memset(a_bd[:, :, :], 0.0)
            dve.memset(zeros[:, :], 0.0)
            dve.memset(one_e[:, :], 1.0)
            for buf in (var1, var2):
                dve.memset(buf[:, :], 1.0)
            dve.memset(rstd2[:, :], 1.0).then_inc(memset_done, 1)
            dve.wait_ge(ld_const, 16 * N_LOADS)
            n = [0]

            def link(ins):
                n[0] += 1
                ins.then_inc(dve_setup, 1)

            def settle():
                dve.wait_ge(dve_setup, n[0])

            link(dve.tensor_copy(pref[:, :], cst[:, C_PREF:C_PREF + P]))
            link(dve.tensor_copy(base[:, :], cst[:, C_BASE:C_BASE + E]))
            link(dve.tensor_tensor(hcls[:, :], hcls[:, :], pos0[:, :], ALU.mult))
            settle()
            link(dve.bn_stats(st[:, 0], hcls[:, :]))
            settle()
            link(dve.bn_aggr(mv[:, 0], st[:, 0]))
            settle()
            dve.tensor_scalar(var1[:, 0:1], mv[:, 0, 1:2], EPS, None, ALU.add).then_inc(cls_var, 1)
            dve.wait_ge(cls_rstd, 1)
            dve.tensor_scalar(xcls[:, :], hcls[:, :], mv[:, 0, 0:1], rstd1[:, 0:1], ALU.subtract, ALU.mult)\
               .then_inc(xcls_ready, 1)
            dve.wait_ge(xcls_ready, 1)
            link(dve.tensor_scalar(vcls[:, :], xcls[:, :], cst[:, C_CLS:C_CLS + 1], None, ALU.mult))
            dve.wait_ge(cols_ready, 1)
            dve.tensor_scalar(sb2q[:, :], col(V_SB2), SHARED, None, ALU.mult).then_inc(sb2q_ready, 1)
            settle()

            def stats(src, nt, link, settle):
                for t in range(nt):
                    ins = dve.bn_stats(st[:, t], src(t))
                link(ins)
                settle()
                plain(dve)
                for t in range(nt):
                    ins = dve.bn_aggr(mv[:, t], st[:, t])
                link(ins)
                settle()

            def normalise(dst, src, scale, nt):
                for t in range(nt):
                    ins = dve.tensor_scalar(dst[:, t], src[:, t], mv[:, t, 0:1], scale[:, t:t + 1],
                                            ALU.subtract, ALU.mult)
                return ins

            def attend(g, k, h_, link, settle):
                dve.wait_ge(t1_done, g + 1)
                dve.tensor_tensor(h[:, :, :], t1, bc(pos_t[:, :].unsqueeze(1), [P, GT, D]), ALU.mult)\
                   .then_inc(h_ready, 1)
                dve.wait_ge(h_ready, g + 1)
                stats(lambda t: h[:, t], GT, link, settle)
                dve.tensor_scalar(var1[:, :], mv[:, :, 1], EPS, None, ALU.add).then_inc(var1_ready, 1)
                dve.wait_ge(rstd1_ready, g + 1)
                normalise(xh, h, rstd1, GT).then_inc(xh_ready, 1)
                dve.wait_ge(xh_ready, g + 1)
                dve.scalar_tensor_tensor(out=vp[:, :, :], in0=xh[:, :, :], scalar=cst[:, C_KEEP:C_KEEP + 1],
                                         in1=bc(vcls[:, :].unsqueeze(1), [P, GT, D]), op0=ALU.mult,
                                         op1=ALU.add).then_inc(vp_ready, 1)
                mask3 = bc(mask.unsqueeze(1), [P, GT, SEQ])
                dve.wait_ge(s_done, g + 1)
                link(dve.tensor_tensor(s_t[:, :, :], s_ps, mask3, ALU.mult))
                settle()
                link(dve.tensor_reduce(mx[:, :], s_t[:, :, :], AX.X, ALU.max))
                settle()
                dve.tensor_tensor(s_t[:, :, :], s_t[:, :, :], bc(mx[:, :].unsqueeze(2), [P, GT, SEQ]),
                                  ALU.subtract).then_inc(smax_ready, 1)
                dve.wait_ge(e_ready, g + 1)
                link(dve.tensor_reduce(sm[:, :], e_t[:, :, :], AX.X, ALU.add))
                link(dve.tensor_tensor(s_t[:, :, :], e_t[:, :, :], mask3, ALU.mult))
                settle()
                link(dve.reciprocal(rsm[:, :], sm[:, :]))
                settle()
                for i in range(2):
                    q = slice(i * SEQ, (i + 1) * SEQ)
                    ins = dve.tensor_tensor(a_bd[q, :, q], s_t[q], bc(rsm[q, :].unsqueeze(2), [SEQ, GT, SEQ]), ALU.mult)
                ins.then_inc(a_ready, 1)

            def route(g, k, h_, nt, link, settle):
                dve.wait_ge(t4_done, g + 1)
                src = h[:, 0:nt] if nt == GT else hcls[:, :].unsqueeze(1)
                link(dve.scalar_tensor_tensor(out=h2[:, 0:nt], in0=t4[:, 0:nt], scalar=0.5, in1=src,
                                              op0=ALU.mult, op1=ALU.add))
                settle()
                stats(lambda t: h2[:, t], nt, link, settle)
                dve.tensor_scalar(var2[:, 0:nt], mv[:, 0:nt, 1], EPS, None, ALU.add)
                dve.tensor_scalar(var2[:, GT:GT + nt], mv[:, 0:nt, 1], 1.0 + EPS, EPS * EPS, ALU.mult, ALU.add)\
                   .then_inc(var2_ready, 1)
                dve.wait_ge(rstd2_ready, g + 1)
                dve.wait_ge(z_free[k], h_ * (16 * TOPK * GT) + 16)
                normalise(z[k], h2, rstd2[:, GT:2 * GT], nt).then_inc(z_ready, 1)
                link(dve.tensor_scalar(rs1[:, 0:nt], rstd2[:, 0:nt], 1.0, None, ALU.add))
                link(dve.tensor_tensor(rs2[:, 0:nt], mv[:, 0:nt, 0], rstd2[:, 0:nt], ALU.mult))
                settle()
                link(dve.tensor_scalar(rs2[:, 0:nt], rs2[:, 0:nt], -1.0, 0.5, ALU.mult, ALU.add))
                settle()
                dve.wait_ge(r_free[k], h_ * 16 + 16)
                for t in range(nt):
                    ins = dve.tensor_scalar(rr[k][:, t], h2[:, t], rs1[:, t:t + 1], rs2[:, t:t + 1], ALU.mult, ALU.add)
                ins.then_inc(r_ready, 1)
                dve.wait_ge(l_done, g + 1)
                link(dve.tensor_tensor(lg[:, 0:nt], l_ps[:, 0:nt], bc(rb[:, :].unsqueeze(1), [P, nt, E]), ALU.add))
                settle()
                plain(dve)
                for t in range(nt):
                    ins = dve.max(m8[:, t], lg[:, t])
                link(ins)
                settle()
                plain(dve)
                for t in range(nt):
                    ins = dve.max_index(i8[:, t], m8[:, t], lg[:, t])
                link(ins)
                top = m8[:, 0:nt, 0:1]
                dve.tensor_tensor(d18[:, 0:nt, 0:E], lg[:, 0:nt], bc(top, [P, nt, E]), ALU.subtract)
                dve.tensor_tensor(d18[:, 0:nt, E:E + TOPK], m8[:, 0:nt, 0:TOPK], bc(top, [P, nt, TOPK]),
                                  ALU.subtract).then_inc(gate_ready, 1)
                settle()
                nk = nt * TOPK
                link(dve.tensor_copy(i2[:, 0:nk].rearrange("p (t k) -> p t k", k=TOPK), i8[:, 0:nt, 0:TOPK]))
                settle()
                link(dve.tensor_tensor(oh[:, 0:nk], bc(iota.unsqueeze(1), [P, nk, E]),
                                       bc(i2[:, 0:nk].unsqueeze(2), [P, nk, E]), ALU.is_equal))
                settle()
                oh4 = oh[:, 0:nk].rearrange("p (t k) e -> p t k e", k=TOPK)
                dve.tensor_tensor(m2[:, 0:nt], oh4[:, :, 0], oh4[:, :, 1], ALU.add).then_inc(m2_ready, 1)
                dve.wait_ge(gexp_ready, g + 1)
                link(dve.tensor_reduce(sm[:, 0:nt], d18[:, 0:nt, 0:E], AX.X, ALU.add))
                settle()
                link(dve.reciprocal(rsm[:, 0:nt], sm[:, 0:nt]))
                settle()
                w_out = w_all[:, bass.ds(g * (GT * TOPK), nk)].rearrange("p (t k) -> p t k", k=TOPK)
                dve.tensor_tensor(w_out, d18[:, 0:nt, E:E + TOPK], bc(rsm[:, 0:nt].unsqueeze(2), [P, nt, TOPK]), ALU.mult)
                dve.wait_ge(p_done, g + 1)
                base4 = bc(base[:, :].unsqueeze(1), [P, nt, E])
                for s in range(TOPK):
                    ins = dve.tensor_tensor(pp[:, 0:nt, s], p_ps[:, 0:nt], base4, ALU.add)
                link(ins)
                settle()
                link(dve.tensor_tensor(base[:, :], base[:, :], p_ps[:, nt], ALU.add))
                pk = pp[:, 0:nt].rearrange("p t k e -> p (t k) e")
                link(dve.tensor_tensor(pk, pk, oh[:, 0:nk], ALU.mult))
                settle()
                link(dve.tensor_reduce(posf[:, 0:nk], pk, AX.X, ALU.add))
                settle()
                dve.tensor_copy(pos_all[:, bass.ds(g * (GT * TOPK), nk)], posf[:, 0:nk])
                dve.tensor_copy(posg[k][:, 0:nk], posf[:, 0:nk]).then_inc(pos_ready, 1)

            def body(g, k, h_, nt=GT):
                m = [0]

                def link(ins):
                    m[0] += 1
                    ins.then_inc(dve_step, 1)

                def settle():
                    dve.wait_ge(dve_step, g * DVE_STEPS + m[0])

                if nt == GT:
                    attend(g, k, h_, link, settle)
                route(g, k, h_, nt, link, settle)
                assert m[0] == DVE_STEPS or nt < GT, m[0]
                return m[0]

            groups(dve, 0, GROUPS, body)
            steps = GROUPS * DVE_STEPS + body(GROUPS, 0, GROUPS // 2, 1)
            dve.wait_ge(dve_step, steps)
            n[0] = 0

            def tlink(ins):
                n[0] += 1
                ins.then_inc(tab_step, 1)
                dve.wait_ge(tab_step, n[0])

            ebase = cst[:, C_BASE:C_BASE + E]
            tlink(dve.tensor_copy(tail[:, :], base[0:1, :]))
            tlink(dve.tensor_tensor(cnt[:, :], base[:, :], ebase, ALU.subtract))
            tlink(dve.tensor_scalar(cnti[:, :], cnt[:, :], float(EROWS - 1), None, ALU.add))
            tlink(dve.tensor_scalar(nti[:, :], cnti[:, :], EROWS.bit_length() - 1, None, ALU.arith_shift_right))
            tlink(dve.tensor_copy(nt[:, :], nti[:, :]))
            tlink(dve.tensor_tensor_scan(cum[:, :], one_e[:, :], nt[0:1, :], 0.0, ALU.mult, ALU.add))
            tile_no = cst[0:1, C_TILE:C_TILE + EXPERT_TILES]
            full = [1, EXPERT_TILES, E]
            tlink(dve.tensor_tensor(cmp[:, :, :], bc(tile_no.unsqueeze(2), full), bc(cum[:, :].unsqueeze(1), full), ALU.is_ge))
            tlink(dve.tensor_reduce(ej[:, :], cmp[:, :, :], AX.X, ALU.add))
            tlink(dve.tensor_tensor(cmp[:, :, :], cmp[:, :, :], bc(nt[0:1, :].unsqueeze(1), full), ALU.mult))
            tlink(dve.tensor_reduce(tj[:, :], cmp[:, :, :], AX.X, ALU.add))
            tlink(dve.tensor_tensor(tj[:, :], tile_no, tj[:, :], ALU.subtract))
            tlink(dve.tensor_scalar(ejc[:, :], ej[:, :], float(E - 1), None, ALU.min))
            tlink(dve.tensor_scalar(tj[:, :], tj[:, :], float(EROWS), None, ALU.mult))
            dve.scalar_tensor_tensor(out=rowj[:, :], in0=ej[:, :], scalar=float(CAP), in1=tj[:, :], op0=ALU.mult,
                                     op1=ALU.add).then_inc(tab_ready, 1)

            slots = TILES * TOPK
            grid = [P, slots, E]
            cmpa = wnat.rearrange("h c y x -> h (c y x)")[:, 0:slots * E].rearrange("p (s e) -> p s e", e=E)
            tlink(dve.memset(dsh[:, :], 0.0))
            tlink(dve.tensor_scalar(dsh[:, 1:E], nt[:, 0:E - 1], float(EROWS), float(-CAP), ALU.mult, ALU.add))
            tlink(dve.tensor_tensor(cmpa, bc(pos_all[:, :].unsqueeze(2), grid), bc(ebase.unsqueeze(1), grid), ALU.is_ge))
            tlink(dve.tensor_tensor(cmpa, cmpa, bc(dsh[:, :].unsqueeze(1), grid), ALU.mult))
            tlink(dve.tensor_reduce(shift[:, :], cmpa, AX.X, ALU.add))
            tlink(dve.tensor_tensor(pos_all[:, :], pos_all[:, :], shift[:, :], ALU.add))

            dve.wait_ge(tab_ready, 1)

            def down_bias(j, n):
                ex = dve.value_load(ejc[0:1, bass.ds(j, 1)], min_val=0, max_val=E - 1)
                bias = cols[:, bass.ds(ex + V_EB2, 1)]
                dve.wait_ge(down_done, j + 1)
                dve.tensor_scalar(eyT[n % 2], bank[5 + n % 2][:, 0:EROWS], bias, None, ALU.add).then_inc(eyT_ready, 1)

            def rows_out(j, n, h_):
                if not (isinstance(h_, int) and h_ == 0):
                    dve.wait_ge(y_free[n % 2], h_ * 16)
                dve.wait_ge(tout_done, j + 1)
                dve.tensor_copy(yout[n % 2], bank[7][:, 0:EROWS].rearrange("p (h d) -> p h d", h=EH)).then_inc(yout_ready, 1)

            def step2(j, n, h_):
                rows_out(j - 1, n + 1, h_)
                down_bias(j, n)

            down_bias(0, 0)
            for j in (1, 2):
                step2(j, j, 0)
            with dve.Fori(1, (EXPERT_TILES - 2) // 2) as i:
                step2(i * 2 + 1, 1, i)
                step2(i * 2 + 2, 2, i)
            step2(EXPERT_TILES - 1, 1, EXPERT_TILES // 2 - 1)
            rows_out(EXPERT_TILES - 1, 1, EXPERT_TILES // 2 - 1)

            def copy_idx(q, k, nt=GT):
                dve.tensor_copy(gidx[k][:, 0:nt * TOPK], pos_all[:, bass.ds(q * (GT * TOPK), nt * TOPK)]).then_inc(idx_ready, 1)

            def mix(q, k, h_, nt=GT):
                m = [0]

                def link(ins):
                    m[0] += 1
                    ins.then_inc(dve_step3, 1)

                def settle():
                    dve.wait_ge(dve_step3, q * DVE_STEPS3 + m[0])

                dve.wait_ge(gathered[k], h_ * (16 * GT * TOPK) + 16 * nt * TOPK)
                dve.wait_ge(tsh_done, q + 1)
                if not (isinstance(q, int) and q == 0):
                    dve.wait_ge(z4_ready, q)
                tsh = tiles_of(6)
                for s in range(TOPK):
                    for t in range(nt):
                        w = w_all[:, bass.ds(q * (GT * TOPK) + (t * TOPK + s), 1)]
                        ins = dve.scalar_tensor_tensor(out=moe[:, t], in0=gat[k][:, t, s], scalar=w,
                                                       in1=tsh[:, t] if s == 0 else moe[:, t], op0=ALU.mult, op1=ALU.add)
                    link(ins) if s == 0 else ins.then_inc(mix_done, 1)
                    settle() if s == 0 else dve.wait_ge(mix_done, q + 1)
                stats(lambda t: moe[:, t], nt, link, settle)
                dve.tensor_scalar(var1[:, 0:nt], mv[:, 0:nt, 1], EPS, None, ALU.add).then_inc(var4_ready, 1)
                res = r_res[:, bass.ds(q * GTOK, nt * D)].rearrange("p (t d) -> p t d", t=nt)
                link(dve.tensor_tensor(res, res, moe[:, 0:nt], ALU.add))
                dve.wait_ge(rstd4_ready, q + 1)
                if not (isinstance(q, int) and q == 0):
                    dve.wait_ge(tz_done, q)
                normalise(z4, moe, rstd1, nt).then_inc(z4_ready, 1)
                settle()
                assert m[0] == DVE_STEPS3, m[0]

            def out3(q, nt=GT):
                dve.wait_ge(tout3_done, q + 1)
                res = r_res[:, bass.ds(q * GTOK, nt * D)].rearrange("p (t d) -> p t d", t=nt)
                dve.tensor_tensor(res, tiles_of(7)[:, 0:nt], res, ALU.add).then_inc(out_ready, 1)

            def step3(q, k, h_):
                mix(q + 2, k, h_ + 1)
                copy_idx(q + 4, k)
                out3(q)

            dve.sem_inc(out_ready, 1)
            dve.wait_ge(r_loaded, 16)
            for q in range(3):
                copy_idx(q, q % 2) if q < 2 else None
            mix(0, 0, 0)
            copy_idx(2, 0)
            mix(1, 1, 0)
            copy_idx(3, 1)
            groups(dve, 0, GROUPS - 4, step3)
            mix(GROUPS - 2, 0, (GROUPS - 2) // 2)
            copy_idx(GROUPS, 0, 1)
            out3(GROUPS - 4)
            mix(GROUPS - 1, 1, (GROUPS - 1) // 2)
            out3(GROUPS - 3)
            mix(GROUPS, 0, GROUPS // 2, 1)
            for q in range(GROUPS - 2, GROUPS):
                out3(q)
            out3(GROUPS, 1)

        @block.tensor
        def _(pe):
            pe.wait_ge(ld_const, 16 * N_LOADS)
            pe.transpose(bank[7][:, 0:V_END], vecs[:, :], ident[0:V_END, 0:V_END]).then_inc(setup_t, 1)
            pe.wait_ge(ld_w, 16)
            for px in range(PATCH):
                ins = pe.transpose(bank[px // 4][0:KROWS, (px % 4) * P:(px % 4 + 1) * P],
                                   wnat[:, :, :, px].rearrange("h c y -> h (c y)"), ident)
                if px % 4 == 3:
                    ins.then_inc(wp_t, 1)
            pe.wait_ge(cols_ready, 1)
            pe.wait_ge(xcls_ready, 1)
            pe.transpose(bank[7][:, P:2 * P], xcls[:, :], ident).then_inc(setup_t, 1)
            pe.wait_ge(wp_ready, PATCH // 4)

            def patch(g, k, h, lo, hi):
                if lo == 0:
                    pe.wait_ge(x_loaded[k], h * (16 * XLOADS) + 16 * XLOADS)
                for px in range(lo, hi):
                    ins = pe.matmul(pa[k][:, :], wp[:, px], xb[k].rearrange("p (t x) -> p t x", x=PATCH)[:, :, px],
                                    start=px == 0, stop=px == PATCH - 1)
                if hi == PATCH:
                    ins.then_inc(patch_done, 1)

            def transposes(dst, src, nt, done):
                for t in range(nt):
                    ins = pe.transpose(dst(t), src(t), ident)
                ins.then_inc(done, 1)

            def attend(g, patches):
                pe.wait_ge(hF_ready, g + 1)
                transposes(lambda t: t1[:, t], lambda t: hF[:, t * P:(t + 1) * P], GT, t1_done)
                patches()
                pe.wait_ge(xh_ready, g + 1)
                transposes(lambda t: t2[:, t * P:(t + 1) * P], lambda t: xh[:, t], GT, t2_done)
                patches()
                pe.wait_ge(xT_ready, g + 1)
                for t in range(GT):
                    for i in range(2):
                        at = t * P + i * SEQ
                        pe.matmul(s_ps[i * SEQ:(i + 1) * SEQ, t, 0:SEQ - 1], xT[:, at:at + SEQ], xT[:, at:at + SEQ - 1],
                                  start=True, stop=True)
                    ins = pe.matmul(s_ps[:, t, SEQ - 1:SEQ], xT[:, t * P:(t + 1) * P], xclsT[:, 0:1], start=True, stop=True)
                ins.then_inc(s_done, 1)
                patches()
                pe.wait_ge(a_ready, g + 1)
                transposes(lambda t: t3[:, t * P:(t + 1) * P], lambda t: a_bd[:, t], GT, t3_done)
                patches()
                pe.wait_ge(vp_ready, g + 1)
                pe.wait_ge(aT_ready, g + 1)
                for t in range(GT):
                    ins = pe.matmul(c_ps[:, t * P:(t + 1) * P], vp[:, t], aT[:, t * P:(t + 1) * P], start=True, stop=True)
                ins.then_inc(c_done, 1)
                patches()
                pe.wait_ge(cT_ready, g + 1)
                pe.matmul(w_ps[:, :], wc[:, 0], cT[:, :], start=True, stop=False)
                pe.matmul(w_ps[:, :], wc[:, 1], xT[:, :], start=False, stop=True).then_inc(w_done, 1)

            def route(g, k, nt, patches):
                patches()
                pe.wait_ge(th_ready, g + 1)
                transposes(lambda t: t4[:, t], lambda t: th[:, t * P:(t + 1) * P], nt, t4_done)
                patches()
                pe.wait_ge(z_ready, g + 1)
                transposes(lambda t: t5[:, t * P:(t + 1) * P], lambda t: z[k][:, t], nt, t5_done)
                patches()
                pe.wait_ge(hT_ready, g + 1)
                for t in range(nt):
                    ins = pe.matmul(l_ps[:, t], hT[k][:, t * P:(t + 1) * P], rw[:, :], start=True, stop=True)
                ins.then_inc(l_done, 1)
                patches()
                pe.wait_ge(m2_ready, g + 1)
                pe.matmul(p_ps[:, 0:nt], pref[:, :], m2[:, 0:nt], start=True, stop=False)
                ins = pe.matmul(p_ps[:, nt], ones[:, :], m2[:, nt - 1], start=False, stop=nt == 1)
                for s in range(nt - 1):
                    if s == 0:
                        pe.matmul(p_ps[:, 1:nt], ones[:, :], m2[:, 0:nt - 1], start=False, stop=False)
                    else:
                        pe.matmul(p_ps[:, 1 + s:nt + 1], ones[:, :], m2[:, 0:nt - s], start=False, stop=False)
                if nt > 1:
                    ins = pe.matmul(p_ps[:, nt], ones[:, :], m2[:, 0], start=False, stop=True)
                ins.then_inc(p_done, 1)
                patches()

            SPLIT = [0, 3, 5, 9, 11, 13, 16, 21, 24, 28, 28]

            def body(g, k, h, ahead=True):
                slot = [0]

                def patches():
                    if ahead and SPLIT[slot[0]] < SPLIT[slot[0] + 1]:
                        patch(g + 1, (k + 1) % 2, h + k, SPLIT[slot[0]], SPLIT[slot[0] + 1])
                    slot[0] += 1

                attend(g, patches)
                route(g, k, GT, patches)
                assert slot[0] == len(SPLIT) - 1, slot

            patch(0, 0, 0, 0, PATCH)
            pe.wait_ge(xclsT_ready, 1)
            groups(pe, 0, GROUPS - 2, body)
            one(body, GROUPS - 2)
            body(GROUPS - 1, 1, GROUPS // 2 - 1, ahead=False)
            pe.matmul(w_ps[:, 0:P], wc[:, 1], xclsT[:, :], start=True, stop=True).then_inc(w_done, 1)
            route(GROUPS, 0, 1, lambda: None)


            def t_in(j, n, h):
                pe.wait_ge(zin_loaded[n % 4], h * 16 + 16)
                if n > 0:
                    pe.wait_ge(h2T_ready, j)
                for i in range(EH):
                    ins = pe.transpose(bank[0][:, i * P:(i + 1) * P], zin[n % 4][:, i], ident)
                ins.then_inc(tin_done, 1)

            def t_out(j, n):
                pe.wait_ge(eyT_ready, j + 1)
                if n > 0:
                    pe.wait_ge(yout_ready, j)
                for i in range(EH):
                    ins = pe.transpose(bank[7][:, i * P:(i + 1) * P], eyT[n % 2][:, i * P:(i + 1) * P], ident)
                ins.then_inc(tout_done, 1)

            def up(j, n, h):
                pe.wait_ge(ew_loaded[n % 4], h * 32 + 32)
                pe.wait_ge(h2T_ready, j + 1)
                for c in range(EC):
                    if n > 0:
                        pe.wait_ge(eh_ready, j * EC + (c + 1 - EC))
                    pe.matmul(bank[1 + c][:, 0:EROWS], w1b[n % 4][:, c * P:(c + 1) * P], h2T[n % 2],
                              start=True, stop=True).then_inc(up_done, 1)

            def down(j, n):
                for c in range(EC):
                    pe.wait_ge(eh_ready, j * EC + c + 1)
                    ins = pe.matmul(bank[5 + n % 2][:, 0:EROWS], w2b[n % 4][:, c], ehT[n % 2][:, c],
                                    start=c == 0, stop=c == EC - 1)
                ins.then_inc(down_done, 1)

            def step2(j, n, h, first=0):
                if not (isinstance(j, int) and j + 1 >= EXPERT_TILES):
                    t_in(j + 1, n + 1, h + (n % 4 + 1) // 4)
                if n - 2 >= first:
                    t_out(j - 2, n - 2)
                if not (isinstance(j, int) and j >= EXPERT_TILES):
                    up(j, n, h)
                if n - 1 >= first and not (isinstance(j, int) and j > EXPERT_TILES):
                    down(j - 1, n - 1)

            t_in(0, 0, 0)
            for j in range(4):
                step2(j, j, 0)
            with pe.Fori(1, EXPERT_TILES // 4 - 1) as i:
                for n in range(4):
                    step2(i * 4 + n, 4 + n, i)
            for j in range(EXPERT_TILES - 4, EXPERT_TILES + 2):
                step2(j, j, j // 4)


            def sh_up(q, k, h, n, nt=GT):
                pe.wait_ge(ht_loaded[k], h * 16 + 16)
                for c in range(SC):
                    if not (isinstance(n, int) and n + c < 3):
                        pe.wait_ge(u_used, n + c - 2)
                    pe.matmul(bank[(4 + c) % 3][:, 0:nt * P], sw1_t[:, c * P:(c + 1) * P], ht3[k][:, 0:nt * P],
                              start=True, stop=True).then_inc(u_done, 1)

            def sh_down(q, n, nt=GT):
                pe.wait_ge(u_used, n)
                for c in range(SC):
                    ins = pe.matmul(bank[3][:, 0:nt * P], sw2_t[:, c], shs[:, c, 0:nt * P], start=c == 0, stop=c == SC - 1)
                ins.then_inc(shd_done, 1)

            def t_sh(q, nt=GT):
                pe.wait_ge(shF_ready, q + 1)
                transposes(lambda t: bank[6][:, t * P:(t + 1) * P], lambda t: shF[:, t * P:(t + 1) * P], nt, tsh_done)

            def t_z(q, nt=GT):
                pe.wait_ge(z4_ready, q + 1)
                transposes(lambda t: bank[5][:, t * P:(t + 1) * P], lambda t: z4[:, t], nt, tz_done)

            def ff_up(q, n, nt=GT, tail=False):
                pe.wait_ge(h4T_ready, q + 1)
                for c in range(EC):
                    pe.wait_ge(u_used, n if tail and c == 0 else n + (c - 2))
                    pe.matmul(bank[c % 3][:, 0:nt * P], fw1_t[:, c * P:(c + 1) * P], h4T[:, 0:nt * P],
                              start=True, stop=True).then_inc(u_done, 1)

            def ff_down(q, n, nt=GT):
                for c in range(EC):
                    pe.wait_ge(u_used, n + c + 1)
                    ins = pe.matmul(bank[4][:, 0:nt * P], fw2_t[:, c], ffs[:, c, 0:nt * P], start=c == 0, stop=c == EC - 1)
                ins.then_inc(ffd_done, 1)

            def t_out3(q, nt=GT):
                pe.wait_ge(oF_ready, q + 1)
                pe.wait_ge(out_ready, q + 1)
                transposes(lambda t: bank[7][:, t * P:(t + 1) * P], lambda t: oF[:, t * P:(t + 1) * P], nt, tout3_done)

            pe.wait_ge(w3_loaded, 64)
            for q in range(3):
                if q > 0:
                    pe.wait_ge(u_used, SC * q)
                sh_up(q, q % 2, q // 2, SC * q) if q == 0 else sh_up(q, q % 2, q // 2, SC * q + 1)
                if q < 2:
                    sh_down(q, SC * (q + 1))
                    if q == 1:
                        pe.wait_ge(mix_done, 1)
                    t_sh(q)
            t_z(0)

            def step3(q, k, h, sh3=GT, sh2=GT, z1=GT, now=GT, n=None):
                tail = n is not None
                n = q * 6 + 6 if n is None else n
                ff_up(q, n, now, tail)
                if sh2:
                    sh_down(q + 2, n, sh2)
                if z1:
                    t_z(q + 1, z1)
                ff_down(q, n, now)
                if sh2:
                    t_sh(q + 2, sh2)
                if sh3:
                    sh_up(q + 3, (k + 3) % 2, h + (k + 3) // 2, n + 4, sh3)
                t_out3(q, now)

            groups(pe, 0, GROUPS - 4, step3)
            one(step3, GROUPS - 4)
            step3(GROUPS - 3, 1, (GROUPS - 3) // 2, sh3=1)
            last = (GROUPS - 3) * 6 + 12
            step3(GROUPS - 2, 0, (GROUPS - 2) // 2, sh3=0, sh2=1, n=last)
            step3(GROUPS - 1, 1, (GROUPS - 1) // 2, sh3=0, sh2=0, z1=1, n=last + EC)
            step3(GROUPS, 0, GROUPS // 2, sh3=0, sh2=0, z1=0, now=1, n=last + 2 * EC)


_INS = ["x", "L0_tok_W", "L0_tok_b", "L0_tok_class_token", "L0_tok_pos_embed", "L0_attn_W_c", "L0_ffn_ln_in_g",
        "L0_ffn_ln_in_b", "L0_ffn_router_w", "L0_ffn_router_b", "L0_ffn_ew1", "L0_ffn_eb1", "L0_ffn_ew2", "L0_ffn_eb2",
        "L0_ffn_sw1", "L0_ffn_sb1", "L0_ffn_sw2", "L0_ffn_sb2", "L0_ffn_ff_ln_g", "L0_ffn_ff_ln_b", "L0_ffn_ff_w1",
        "L0_ffn_ff_b1", "L0_ffn_ff_w2", "L0_ffn_ff_b2"]


def kernel(**inputs):
    import numpy as _np
    import concourse.bacc as _bacc
    from concourse import mybir as _mybir
    from concourse.bass_utils import run_bass_kernel_spmd as _run

    nc = _bacc.Bacc("TRN2", target_bir_lowering=False, num_devices=1)
    arrays, args = {"consts": constants()}, []
    for name in _INS:
        arrays[f"in_{name}"] = _np.ascontiguousarray(inputs[name])
    for name, a in arrays.items():
        args.append(nc.dram_tensor(name, a.shape, _mybir.dt.from_np(a.dtype), kind="ExternalInput").ap())
    out = nc.dram_tensor("out_0", (BATCH, SEQ + 1, D), _mybir.dt.float32, kind="ExternalOutput").ap()
    build(nc, *args, out)
    r = _run(nc, [arrays], core_ids=[0])
    return r.results[0]["out_0"]
```

```python
from contextlib import ExitStack

import numpy as np

import concourse.bass as bass
from concourse import mybir

F32 = mybir.dt.float32
F32R = mybir.dt.float32r
BF16 = mybir.dt.bfloat16
U32 = mybir.dt.uint32
I32 = mybir.dt.int32
ALU = mybir.AluOpType
ACT = mybir.ActivationFunctionType
AX = mybir.AxisListType

P = 128
D = 128
BATCH, CH, IMG, PATCH = 128, 3, 224, 28
NP = IMG // PATCH
SEQ = NP * NP
KROWS = CH * PATCH
PATCH_TILES = BATCH * SEQ // P
TILES = PATCH_TILES + 1
GT = 4
GTOK = GT * P
GIMG = GTOK // SEQ
GROUPS = PATCH_TILES // GT
TOKENS = TILES * P
E, DH, DS = 16, 512, 256
EC, SC = DH // P, DS // P
TOPK = 2
TEMP = 0.7
SHARED = 0.25
EPS = 1e-5
EROWS = 256
EH = EROWS // P
CAP = -(-TOKENS // EROWS) * EROWS + EROWS
EXPERT_TILES = (TOKENS * TOPK + E * (EROWS - 1)) // EROWS
SPARE_TILES = EXPERT_TILES - TOKENS * TOPK // EROWS
ZROWS = E * CAP + SPARE_TILES * EROWS
XLOADS = GIMG * CH
TAIL = GTOK + EROWS
XS, XR = 10, 5
PX_ORDER = [*range(XR), *range(XS, XS + 8), *range(XR, XS), *range(XS + 8, PATCH)]
N_LOADS = 18

C_ID, C_MASK, C_CLS, C_KEEP, C_IOTA, C_PREF, C_BASE, C_TILE = 0, 128, 192, 193, 194, 210, 338, 354
C_END = C_TILE + 1

V_EB1, V_EB2 = 0, E * EC
V_SB1 = V_EB2 + E
V_SB2 = V_SB1 + SC
V_FB1 = V_SB2 + 1
V_FB2 = V_FB1 + EC
V_LG, V_LB, V_FG, V_FB, V_TB = V_FB2 + 1, V_FB2 + 2, V_FB2 + 3, V_FB2 + 4, V_FB2 + 5
V_END = V_TB + 1


def constants():
    c = np.zeros((P, C_END), np.float32)
    c[:, C_ID:C_ID + P] = np.eye(P)
    row = np.arange(P) % SEQ
    c[:, C_MASK:C_MASK + SEQ] = np.arange(SEQ)[None] < row[:, None]
    c[:, C_MASK + SEQ - 1] = 1
    c[:, C_CLS] = row == SEQ - 1
    c[:, C_KEEP] = row != SEQ - 1
    c[:, C_IOTA:C_IOTA + E] = np.arange(E)
    c[:, C_PREF:C_PREF + P] = np.arange(P)[:, None] < np.arange(P)[None]
    c[:, C_BASE:C_BASE + E] = np.arange(E) * CAP
    c[:, C_TILE] = np.arange(P)
    return c


def build(nc, consts, x, tok_w, tok_b, cls_tok, pos, w_c, ln_g, ln_b, r_w, r_b, ew1, eb1, ew2, eb2,
          sw1, sb1, sw2, sb2, f_g, f_b, fw1, fb1, fw2, fb2, out):
    with ExitStack() as ctx:
        def sb(name, shape, dt=F32):
            return ctx.enter_context(nc.sbuf_tensor(name, shape, dt))

        def sem(name):
            return ctx.enter_context(nc.semaphore(name))

        def dram(name, shape, dt=F32):
            return nc.dram_tensor(name, shape, dt, kind="Internal").ap()

        z_rows = dram("z_rows", [ZROWS, D])
        y_rows = dram("y_rows", [EXPERT_TILES * EROWS, D])
        r_dram = dram("r_dram", [P, TILES, D])
        ht_dram = dram("ht_dram", [P, TILES, P])

        cst = sb("cst", [P, C_END])
        ident = cst[:, C_ID:C_ID + P]
        mask = cst[:, C_MASK:C_MASK + SEQ]
        iota = cst[:, C_IOTA:C_IOTA + E]
        pref = sb("pref", [P, P], BF16)
        ones = sb("ones", [P, P], BF16)
        neghalf = sb("neghalf", [P, 2 * GT])
        spare = sb("spare", [P, 1])
        vecs = sb("vecs", [V_END, D])
        cols = sb("cols", [P, V_END])
        sb2q = sb("sb2q", [P, 1])
        pos_t = sb("pos_t", [P, D])
        wp = sb("wp", [P, PATCH, D])
        wc = sb("wc", [P, 2, D])
        rw = sb("rw", [P, E])
        rb = sb("rb", [P, E])
        hcls = sb("hcls", [P, D])
        pos0 = sb("pos0", [P, D])
        xcls = sb("xcls", [P, D])
        xclsT = sb("xclsT", [P, P])
        vcls = sb("vcls", [P, D])
        pos_all = sb("pos_all", [P, TILES * TOPK])
        w_all = sb("w_all", [P, TILES * TOPK])
        shift = sb("shift", [P, TILES * TOPK])
        base = sb("base", [P, E])

        XCOLS = GIMG * NP * IMG
        XZ = XCOLS // 2
        region = sb("region", [P, 2 * XCOLS])
        xb = [region[:, u * XCOLS:(u + 1) * XCOLS] for u in range(2)]
        wnat = region[:, XCOLS:XCOLS + CH * PATCH * PATCH].rearrange("h (c y x) -> h c y x", c=CH, y=PATCH)
        carved = [0]

        def carve(n):
            carved[0] += n
            assert carved[0] <= 2 * XCOLS
            return region[:, carved[0] - n:carved[0]]

        W = EC * P
        w1b = [carve(W) for _ in range(4)]
        w2b = [carve(W).rearrange("p (c d) -> p c d", c=EC) for _ in range(4)]
        zin = [carve(EH * D).rearrange("p (h d) -> p h d", h=EH) for _ in range(4)]
        h2T = [carve(EROWS) for _ in range(2)]
        ehT = [carve(EC * EROWS).rearrange("p (c r) -> p c r", c=EC) for _ in range(2)]
        eyT = [carve(EROWS) for _ in range(2)]
        yout = [carve(EH * D).rearrange("p (h d) -> p h d", h=EH) for _ in range(2)]
        sw1_t = carve(DS)
        sw2_t = carve(SC * D).rearrange("p (c d) -> p c d", c=SC)
        fw1_t = carve(DH)
        fw2_t = carve(EC * D).rearrange("p (c d) -> p c d", c=EC)
        gat = [carve(GT * TOPK * D).rearrange("p (t k d) -> p t k d", t=GT, k=TOPK) for _ in range(2)]
        shs = carve(SC * GTOK).rearrange("p (c r) -> p c r", c=SC)
        shF = carve(GTOK)
        moe = carve(GT * D).rearrange("p (t d) -> p t d", t=GT)
        z4 = carve(GT * D).rearrange("p (t d) -> p t d", t=GT)
        h4T = carve(GTOK)
        ffs = carve(EC * GTOK).rearrange("p (c r) -> p c r", c=EC)
        oF = carve(GTOK)
        ht3 = [carve(GTOK) for _ in range(2)]
        r_res = carve(TILES * D)

        parts = sb("parts", [P, 2 * XR * GTOK], F32R)
        w1h, w1l = ([parts[:, (2 * c + u) * W:(2 * c + u + 1) * W] for u in range(2)] for c in range(2))
        h2h, h2l = ([parts[:, 4 * W + (2 * c + u) * EROWS:4 * W + (2 * c + u + 1) * EROWS] for u in range(2)] for c in range(2))
        xhi, xlo = ([parts[:, (2 * u + c) * GTOK:(2 * u + c + 1) * GTOK] for u in range(XR)] for c in range(2))
        wph, wpl = (sb(f"wp{c}", [P, XS, D], F32R) for c in "hl")

        def tm(name):
            return sb(name, [P, GT, D])

        h = [tm(f"h{u}") for u in range(2)]
        xh = tm("xh")
        vp = tm("vp")
        fm = sb("fm", [P, 5 * GTOK])
        xT, aT, cT, th, hF = (fm[:, i * GTOK:(i + 1) * GTOK] for i in range(5))
        past = fm[:, 0:TILES * TOPK * E].rearrange("p (s e) -> p s e", e=E)
        s_t = sb("s_t", [P, GT, SEQ])
        e_t = sb("e_t", [P, GT, SEQ])
        a_bd = tm("a_bd")
        h2 = tm("h2")
        z = [tm(f"z{u}") for u in range(2)]
        rr = [tm(f"rr{u}") for u in range(2)]
        hT = [sb(f"hT{u}", [P, GTOK]) for u in range(2)]
        st = sb("st", [P, GT, 6])
        mv = sb("mv", [P, GT, 2])
        var1 = sb("var1", [P, GT])
        rstd1 = sb("rstd1", [P, GT])
        var2 = sb("var2", [P, 2 * GT])
        rstd2 = sb("rstd2", [P, 2 * GT])
        rs1 = sb("rs1", [P, GT])
        rs2 = sb("rs2", [P, GT])
        mx = sb("mx", [P, GT])
        sm = sb("sm", [P, GT])
        rsm = sb("rsm", [P, GT])
        st2 = sb("st2", [P, GT, 6])
        mv2 = sb("mv2", [P, GT, 2])
        gsm = sb("gsm", [P, GT])
        rgsm = sb("rgsm", [P, GT])
        lg = sb("lg", [P, GT, E])
        m8 = sb("m8", [P, GT, 8])
        i8 = sb("i8", [P, GT, 8], U32)
        i2 = sb("i2", [P, GT * TOPK])
        d18 = sb("d18", [P, GT, E + TOPK])
        oh = sb("oh", [P, GT * TOPK, E])
        m2 = sb("m2", [P, GT, E], BF16)
        pp = sb("pp", [P, GT, TOPK, E])
        posf = sb("posf", [P, GT * TOPK])
        posg = [sb(f"posg{u}", [P, GT * TOPK], U32) for u in range(2)]
        gidx = [sb(f"gidx{u}", [P, GT * TOPK], U32) for u in range(2)]
        cnt = sb("cnt", [P, E])
        cnti = sb("cnti", [P, E], I32)
        nt = sb("nt", [P, E])
        nti = sb("nti", [P, E], I32)
        dsh = sb("dsh", [P, E])
        one_e = sb("one_e", [P, E])
        cum = sb("cum", [P, E])
        cmp = sb("cmp", [P, E])
        ejt = sb("ejt", [P, 2])
        tj = sb("tj", [P, 1])
        ejc = sb("ejc", [1, EXPERT_TILES], I32)
        rowj = sb("rowj", [1, EXPERT_TILES], I32)
        tail = sb("tail", [1, E], I32)
        zeros = sb("zeros", [P, EH * D])
        zsrc = zeros[:, :].rearrange("p (h d) -> p h d", h=EH)

        bank = [ctx.enter_context(nc.psum_tensor(f"bank{i}", [P, 512], F32)) for i in range(8)]

        def tiles_of(b, w=D):
            return bank[b][:, 0:GT * w].rearrange("p (t d) -> p t d", t=GT)

        pa = bank[0]
        t1, t2, s_ps, t3 = tiles_of(2), bank[3], tiles_of(4, SEQ), bank[5]
        c_ps, w_ps, t4, t5 = bank[2], bank[3], tiles_of(4), bank[5]
        l_ps = bank[6][:, 0:GT * E].rearrange("p (t e) -> p t e", t=GT)
        p_ps = bank[7][:, 0:(GT + 1) * E].rearrange("p (t e) -> p t e", t=GT + 1)

        x_zeroed, x_zeroed_act, wp_zeroed = sem("x_zeroed"), sem("x_zeroed_act"), sem("wp_zeroed") 
        ld_id, ld_const, ld_w = sem("ld_id"), sem("ld_const"), sem("ld_w")
        memset_done, dve_setup = sem("memset_done"), sem("dve_setup")
        cls_var, cls_rstd, xcls_ready = sem("cls_var"), sem("cls_rstd"), sem("xcls_ready")
        setup_t, wp_t = sem("setup_t"), sem("wp_t")
        cols_ready, xclsT_ready, wp_ready = sem("cols_ready"), sem("xclsT_ready"), sem("wp_ready")
        xhi_ready, xlo_ready, xparts_used = sem("xhi_ready"), sem("xlo_ready"), sem("xparts_used")
        wph_ready, wpl_ready = sem("wph_ready"), sem("wpl_ready")
        x_loaded = [sem(f"x_loaded{u}") for u in range(2)]
        patch_done, hF_ready, t1_done, h_ready = sem("patch_done"), sem("hF_ready"), sem("t1_done"), sem("h_ready")
        var1_ready, rstd1_ready, xh_ready, vp_ready = sem("var1_ready"), sem("rstd1_ready"), sem("xh_ready"), sem("vp_ready")
        t2_done, xT_ready, s_done, smax_ready = sem("t2_done"), sem("xT_ready"), sem("s_done"), sem("smax_ready")
        e_ready, a_ready, t3_done, aT_ready = sem("e_ready"), sem("a_ready"), sem("t3_done"), sem("aT_ready")
        c_done, cT_ready, w_done, th_ready = sem("c_done"), sem("cT_ready"), sem("w_done"), sem("th_ready")
        t4_done, var2_ready, rstd2_ready, z_ready = sem("t4_done"), sem("var2_ready"), sem("rstd2_ready"), sem("z_ready")
        r_ready, t5_done, hT_ready, l_done = sem("r_ready"), sem("t5_done"), sem("hT_ready"), sem("l_done")
        rs_ready = sem("rs_ready")
        gate_ready, gexp_ready, m2_ready, p_done, pos_ready = (
            sem("gate_ready"), sem("gexp_ready"), sem("m2_ready"), sem("p_done"), sem("pos_ready"))
        dve_step = sem("dve_step")
        r_free = [sem(f"r_free{u}") for u in range(2)]
        hT_free = [sem(f"hT_free{u}") for u in range(2)]
        z_free = [sem(f"z_free{u}") for u in range(2)]
        tab_step, tab_ready, spare_zeroed, tails_zeroed = sem("tab_step"), sem("tab_ready"), sem("spare_zeroed"), sem("tails_zeroed")
        tail_ready, past_ready, shift_ready, ejt_ready, tej_done = (
            sem("tail_ready"), sem("past_ready"), sem("shift_ready"), sem("ejt_ready"), sem("tej_done"))
        w1_loaded = [sem(f"w1_loaded{u}") for u in range(4)]
        w2_loaded = [sem(f"w2_loaded{u}") for u in range(4)]
        zin_loaded = [sem(f"zin_loaded{u}") for u in range(4)]
        tin_done, h2T_ready, up_done, eh_ready = sem("tin_done"), sem("h2T_ready"), sem("up_done"), sem("eh_ready")
        w1h_ready, w1l_ready, h2h_ready, h2l_ready = sem("w1h_ready"), sem("w1l_ready"), sem("h2h_ready"), sem("h2l_ready")
        down_done, eyT_ready, tout_done, yout_ready = sem("down_done"), sem("eyT_ready"), sem("tout_done"), sem("yout_ready")
        y_free = [sem(f"y_free{u}") for u in range(2)]
        w3_loaded, r_loaded = sem("w3_loaded"), sem("r_loaded")
        ht_loaded = [sem(f"ht_loaded{u}") for u in range(2)]
        idx_ready, sb2q_ready = sem("idx_ready"), sem("sb2q_ready")
        gathered = [sem(f"gathered{u}") for u in range(2)]
        u_done, u_used = sem("u_done"), sem("u_used")
        shd_done, shF_ready, tsh_done, mix_done = sem("shd_done"), sem("shF_ready"), sem("tsh_done"), sem("mix_done")
        var4_ready, rstd4_ready, z4_ready, tz_done, h4T_ready = (
            sem("var4_ready"), sem("rstd4_ready"), sem("z4_ready"), sem("tz_done"), sem("h4T_ready"))
        ffd_done, oF_ready, tout3_done, out_ready, out_stored = (
            sem("ffd_done"), sem("oF_ready"), sem("tout3_done"), sem("out_ready"), sem("out_stored"))
        wait_carried = sem("wait_carried")
        dve_step3 = sem("dve_step3")
        A_STEPS, R_STEPS = 7, 16
        DVE_STEPS, DVE_STEPS3 = A_STEPS + R_STEPS, 4

        def bc(ap, shape):
            return ap.to_broadcast(shape)

        def groups(eng, first, last, body):
            assert (last - first) % 2 == 0
            with eng.Fori(0, (last - first) // 2) as i:
                for j in range(first, first + 2):
                    body(i * 2 + j, j % 2, i + j // 2)

        def one(body, g):
            body(g, g % 2, g // 2)

        def plain(eng):
            eng.sem_inc(wait_carried, 1)

        def col(n):
            return cols[:, n:n + 1]

        def pixels(k, px):
            return xb[k].rearrange("p (t x) -> p t x", x=PATCH)[:, :, px]

        block = ctx.enter_context(nc.Block())

        @block.sync
        def _(sp):
            loads = [(vecs[V_EB1:V_EB2], eb1.rearrange("e (c p) -> (e c) p", p=P)),
                     (vecs[V_EB2:V_SB1], eb2), (vecs[V_SB1:V_SB2], sb1.rearrange("(c p) -> c p", p=P)),
                     (vecs[V_SB2:V_FB1], sb2.unsqueeze(0)), (vecs[V_FB1:V_FB2], fb1.rearrange("(c p) -> c p", p=P)),
                     (vecs[V_FB2:V_LG], fb2.unsqueeze(0)), (vecs[V_LG:V_LB], ln_g.unsqueeze(0)),
                     (vecs[V_LB:V_FG], ln_b.unsqueeze(0)), (vecs[V_FG:V_FB], f_g.unsqueeze(0)),
                     (vecs[V_FB:V_TB], f_b.unsqueeze(0)), (vecs[V_TB:V_END], tok_b.unsqueeze(0)),
                     (pos_t[0:SEQ], pos[1:SEQ + 1]), (pos_t[SEQ:P], pos[1:SEQ + 1]),
                     (hcls[:, :], cls_tok[0].partition_broadcast(P)), (pos0[:, :], pos[0].partition_broadcast(P)),
                     (wc[:, :, :], w_c.rearrange("(k f) o -> f k o", k=2)), (rw[:, :], r_w),
                     (rb[:, :], r_b.partition_broadcast(P))]
            assert len(loads) == N_LOADS

            def load_x(g, k, h):
                dst = xb[k].rearrange("p (b n w) -> p b n w", b=GIMG, n=NP)
                for c in range(CH):
                    if isinstance(g, int) and g < 2 and c == CH - 1:
                        sp.wait_ge(x_zeroed, g + 1)
                        sp.wait_ge(x_zeroed_act, 1)
                    for b in range(GIMG):
                        src = x[bass.ds(g * GIMG + b, 1), c].rearrange("o (n y) w -> y (o n) w", y=PATCH)
                        sp.dma_start(dst[c * PATCH:(c + 1) * PATCH, b], src).then_inc(x_loaded[k], 16)

            def reload_x(g, k, h):
                sp.wait_ge(patch_done, g - 1)
                load_x(g, k, h)

            def stores(r, k, h, nt=GT):
                tile = r * GT - GT if nt == GT else PATCH_TILES
                sp.wait_ge(hT_ready, r + 1)
                sp.dma_start(ht_dram[:, bass.ds(tile, nt)],
                             hT[k][:, 0:nt * P].rearrange("p (t c) -> p t c", t=nt)).then_inc(hT_free[k], 16)
                sp.wait_ge(r_ready, r + 1)
                sp.dma_start(r_dram[:, bass.ds(tile, nt)], rr[k][:, 0:nt]).then_inc(r_free[k], 16)

            sp.dma_start(cst[:, :], consts).then_inc(ld_id, 16)
            sp.dma_start(wnat, tok_w.rearrange("h (c y x) -> h c y x", c=CH, y=PATCH)).then_inc(ld_w, 16)
            load_x(0, 0, 0)
            for dst, src in loads:
                sp.dma_start(dst, src).then_inc(ld_const, 16)
            sp.wait_ge(wp_t, PATCH // 4)
            load_x(1, 1, 0)
            for k in range(2):
                sp.sem_inc(r_free[k], 16)
                sp.sem_inc(hT_free[k], 16)
            sp.wait_ge(memset_done, 2)
            for s in range(2, SPARE_TILES):
                at = E * CAP + s * EROWS
                sp.dma_start(z_rows[at:at + EROWS].rearrange("(h p) d -> p h d", p=P), zsrc).then_inc(spare_zeroed, 16)

            def step(g, k, h):
                reload_x(g + 2, k, h + 1)
                stores(g, k, h)

            reload_x(2, 0, 1)
            stores(0, 0, 0, 1)
            groups(sp, 1, GROUPS - 3, step)
            one(step, GROUPS - 3)
            one(stores, GROUPS - 2)
            one(stores, GROUPS - 1)

            sp.wait_ge(tail_ready, 1)
            with sp.Fori(0, E // 4) as e:
                rows = [sp.value_load(tail[0:1, bass.ds(e * 4 + n, 1)], min_val=0, max_val=ZROWS - TAIL) for n in range(4)]
                for row in rows:
                    sp.dma_start(z_rows[bass.ds(row, TAIL)].rearrange("(p h) d -> p h d", p=P),
                                 zeros[:, 0:D].unsqueeze(1).to_broadcast([P, TAIL // P, D])).then_inc(tails_zeroed, 16)
            one(stores, GROUPS)

            def expert_weights(j, n):
                ex = sp.value_load(ejc[0:1, bass.ds(j, 1)], min_val=0, max_val=E - 1)
                sp.wait_ge(w1l_ready, j - 3) if n >= 4 else None
                sp.dma_start(w1b[n % 4], ew1[bass.ds(ex, 1)].rearrange("o d h -> d (o h)")).then_inc(w1_loaded[n % 4], 16)
                sp.wait_ge(down_done, j - 3) if n >= 4 else None
                sp.dma_start(w2b[n % 4], ew2[bass.ds(ex, 1)].rearrange("o (c p) d -> p (o c) d", p=P))\
                  .then_inc(w2_loaded[n % 4], 16)

            def expert_rows(j, n):
                row = sp.value_load(rowj[0:1, bass.ds(j, 1)], min_val=0, max_val=ZROWS - EROWS)
                sp.wait_ge(tin_done, j - 3) if n >= 4 else None
                sp.dma_start(zin[n % 4], z_rows[bass.ds(row, EROWS)].rearrange("(h p) d -> p h d", p=P))\
                  .then_inc(zin_loaded[n % 4], 16)

            def expert_loads(j, n):
                expert_rows(j, n)
                expert_weights(j, n)

            sp.wait_ge(patch_done, GROUPS)
            sp.wait_ge(tab_ready, 1)
            for j in range(4):
                expert_weights(j, j)
            sp.wait_ge(z_free[0], 16 + 16 * TOPK + 16 * TOPK * GT * GROUPS // 2)
            sp.wait_ge(z_free[1], 16 + 16 * TOPK * GT * GROUPS // 2)
            sp.wait_ge(spare_zeroed, 16 * (SPARE_TILES - 2))
            for j in range(4):
                expert_rows(j, j)
            for k in range(2):
                sp.wait_ge(r_free[k], 16 + 16 * (GROUPS // 2 + 1 - k))
                sp.wait_ge(hT_free[k], 16 + 16 * (GROUPS // 2 + 1 - k))
            for dst, src in ((sw1_t, sw1), (sw2_t, sw2.rearrange("(c p) d -> p c d", p=P)), (fw1_t, fw1),
                             (fw2_t, fw2.rearrange("(c p) d -> p c d", p=P))):
                sp.dma_start(dst, src).then_inc(w3_loaded, 16)
            for q in range(2):
                sp.dma_start(ht3[q], ht_dram[:, q * GT:(q + 1) * GT].rearrange("p t c -> p (t c)")).then_inc(ht_loaded[q], 16)
            with sp.Fori(1, 1 + GROUPS) as i:
                for n in range(4):
                    expert_loads(i * 4 + n, 4 + n)
                sp.dma_start(r_res[:, bass.ds(i * GTOK - GTOK, GTOK)].rearrange("p (t d) -> p t d", t=GT),
                             r_dram[:, bass.ds(i * GT - GT, GT)]).then_inc(r_loaded, 16)
            sp.dma_start(r_res[:, PATCH_TILES * D:], r_dram[:, PATCH_TILES]).then_inc(r_loaded, 16)
            with sp.Fori(1 + GROUPS, EXPERT_TILES // 4) as i:
                for n in range(4):
                    expert_loads(i * 4 + n, 4 + n)

            def load_ht(q, k, n, nt=GT):
                sp.wait_ge(u_done, n)
                sp.dma_start(ht3[k][:, 0:nt * P].rearrange("p (t c) -> p t c", t=nt),
                             ht_dram[:, bass.ds(q * GT, nt)]).then_inc(ht_loaded[k], 16)

            def store_out(q, nt=GT):
                sp.wait_ge(out_ready, q + 2)
                res = r_res.rearrange("p (t d) -> p t d", d=D)
                for t in range(nt):
                    if nt == GT:
                        dst = out[bass.ds(q * GIMG + 2 * t, 2), 1:SEQ + 1]
                    else:
                        dst = out[:, 0]
                    sp.dma_start(dst, res[:, bass.ds(q * GT + t, 1)].rearrange("p o d -> p (o d)"))\
                      .then_inc(out_stored, 16)

            def step3(q, k, h):
                store_out(q)
                load_ht(q + 5, (k + 5) % 2, q * 6 + 12)

            for q in range(2, 5):
                load_ht(q, q % 2, SC * (q - 1))
            groups(sp, 0, GROUPS - 6, step3)
            one(step3, GROUPS - 6)
            store_out(GROUPS - 5)
            load_ht(GROUPS, 0, (GROUPS - 5) * 6 + 12, 1)
            for q in range(GROUPS - 4, GROUPS):
                store_out(q)
            store_out(GROUPS, 1)
            sp.wait_ge(out_stored, 16 * TILES)

        @block.scalar
        def _(act):
            act.wait_ge(memset_done, 2)
            act.activation(xb[0][64:P, XZ:], zeros[64:P, 0:1].to_broadcast([P - 64, XCOLS - XZ]), ACT.Copy)\
               .then_inc(x_zeroed_act, 1)
            act.wait_ge(wp_zeroed, 2)
            for b in range(PATCH // 4):
                act.wait_ge(wp_t, b + 1)
                act.activation(wp[0:KROWS, 4 * b:4 * b + 4].rearrange("p x h -> p (x h)"), bank[b][0:KROWS, :], ACT.Copy)\
                   .then_inc(wp_ready, 1)
                if 4 * b < XS:
                    n = min(4, XS - 4 * b)
                    act.activation(wph[0:KROWS, 4 * b:4 * b + n].rearrange("p x h -> p (x h)"), bank[b][0:KROWS, 0:n * P],
                                   ACT.Copy).then_inc(wph_ready, 1)
            act.wait_ge(setup_t, 1)
            act.activation(cols[:, :], bank[7][:, 0:V_END], ACT.Copy).then_inc(cols_ready, 1)
            act.wait_ge(setup_t, 2)
            act.activation(xclsT[:, :], bank[7][:, P:2 * P], ACT.Copy).then_inc(xclsT_ready, 1)
            act.wait_ge(cols_ready, 1)

            def x_high(g, k, h, lo):
                act.wait_ge(x_loaded[k], h * (16 * XLOADS) + 16 * XLOADS)
                for px in range(lo, lo + XR):
                    n = (g - 1) * XS + px
                    if not (isinstance(n, int) and n < XR):
                        act.wait_ge(xparts_used, n + (1 - XR))
                    act.activation(xhi[px % XR], pixels(k, px), ACT.Copy).then_inc(xhi_ready, 1)

            def take_patch(g):
                act.wait_ge(patch_done, g + 1)
                act.activation(hF[:, :], pa[:, :], ACT.Identity, bias=col(V_TB)).then_inc(hF_ready, 1)

            def take_x(g):
                act.wait_ge(t2_done, g + 1)
                act.activation(xT[:, :], t2[:, :], ACT.Copy).then_inc(xT_ready, 1)

            def route_a(g, k, h, nt=GT):
                act.wait_ge(hT_free[k], h * 16 + 16)
                act.wait_ge(t5_done, g + 1)
                act.activation(hT[k][:, 0:nt * P], t5[:, 0:nt * P], ACT.Identity, scale=col(V_LG), bias=col(V_LB))\
                   .then_inc(hT_ready, 1)
                act.wait_ge(r_free[k], h * 16 + 16)
                act.wait_ge(rs_ready, g + 1)
                for t in range(nt):
                    ins = act.activation(rr[k][:, t], h2[:, t], ACT.Identity, scale=rs1[:, t:t + 1], bias=rs2[:, t:t + 1])
                ins.then_inc(r_ready, 1)

            def take_s(g):
                act.wait_ge(smax_ready, g + 1)
                act.activation(e_t[:, :, :], s_t[:, :, :], ACT.Exp).then_inc(e_ready, 1)

            def route_b(g, nt=GT):
                act.wait_ge(gate_ready, g + 1)
                act.activation(d18[:, 0:nt], d18[:, 0:nt], ACT.Exp, scale=1.0 / TEMP).then_inc(gexp_ready, 1)

            def take_a(g):
                act.wait_ge(t3_done, g + 1)
                act.activation(aT[:, :], t3[:, :], ACT.Copy).then_inc(aT_ready, 1)

            def take_c(g):
                act.wait_ge(c_done, g + 1)
                act.activation(cT[:, :], c_ps[:, :], ACT.Copy).then_inc(cT_ready, 1)

            def take_w(g, nt=GT):
                act.wait_ge(w_done, g + 1)
                act.activation(th[:, 0:nt * P], w_ps[:, 0:nt * P], ACT.Tanh, scale=0.5).then_inc(th_ready, 1)

            def body(g, k, h, ahead=2, nt=GT):
                if ahead:
                    x_high(g + 1, 1 - k, h + k, XR)
                take_x(g)
                route_a(g, k, h, nt)
                take_s(g)
                route_b(g, nt)
                if ahead > 1:
                    x_high(g + 2, k, h + 1, 0)
                take_a(g)
                if ahead:
                    take_patch(g + 1)
                take_c(g)
                take_w(g + 1)

            take_w(0, 1)
            take_patch(0)
            x_high(1, 1, 0, 0)
            body(0, 0, 0, nt=1)
            groups(act, 1, GROUPS - 3, body)
            one(body, GROUPS - 3)
            body(GROUPS - 2, 0, GROUPS // 2 - 1, ahead=1)
            body(GROUPS - 1, 1, GROUPS // 2 - 1, ahead=0)
            one(route_a, GROUPS)
            route_b(GROUPS)

            def take_in(j, n):
                act.wait_ge(h2l_ready, j - 1) if n > 1 else None
                act.wait_ge(tin_done, j + 1)
                act.activation(h2T[n % 2], bank[0][:, 0:EROWS], ACT.Identity, scale=col(V_LG), bias=col(V_LB))\
                   .then_inc(h2T_ready, 1)

            def silus(j, n, ahead=True):
                ex = act.value_load(ejc[0:1, bass.ds(j, 1)], min_val=0, max_val=E - 1)
                bias = [cols[:, bass.ds(ex * EC + c, 1)] for c in range(EC)]
                for c in range(EC):
                    if c == 2 and ahead:
                        take_in(j + 1, n + 1)
                    act.wait_ge(up_done, j * EC + c + 1)
                    act.activation(ehT[n % 2][:, c], bank[1 + c][:, 0:EROWS], ACT.Silu, bias=bias[c])\
                       .then_inc(eh_ready, 1)

            act.wait_ge(tab_ready, 1)
            act.wait_ge(memset_done, 2)
            take_in(0, 0)
            for j in range(4):
                silus(j, j)
            with act.Fori(1, EXPERT_TILES // 4 - 1) as i:
                act.activation(spare[:, :], neghalf[:, 0:1], ACT.Silu)
                for n in range(4):
                    silus(i * 4 + n, 4 + n)
            for j in range(EXPERT_TILES - 4, EXPERT_TILES):
                silus(j, j, ahead=j + 1 < EXPERT_TILES)

            def silu3(n, b, dst, bias, w):
                act.wait_ge(u_done, n + 1)
                act.activation(dst[:, 0:w], bank[b][:, 0:w], ACT.Silu, bias=bias).then_inc(u_used, 1)

            def sh_silu(q, n, nt=GT):
                for c in range(SC):
                    silu3(n + c, (4 + c) % 3, shs[:, c], col(V_SB1 + c), nt * P)

            def sh_out(q, nt=GT):
                act.wait_ge(shd_done, q + 1)
                act.activation(shF[:, 0:nt * P], bank[3][:, 0:nt * P], ACT.Identity, scale=SHARED, bias=sb2q[:, 0:1])\
                   .then_inc(shF_ready, 1)

            def z_in(q, nt=GT):
                act.wait_ge(tz_done, q + 1)
                act.activation(h4T[:, 0:nt * P], bank[5][:, 0:nt * P], ACT.Identity, scale=col(V_FG), bias=col(V_FB))\
                   .then_inc(h4T_ready, 1)

            def ff_silu(q, n, nt=GT):
                for c in range(EC):
                    silu3(n + c, c % 3, ffs[:, c], col(V_FB1 + c), nt * P)

            def ff_out(q, nt=GT):
                act.wait_ge(ffd_done, q + 1)
                act.activation(oF[:, 0:nt * P], bank[4][:, 0:nt * P], ACT.Identity, bias=col(V_FB2)).then_inc(oF_ready, 1)

            act.wait_ge(sb2q_ready, 1)
            for q in range(3):
                sh_silu(q, 2 * q)
                if q < 2:
                    sh_out(q)
            z_in(0)

            def step3(q, sh3=GT, sh2=GT, z1=GT, now=GT, n=None):
                n = q * 6 + 6 if n is None else n
                ff_silu(q, n, now)
                if sh2:
                    sh_out(q + 2, sh2)
                if z1:
                    z_in(q + 1, z1)
                ff_out(q, now)
                if sh3:
                    sh_silu(q + 3, n + 4, sh3)

            with act.Fori(0, GROUPS - 3) as q:
                step3(q)
            step3(GROUPS - 3, sh3=1)
            last = (GROUPS - 3) * 6 + 12
            step3(GROUPS - 2, sh3=0, sh2=1, n=last)
            step3(GROUPS - 1, sh3=0, sh2=0, z1=1, n=last + EC)
            step3(GROUPS, sh3=0, sh2=0, z1=0, now=1, n=last + 2 * EC)

        @block.gpsimd
        def _(pool):
            pool.memset(neghalf[:, :], -0.5).then_inc(memset_done, 1)
            def rstd(var_ready, n, dst, var, ready):
                pool.wait_ge(var_ready, n)
                pool.tensor_tensor(dst, var, neghalf[:, 0:var.shape[1]], ALU.pow).then_inc(ready, 1)

            pool.wait_ge(memset_done, 2)
            for u in range(2):
                at = E * CAP + u * EROWS
                pool.dma_start(z_rows[at:at + EROWS].rearrange("(h p) d -> p h d", p=P), zsrc).then_inc(z_free[u], 16)
            rstd(cls_var, 1, rstd1[:, 0:1], var1[:, 0:1], cls_rstd)

            def scatter(r, k, nt=GT):
                pool.wait_ge(z_ready, r + 1)
                pool.wait_ge(pos_ready, r + 1)
                plain(pool)
                for t in range(nt):
                    for s in range(TOPK):
                        n = t * TOPK + s
                        pool.indirect_dma_start(z_rows, bass.IndirectOffsetOnAxis(posg[k][:, n:n + 1], 0),
                                                z[k][:, t], None).then_inc(z_free[k], 16)

            def norms(g):
                rstd(var1_ready, g + 1, rstd1[:, :], var1[:, :], rstd1_ready)
                rstd(var2_ready, g + 1, rstd2[:, :], var2[:, :], rstd2_ready)

            def step(g, k, h):
                norms(g)
                scatter(g - 1, 1 - k)

            norms(0)
            norms(1)
            scatter(0, 0, 1)
            groups(pool, 2, GROUPS, step)
            rstd(var2_ready, GROUPS + 1, rstd2[:, :], var2[:, :], rstd2_ready)
            scatter(GROUPS - 1, 1)
            pool.wait_ge(tails_zeroed, 16 * E)
            scatter(GROUPS, 0)

            pool.wait_ge(past_ready, 1)
            pool.tensor_tensor(past, past, bc(dsh[:, :].unsqueeze(1), [P, TILES * TOPK, E]), ALU.mult)\
                .then_inc(shift_ready, 1)


            def store_y(j, n):
                pool.wait_ge(yout_ready, j + 1)
                plain(pool)
                pool.dma_start(y_rows[bass.ds(j * EROWS, EROWS)].rearrange("(h p) d -> p h d", p=P), yout[n % 2])\
                    .then_inc(y_free[n % 2], 16)

            store_y(0, 0)
            store_y(1, 1)
            with pool.Fori(1, EXPERT_TILES // 2) as i:
                for n in range(2):
                    store_y(i * 2 + n, n)
            for k in range(2):
                pool.wait_ge(y_free[k], 16 * (EXPERT_TILES // 2))

            def gather(q, k, nt=GT):
                pool.wait_ge(idx_ready, q + 1)
                plain(pool)
                for t in range(nt):
                    for s in range(TOPK):
                        n = t * TOPK + s
                        pool.indirect_dma_start(gat[k][:, t, s], None, y_rows,
                                                bass.IndirectOffsetOnAxis(gidx[k][:, n:n + 1], 0))\
                            .then_inc(gathered[k], 16)

            def norms3(q):
                rstd(var4_ready, q + 1, rstd1[:, :], var1[:, :], rstd4_ready)

            def step3(q, k, h):
                gather(q + 3, (k + 3) % 2)
                norms3(q + 2)

            gather(0, 0)
            gather(1, 1)
            norms3(0)
            gather(2, 0)
            norms3(1)
            groups(pool, 0, GROUPS - 4, step3)
            one(step3, GROUPS - 4)
            gather(GROUPS, 0, 1)
            for q in range(GROUPS - 1, GROUPS + 1):
                norms3(q)

        @block.vector
        def _(dve):
            dve.memset(ones[:, :], 1.0)
            dve.memset(a_bd[:, :, :], 0.0)
            dve.memset(zeros[:, :], 0.0)
            dve.memset(one_e[:, :], 1.0)
            for buf in (var1, var2):
                dve.memset(buf[:, :], 1.0)
            dve.memset(rstd2[:, :], 1.0).then_inc(memset_done, 1)
            dve.memset(xb[0][64:P, 0:XZ], 0.0).then_inc(x_zeroed, 1)
            dve.memset(wp[64:P, :, :], 0.0).then_inc(wp_zeroed, 1)
            dve.wait_ge(wp_zeroed, 1)
            dve.tensor_copy(wph[64:P, :, :], wp[64:P, 0:XS]).then_inc(wp_zeroed, 1)
            dve.wait_ge(wp_t, PATCH // 4)
            dve.memset(xb[1][64:P], 0.0).then_inc(x_zeroed, 1)
            dve.wait_ge(wph_ready, -(-XS // 4))
            dve.wait_ge(wp_ready, PATCH // 4)
            dve.tensor_tensor(wpl[:, :, :], wp[:, 0:XS], wph[:, :, :], ALU.subtract).then_inc(wpl_ready, 1)
            dve.wait_ge(ld_id, 16)
            dve.wait_ge(ld_const, 16 * N_LOADS)
            n = [0]

            def link(ins):
                n[0] += 1
                ins.then_inc(dve_setup, 1)

            def settle():
                dve.wait_ge(dve_setup, n[0])

            link(dve.tensor_copy(pref[:, :], cst[:, C_PREF:C_PREF + P]))
            link(dve.tensor_copy(base[:, :], cst[:, C_BASE:C_BASE + E]))
            link(dve.tensor_tensor(hcls[:, :], hcls[:, :], pos0[:, :], ALU.mult))
            settle()
            link(dve.bn_stats(st[:, 0], hcls[:, :]))
            settle()
            link(dve.bn_aggr(mv[:, 0], st[:, 0]))
            settle()
            dve.tensor_scalar(var1[:, 0:1], mv[:, 0, 1:2], EPS, None, ALU.add).then_inc(cls_var, 1)
            dve.wait_ge(cls_rstd, 1)
            dve.tensor_scalar(xcls[:, :], hcls[:, :], mv[:, 0, 0:1], rstd1[:, 0:1], ALU.subtract, ALU.mult)\
               .then_inc(xcls_ready, 1)
            dve.wait_ge(xcls_ready, 1)
            link(dve.tensor_scalar(vcls[:, :], xcls[:, :], cst[:, C_CLS:C_CLS + 1], None, ALU.mult))
            dve.wait_ge(cols_ready, 1)
            dve.tensor_scalar(sb2q[:, :], col(V_SB2), SHARED, None, ALU.mult).then_inc(sb2q_ready, 1)
            settle()

            def stats(src, nt, st, mv, link, settle):
                for t in range(nt):
                    ins = dve.bn_stats(st[:, t], src(t))
                settle(link(ins))
                plain(dve)
                for t in range(nt):
                    ins = dve.bn_aggr(mv[:, t], st[:, t])
                settle(link(ins))

            def normalise(dst, src, mv, scale, nt):
                for t in range(nt):
                    ins = dve.tensor_scalar(dst[:, t], src[:, t], mv[:, t, 0:1], scale[:, t:t + 1],
                                            ALU.subtract, ALU.mult)
                return ins

            mask3 = bc(mask.unsqueeze(1), [P, GT, SEQ])

            def attend_norm(g, k, link, settle):
                dve.wait_ge(h_ready, g + 1)
                stats(lambda t: h[k][:, t], GT, st, mv, link, settle)
                dve.tensor_scalar(var1[:, :], mv[:, :, 1], EPS, None, ALU.add).then_inc(var1_ready, 1)

            def x_low(g, k, lo):
                for px in range(lo, lo + XR):
                    dve.wait_ge(xhi_ready, (g - 1) * XS + (px + 1))
                    dve.tensor_tensor(xlo[px % XR], pixels(k, px), xhi[px % XR], ALU.subtract).then_inc(xlo_ready, 1)

            def body(r, k, h_, nt=GT, attn=True, ahead=2):
                m = [0]
                nk = nt * TOPK
                slot = r * nk - nk if nt == GT else PATCH_TILES * TOPK

                def link(ins):
                    m[0] += 1
                    ins.then_inc(dve_step, 1)
                    return m[0]

                def settle(n):
                    dve.wait_ge(dve_step, r * DVE_STEPS + n)

                if attn:
                    dve.wait_ge(t1_done, r + 1)
                    dve.tensor_tensor(h[k][:, :, :], t1, bc(pos_t[:, :].unsqueeze(1), [P, GT, D]), ALU.mult)\
                       .then_inc(h_ready, 1)
                dve.wait_ge(t4_done, r + 1)
                if not (isinstance(r, int) and r == 0):
                    dve.wait_ge(r_ready, r)
                src = h[1 - k][:, 0:nt] if nt == GT else hcls[:, :].unsqueeze(1)
                h2_step = link(dve.scalar_tensor_tensor(out=h2[:, 0:nt], in0=t4[:, 0:nt], scalar=0.5, in1=src,
                                                        op0=ALU.mult, op1=ALU.add))
                if attn:
                    attend_norm(r, k, link, settle)
                settle(h2_step)
                stats(lambda t: h2[:, t], nt, st2, mv2, link, settle)
                dve.tensor_scalar(var2[:, 0:nt], mv2[:, 0:nt, 1], EPS, None, ALU.add)
                dve.tensor_scalar(var2[:, GT:GT + nt], mv2[:, 0:nt, 1], 1.0 + EPS, EPS * EPS, ALU.mult, ALU.add)\
                   .then_inc(var2_ready, 1)
                if attn:
                    dve.wait_ge(rstd1_ready, r + 1)
                    normalise(xh, h[k], mv, rstd1, GT).then_inc(xh_ready, 1)
                dve.wait_ge(rstd2_ready, r + 1)
                dve.wait_ge(z_free[k], h_ * (16 * TOPK * GT) + 16 - (0 if k == 1 or nt == 1 else 16 * TOPK * (GT - 1)))
                normalise(z[k], h2, mv2, rstd2[:, GT:2 * GT], nt).then_inc(z_ready, 1)
                link(dve.tensor_scalar(rs1[:, 0:nt], rstd2[:, 0:nt], 1.0, None, ALU.add))
                settle(link(dve.tensor_tensor(rs2[:, 0:nt], mv2[:, 0:nt, 0], rstd2[:, 0:nt], ALU.mult)))
                dve.tensor_scalar(rs2[:, 0:nt], rs2[:, 0:nt], -1.0, 0.5, ALU.mult, ALU.add).then_inc(rs_ready, 1)
                if attn:
                    dve.wait_ge(xh_ready, r + 1)
                    dve.scalar_tensor_tensor(out=vp[:, :, :], in0=xh[:, :, :], scalar=cst[:, C_KEEP:C_KEEP + 1],
                                             in1=bc(vcls[:, :].unsqueeze(1), [P, GT, D]), op0=ALU.mult,
                                             op1=ALU.add).then_inc(vp_ready, 1)
                    if ahead:
                        x_low(r + 1, 1 - k, XR)
                    dve.wait_ge(s_done, r + 1)
                    s_step = link(dve.tensor_tensor(s_t[:, :, :], s_ps, mask3, ALU.mult))
                dve.wait_ge(l_done, r + 1)
                lg_step = link(dve.tensor_tensor(lg[:, 0:nt], l_ps[:, 0:nt], bc(rb[:, :].unsqueeze(1), [P, nt, E]), ALU.add))
                if attn:
                    settle(s_step)
                    s_step = link(dve.tensor_reduce(mx[:, :], s_t[:, :, :], AX.X, ALU.max))
                settle(lg_step)
                plain(dve)
                for t in range(nt):
                    ins = dve.max(m8[:, t], lg[:, t])
                m8_step = link(ins)
                if attn:
                    settle(s_step)
                    dve.tensor_tensor(s_t[:, :, :], s_t[:, :, :], bc(mx[:, :].unsqueeze(2), [P, GT, SEQ]),
                                      ALU.subtract).then_inc(smax_ready, 1)
                settle(m8_step)
                plain(dve)
                for t in range(nt):
                    ins = dve.max_index(i8[:, t], m8[:, t], lg[:, t])
                i8_step = link(ins)
                top = m8[:, 0:nt, 0:1]
                dve.tensor_tensor(d18[:, 0:nt, 0:E], lg[:, 0:nt], bc(top, [P, nt, E]), ALU.subtract)
                dve.tensor_tensor(d18[:, 0:nt, E:E + TOPK], m8[:, 0:nt, 0:TOPK], bc(top, [P, nt, TOPK]),
                                  ALU.subtract).then_inc(gate_ready, 1)
                settle(i8_step)
                settle(link(dve.tensor_copy(i2[:, 0:nk].rearrange("p (t k) -> p t k", k=TOPK), i8[:, 0:nt, 0:TOPK])))
                settle(link(dve.tensor_tensor(oh[:, 0:nk], bc(iota.unsqueeze(1), [P, nk, E]),
                                              bc(i2[:, 0:nk].unsqueeze(2), [P, nk, E]), ALU.is_equal)))
                oh4 = oh[:, 0:nk].rearrange("p (t k) e -> p t k e", k=TOPK)
                dve.tensor_tensor(m2[:, 0:nt], oh4[:, :, 0], oh4[:, :, 1], ALU.add).then_inc(m2_ready, 1)
                if attn:
                    dve.wait_ge(e_ready, r + 1)
                    sm_step = link(dve.tensor_reduce(sm[:, :], e_t[:, :, :], AX.X, ALU.add))
                    e_step = link(dve.tensor_tensor(s_t[:, :, :], e_t[:, :, :], mask3, ALU.mult))
                    settle(sm_step)
                    settle(link(dve.reciprocal(rsm[:, :], sm[:, :])))
                    settle(e_step)
                    for i in range(2):
                        q = slice(i * SEQ, (i + 1) * SEQ)
                        ins = dve.tensor_tensor(a_bd[q, :, q], s_t[q], bc(rsm[q, :].unsqueeze(2), [SEQ, GT, SEQ]), ALU.mult)
                    ins.then_inc(a_ready, 1)
                    if ahead > 1:
                        x_low(r + 2, k, 0)
                dve.wait_ge(gexp_ready, r + 1)
                gsm_step = link(dve.tensor_reduce(gsm[:, 0:nt], d18[:, 0:nt, 0:E], AX.X, ALU.add))
                dve.wait_ge(p_done, r + 1)
                base4 = bc(base[:, :].unsqueeze(1), [P, nt, E])
                for s in range(TOPK):
                    ins = dve.tensor_tensor(pp[:, 0:nt, s], p_ps[:, 0:nt], base4, ALU.add)
                pp_step = link(ins)
                settle(gsm_step)
                gsm_step = link(dve.reciprocal(rgsm[:, 0:nt], gsm[:, 0:nt]))
                settle(pp_step)
                link(dve.tensor_tensor(base[:, :], base[:, :], p_ps[:, nt], ALU.add))
                pk = pp[:, 0:nt].rearrange("p t k e -> p (t k) e")
                pp_step = link(dve.tensor_tensor(pk, pk, oh[:, 0:nk], ALU.mult))
                settle(gsm_step)
                w_out = w_all[:, bass.ds(slot, nk)].rearrange("p (t k) -> p t k", k=TOPK)
                dve.tensor_tensor(w_out, d18[:, 0:nt, E:E + TOPK], bc(rgsm[:, 0:nt].unsqueeze(2), [P, nt, TOPK]), ALU.mult)
                settle(pp_step)
                settle(link(dve.tensor_reduce(posf[:, 0:nk], pk, AX.X, ALU.add)))
                dve.tensor_copy(pos_all[:, bass.ds(slot, nk)], posf[:, 0:nk])
                dve.tensor_copy(posg[k][:, 0:nk], posf[:, 0:nk]).then_inc(pos_ready, 1)
                assert m[0] == A_STEPS * attn + R_STEPS, m[0]

            x_low(1, 1, 0)
            body(0, 0, 0, nt=1)
            groups(dve, 1, GROUPS - 3, body)
            one(body, GROUPS - 3)
            body(GROUPS - 2, 0, GROUPS // 2 - 1, ahead=1)
            body(GROUPS - 1, 1, GROUPS // 2 - 1, ahead=0)
            dve.wait_ge(dve_step, GROUPS * DVE_STEPS)
            dve.tensor_copy(tail[:, :], base[0:1, :]).then_inc(tail_ready, 1)
            body(GROUPS, 0, GROUPS // 2, attn=False)
            dve.wait_ge(dve_step, GROUPS * DVE_STEPS + R_STEPS)
            n[0] = 0

            def tlink(ins):
                n[0] += 1
                ins.then_inc(tab_step, 1)
                dve.wait_ge(tab_step, n[0])

            ebase = cst[:, C_BASE:C_BASE + E]
            tlink(dve.tensor_tensor(cnt[:, :], base[:, :], ebase, ALU.subtract))
            tlink(dve.tensor_scalar(cnti[:, :], cnt[:, :], float(EROWS - 1), None, ALU.add))
            tlink(dve.tensor_scalar(nti[:, :], cnti[:, :], EROWS.bit_length() - 1, None, ALU.arith_shift_right))
            tlink(dve.tensor_copy(nt[:, :], nti[:, :]))
            tlink(dve.memset(dsh[:, :], 0.0))
            tlink(dve.tensor_scalar(dsh[:, 1:E], nt[:, 0:E - 1], float(EROWS), float(-CAP), ALU.mult, ALU.add))
            tlink(dve.tensor_tensor_scan(cum[:, :], one_e[:, :], nt[:, :], 0.0, ALU.mult, ALU.add))
            tlink(dve.tensor_scalar(cmp[:, :], cum[:, :], cst[:, C_TILE:C_TILE + 1], None, ALU.is_le))
            tlink(dve.tensor_reduce(ejt[:, 0:1], cmp[:, :], AX.X, ALU.add))
            tlink(dve.tensor_tensor(cmp[:, :], cmp[:, :], nt[:, :], ALU.mult))
            tlink(dve.tensor_reduce(tj[:, :], cmp[:, :], AX.X, ALU.add))
            tlink(dve.tensor_scalar(tj[:, :], tj[:, :], cst[:, C_TILE:C_TILE + 1], float(-EROWS), ALU.subtract, ALU.mult))
            dve.scalar_tensor_tensor(out=ejt[:, 1:2], in0=ejt[:, 0:1], scalar=float(CAP), in1=tj[:, :], op0=ALU.mult,
                                     op1=ALU.add).then_inc(ejt_ready, 1)
            dve.wait_ge(tej_done, 1)
            tlink(dve.tensor_scalar(ejc[:, :], bank[6][0:1, 0:EXPERT_TILES], float(E - 1), None, ALU.min))
            dve.tensor_copy(rowj[:, :], bank[6][0:1, P:P + EXPERT_TILES]).then_inc(tab_ready, 1)
            grid = [P, TILES * TOPK, E]
            dve.tensor_tensor(past, bc(pos_all[:, :].unsqueeze(2), grid), bc(ebase.unsqueeze(1), grid), ALU.is_ge)\
               .then_inc(past_ready, 1)

            dve.wait_ge(tab_ready, 1)

            def down_bias(j, n):
                ex = dve.value_load(ejc[0:1, bass.ds(j, 1)], min_val=0, max_val=E - 1)
                bias = cols[:, bass.ds(ex + V_EB2, 1)]
                dve.wait_ge(down_done, j + 1)
                dve.tensor_scalar(eyT[n % 2], bank[5 + n % 2][:, 0:EROWS], bias, None, ALU.add).then_inc(eyT_ready, 1)

            def rows_out(j, n, h_):
                if n > 1:
                    dve.wait_ge(y_free[n % 2], h_ * 16)
                dve.wait_ge(tout_done, j + 1)
                dve.tensor_copy(yout[n % 2], bank[7][:, 0:EROWS].rearrange("p (h d) -> p h d", h=EH)).then_inc(yout_ready, 1)

            def split_w1(j, n, h):
                dve.wait_ge(up_done, j * EC - EC) if n > 1 else None
                dve.wait_ge(w1_loaded[n % 4], h * 16 + 16)
                dve.tensor_copy(w1h[n % 2], w1b[n % 4]).then_inc(w1h_ready, 1)
                dve.wait_ge(w1h_ready, j + 1)
                dve.tensor_tensor(w1l[n % 2], w1b[n % 4], w1h[n % 2], ALU.subtract).then_inc(w1l_ready, 1)

            def split_rows(j, n):
                dve.wait_ge(up_done, j * EC - EC) if n > 1 else None
                dve.wait_ge(h2T_ready, j + 1)
                dve.tensor_copy(h2h[n % 2], h2T[n % 2]).then_inc(h2h_ready, 1)
                dve.wait_ge(h2h_ready, j + 1)
                dve.tensor_tensor(h2l[n % 2], h2T[n % 2], h2h[n % 2], ALU.subtract).then_inc(h2l_ready, 1)

            def step2(j, n, q=0):
                static = isinstance(j, int)
                if not static or j + 1 < EXPERT_TILES:
                    split_rows(j + 1, n + 1)
                if n >= 2:
                    rows_out(j - 2, n - 2, q * 2 + (n - 2) // 2)
                if not static or j + 2 < EXPERT_TILES:
                    split_w1(j + 2, n + 2, q + (n + 2) // 4)
                if n >= 1 and not (static and j > EXPERT_TILES):
                    down_bias(j - 1, n - 1)

            split_rows(0, 0)
            split_w1(0, 0, 0)
            split_w1(1, 1, 0)
            for j in range(4):
                step2(j, j)
            dve.wait_ge(shift_ready, 1)
            tlink(dve.tensor_reduce(shift[:, :], past, AX.X, ALU.add))
            tlink(dve.tensor_tensor(pos_all[:, :], pos_all[:, :], shift[:, :], ALU.add))
            with dve.Fori(1, EXPERT_TILES // 4 - 1) as i:
                for n in range(4):
                    step2(i * 4 + n, 4 + n, i - 1)
            for j in range(EXPERT_TILES - 4, EXPERT_TILES + 2):
                step2(j, j)

            def copy_idx(q, k, nt=GT):
                dve.tensor_copy(gidx[k][:, 0:nt * TOPK], pos_all[:, bass.ds(q * (GT * TOPK), nt * TOPK)]).then_inc(idx_ready, 1)

            def mix(q, k, h_, nt=GT):
                m = [0]

                def link(ins):
                    m[0] += 1
                    ins.then_inc(dve_step3, 1)
                    return m[0]

                def settle(n):
                    dve.wait_ge(dve_step3, q * DVE_STEPS3 + n)

                dve.wait_ge(gathered[k], h_ * (16 * GT * TOPK) + 16 * nt * TOPK)
                dve.wait_ge(tsh_done, q + 1)
                if not (isinstance(q, int) and q == 0):
                    dve.wait_ge(z4_ready, q)
                tsh = tiles_of(6)
                for s in range(TOPK):
                    for t in range(nt):
                        w = w_all[:, bass.ds(q * (GT * TOPK) + (t * TOPK + s), 1)]
                        ins = dve.scalar_tensor_tensor(out=moe[:, t], in0=gat[k][:, t, s], scalar=w,
                                                       in1=tsh[:, t] if s == 0 else moe[:, t], op0=ALU.mult, op1=ALU.add)
                    settle(link(ins)) if s == 0 else ins.then_inc(mix_done, 1)
                dve.wait_ge(mix_done, q + 1)
                stats(lambda t: moe[:, t], nt, st, mv, link, settle)
                dve.tensor_scalar(var1[:, 0:nt], mv[:, 0:nt, 1], EPS, None, ALU.add).then_inc(var4_ready, 1)
                res = r_res[:, bass.ds(q * GTOK, nt * D)].rearrange("p (t d) -> p t d", t=nt)
                res_step = link(dve.tensor_tensor(res, res, moe[:, 0:nt], ALU.add))
                dve.wait_ge(rstd4_ready, q + 1)
                if not (isinstance(q, int) and q == 0):
                    dve.wait_ge(tz_done, q)
                normalise(z4, moe, mv, rstd1, nt).then_inc(z4_ready, 1)
                settle(res_step)
                assert m[0] == DVE_STEPS3, m[0]

            def out3(q, nt=GT):
                dve.wait_ge(tout3_done, q + 1)
                res = r_res[:, bass.ds(q * GTOK, nt * D)].rearrange("p (t d) -> p t d", t=nt)
                dve.tensor_tensor(res, tiles_of(7)[:, 0:nt], res, ALU.add).then_inc(out_ready, 1)

            def step3(q, k, h_):
                mix(q + 2, k, h_ + 1)
                copy_idx(q + 4, k)
                out3(q)

            dve.sem_inc(out_ready, 1)
            dve.wait_ge(r_loaded, 16 * (GROUPS + 1))
            for q in range(3):
                copy_idx(q, q % 2) if q < 2 else None
            mix(0, 0, 0)
            copy_idx(2, 0)
            mix(1, 1, 0)
            copy_idx(3, 1)
            groups(dve, 0, GROUPS - 4, step3)
            mix(GROUPS - 2, 0, (GROUPS - 2) // 2)
            copy_idx(GROUPS, 0, 1)
            out3(GROUPS - 4)
            mix(GROUPS - 1, 1, (GROUPS - 1) // 2)
            out3(GROUPS - 3)
            mix(GROUPS, 0, GROUPS // 2, 1)
            for q in range(GROUPS - 2, GROUPS):
                out3(q)
            out3(GROUPS, 1)

        @block.tensor
        def _(pe):
            pe.wait_ge(ld_id, 16)
            pe.wait_ge(memset_done, 2)
            pe.wait_ge(ld_w, 16)
            for px in range(PATCH):
                ins = pe.transpose(bank[px // 4][0:KROWS, (px % 4) * P:(px % 4 + 1) * P],
                                   wnat[:, :, :, px].rearrange("h c y -> h (c y)"), ident)
                if px % 4 == 3:
                    ins.then_inc(wp_t, 1)
            pe.wait_ge(wp_ready, PATCH // 4)
            WARM = 10

            def patch(g, k, h, lo, hi):
                if lo == 0:
                    pe.wait_ge(x_loaded[k], h * (16 * XLOADS) + 16 * XLOADS)
                for n in range(lo, hi):
                    px = PX_ORDER[n]
                    if px >= XS or (isinstance(g, int) and g == 0):
                        ins = pe.matmul(pa[:, :], wp[:, px], pixels(k, px), start=n == 0, stop=n == PATCH - 1)
                        continue
                    pe.wait_ge(xlo_ready, (g - 1) * XS + (px + 1))
                    u = px % XR
                    pe.matmul(pa[:, :], wph[:, px], xhi[u], start=n == 0, stop=False)
                    pe.matmul(pa[:, :], wph[:, px], xlo[u], start=False, stop=False)
                    pe.matmul(pa[:, :], wpl[:, px], xhi[u], start=False, stop=False).then_inc(xparts_used, 1)
                if hi == PATCH:
                    ins.then_inc(patch_done, 1)

            def transposes(dst, src, nt, done):
                for t in range(nt):
                    ins = pe.transpose(dst(t), src(t), ident)
                ins.then_inc(done, 1)

            def scores(g):
                pe.wait_ge(xT_ready, g + 1)
                for t in range(GT):
                    for i in range(2):
                        at = t * P + i * SEQ
                        pe.matmul(s_ps[i * SEQ:(i + 1) * SEQ, t, 0:SEQ - 1], xT[:, at:at + SEQ], xT[:, at:at + SEQ - 1],
                                  start=True, stop=True)
                    ins = pe.matmul(s_ps[:, t, SEQ - 1:SEQ], xT[:, t * P:(t + 1) * P], xclsT[:, 0:1], start=True, stop=True)
                ins.then_inc(s_done, 1)

            def context(g):
                pe.wait_ge(vp_ready, g + 1)
                pe.wait_ge(aT_ready, g + 1)
                for t in range(GT):
                    ins = pe.matmul(c_ps[:, t * P:(t + 1) * P], vp[:, t], aT[:, t * P:(t + 1) * P], start=True, stop=True)
                ins.then_inc(c_done, 1)

            def t_th(g, nt=GT):
                pe.wait_ge(th_ready, g + 1)
                transposes(lambda t: t4[:, t], lambda t: th[:, t * P:(t + 1) * P], nt, t4_done)

            def t_zz(g, k, nt=GT):
                pe.wait_ge(z_ready, g + 1)
                transposes(lambda t: t5[:, t * P:(t + 1) * P], lambda t: z[k][:, t], nt, t5_done)

            def gates(g, k, nt=GT):
                pe.wait_ge(hT_ready, g + 1)
                for t in range(nt):
                    ins = pe.matmul(l_ps[:, t], hT[k][:, t * P:(t + 1) * P], rw[:, :], start=True, stop=True)
                ins.then_inc(l_done, 1)

            def ranks(g, nt=GT):
                pe.wait_ge(m2_ready, g + 1)
                pe.matmul(p_ps[:, 0:nt], pref[:, :], m2[:, 0:nt], start=True, stop=False)
                ins = pe.matmul(p_ps[:, nt], ones[:, :], m2[:, nt - 1], start=False, stop=nt == 1)
                for s in range(nt - 1):
                    if s == 0:
                        pe.matmul(p_ps[:, 1:nt], ones[:, :], m2[:, 0:nt - 1], start=False, stop=False)
                    else:
                        pe.matmul(p_ps[:, 1 + s:nt + 1], ones[:, :], m2[:, 0:nt - s], start=False, stop=False)
                if nt > 1:
                    ins = pe.matmul(p_ps[:, nt], ones[:, :], m2[:, 0], start=False, stop=True)
                ins.then_inc(p_done, 1)

            CUT = [13, 24, 25, PATCH]

            def body(g, k, h, ahead=True, nt=GT):
                slot = [0, 0]

                def patches():
                    if ahead:
                        patch(g + 1, 1 - k, h + k, slot[1], CUT[slot[0]])
                    slot[:] = slot[0] + 1, CUT[slot[0]]

                pe.wait_ge(hF_ready, g + 1)
                transposes(lambda t: t1[:, t], lambda t: hF[:, t * P:(t + 1) * P], GT, t1_done)
                t_th(g, nt)
                patches()
                pe.wait_ge(xh_ready, g + 1)
                transposes(lambda t: t2[:, t * P:(t + 1) * P], lambda t: xh[:, t], GT, t2_done)
                t_zz(g, k, nt)
                scores(g)
                gates(g, k, nt)
                patches()
                ranks(g, nt)
                patches()
                pe.wait_ge(a_ready, g + 1)
                transposes(lambda t: t3[:, t * P:(t + 1) * P], lambda t: a_bd[:, t], GT, t3_done)
                patches()
                context(g)
                pe.matmul(w_ps[:, :], wc[:, 1], xT[:, :], start=True, stop=False)
                pe.wait_ge(cT_ready, g + 1)
                pe.matmul(w_ps[:, :], wc[:, 0], cT[:, :], start=False, stop=True).then_inc(w_done, 1)

            for _ in range(WARM):
                pe.matmul(bank[1][:, :], a_bd[:, 0], a_bd[:, :].rearrange("p t d -> p (t d)"), start=True, stop=True)
            patch(0, 0, 0, 0, PATCH)
            pe.wait_ge(ld_const, 16 * N_LOADS)
            pe.transpose(bank[7][:, 0:V_END], vecs[:, :], ident[0:V_END, 0:V_END]).then_inc(setup_t, 1)
            pe.wait_ge(cols_ready, 1)
            pe.wait_ge(xcls_ready, 1)
            pe.transpose(bank[7][:, P:2 * P], xcls[:, :], ident).then_inc(setup_t, 1)
            pe.wait_ge(xclsT_ready, 1)
            pe.matmul(w_ps[:, 0:P], wc[:, 1], xclsT[:, :], start=True, stop=True).then_inc(w_done, 1)
            pe.wait_ge(wpl_ready, 1)
            body(0, 0, 0, nt=1)
            groups(pe, 1, GROUPS - 1, body)
            body(GROUPS - 1, 1, GROUPS // 2 - 1, ahead=False)
            t_th(GROUPS)
            t_zz(GROUPS, 0)
            gates(GROUPS, 0)
            ranks(GROUPS)
            pe.wait_ge(ejt_ready, 1)
            for c in range(2):
                ins = pe.transpose(bank[6][0:1, c * P:(c + 1) * P], ejt[:, c:c + 1], ident)
            ins.then_inc(tej_done, 1)


            def t_in(j, n, h):
                pe.wait_ge(zin_loaded[n % 4], h * 16 + 16)
                if n > 0:
                    pe.wait_ge(h2T_ready, j)
                for i in range(EH):
                    ins = pe.transpose(bank[0][:, i * P:(i + 1) * P], zin[n % 4][:, i], ident)
                ins.then_inc(tin_done, 1)

            def t_out(j, n):
                pe.wait_ge(eyT_ready, j + 1)
                if n > 0:
                    pe.wait_ge(yout_ready, j)
                for i in range(EH):
                    ins = pe.transpose(bank[7][:, i * P:(i + 1) * P], eyT[n % 2][:, i * P:(i + 1) * P], ident)
                ins.then_inc(tout_done, 1)

            def up(j, n, h):
                pe.wait_ge(h2l_ready, j + 1)
                pe.wait_ge(w1l_ready, j + 1)
                terms = ((w1h, h2h), (w1h, h2l), (w1l, h2h))
                for c in range(EC):
                    if n > 0:
                        pe.wait_ge(eh_ready, j * EC + (c + 1 - EC))
                    for i, (w, v) in enumerate(terms):
                        ins = pe.matmul(bank[1 + c][:, 0:EROWS], w[n % 2][:, c * P:(c + 1) * P], v[n % 2],
                                        start=i == 0, stop=i == len(terms) - 1)
                    ins.then_inc(up_done, 1)

            def down(j, n, h):
                pe.wait_ge(w2_loaded[n % 4], h * 16 + 16)
                for c in range(EC):
                    pe.wait_ge(eh_ready, j * EC + c + 1)
                    ins = pe.matmul(bank[5 + n % 2][:, 0:EROWS], w2b[n % 4][:, c], ehT[n % 2][:, c],
                                    start=c == 0, stop=c == EC - 1)
                ins.then_inc(down_done, 1)

            def step2(j, n, h, first=0):
                if not (isinstance(j, int) and j + 1 >= EXPERT_TILES):
                    t_in(j + 1, n + 1, h + (n % 4 + 1) // 4)
                if not (isinstance(j, int) and j >= EXPERT_TILES):
                    up(j, n, h)
                if n - 2 >= first:
                    t_out(j - 2, n - 2)
                if n - 1 >= first and not (isinstance(j, int) and j > EXPERT_TILES):
                    down(j - 1, n - 1, h - (n % 4 == 0))

            t_in(0, 0, 0)
            for j in range(4):
                step2(j, j, 0)
            with pe.Fori(1, EXPERT_TILES // 4 - 1) as i:
                for n in range(4):
                    step2(i * 4 + n, 4 + n, i)
            for j in range(EXPERT_TILES - 4, EXPERT_TILES + 2):
                step2(j, j, j // 4)


            def sh_up(q, k, h, n, nt=GT):
                pe.wait_ge(ht_loaded[k], h * 16 + 16)
                for c in range(SC):
                    if not (isinstance(n, int) and n + c < 3):
                        pe.wait_ge(u_used, n + c - 2)
                    pe.matmul(bank[(4 + c) % 3][:, 0:nt * P], sw1_t[:, c * P:(c + 1) * P], ht3[k][:, 0:nt * P],
                              start=True, stop=True).then_inc(u_done, 1)

            def sh_down(q, n, nt=GT):
                pe.wait_ge(u_used, n)
                for c in range(SC):
                    ins = pe.matmul(bank[3][:, 0:nt * P], sw2_t[:, c], shs[:, c, 0:nt * P], start=c == 0, stop=c == SC - 1)
                ins.then_inc(shd_done, 1)

            def t_sh(q, nt=GT):
                pe.wait_ge(shF_ready, q + 1)
                transposes(lambda t: bank[6][:, t * P:(t + 1) * P], lambda t: shF[:, t * P:(t + 1) * P], nt, tsh_done)

            def t_z(q, nt=GT):
                pe.wait_ge(z4_ready, q + 1)
                transposes(lambda t: bank[5][:, t * P:(t + 1) * P], lambda t: z4[:, t], nt, tz_done)

            def ff_up(q, n, nt=GT, tail=False):
                pe.wait_ge(h4T_ready, q + 1)
                for c in range(EC):
                    pe.wait_ge(u_used, n if tail and c == 0 else n + (c - 2))
                    pe.matmul(bank[c % 3][:, 0:nt * P], fw1_t[:, c * P:(c + 1) * P], h4T[:, 0:nt * P],
                              start=True, stop=True).then_inc(u_done, 1)

            def ff_down(q, n, nt=GT):
                for c in range(EC):
                    pe.wait_ge(u_used, n + c + 1)
                    ins = pe.matmul(bank[4][:, 0:nt * P], fw2_t[:, c], ffs[:, c, 0:nt * P], start=c == 0, stop=c == EC - 1)
                ins.then_inc(ffd_done, 1)

            def t_out3(q, nt=GT):
                pe.wait_ge(oF_ready, q + 1)
                pe.wait_ge(out_ready, q + 1)
                transposes(lambda t: bank[7][:, t * P:(t + 1) * P], lambda t: oF[:, t * P:(t + 1) * P], nt, tout3_done)

            pe.wait_ge(w3_loaded, 64)
            for q in range(3):
                if q > 0:
                    pe.wait_ge(u_used, SC * q)
                sh_up(q, q % 2, q // 2, SC * q) if q == 0 else sh_up(q, q % 2, q // 2, SC * q + 1)
                if q < 2:
                    sh_down(q, SC * (q + 1))
                    if q == 1:
                        pe.wait_ge(mix_done, 1)
                    t_sh(q)
            t_z(0)

            def step3(q, k, h, sh3=GT, sh2=GT, z1=GT, now=GT, n=None):
                tail = n is not None
                n = q * 6 + 6 if n is None else n
                ff_up(q, n, now, tail)
                if sh2:
                    sh_down(q + 2, n, sh2)
                if z1:
                    t_z(q + 1, z1)
                ff_down(q, n, now)
                if sh2:
                    t_sh(q + 2, sh2)
                if sh3:
                    sh_up(q + 3, (k + 3) % 2, h + (k + 3) // 2, n + 4, sh3)
                t_out3(q, now)

            groups(pe, 0, GROUPS - 4, step3)
            one(step3, GROUPS - 4)
            step3(GROUPS - 3, 1, (GROUPS - 3) // 2, sh3=1)
            last = (GROUPS - 3) * 6 + 12
            step3(GROUPS - 2, 0, (GROUPS - 2) // 2, sh3=0, sh2=1, n=last)
            step3(GROUPS - 1, 1, (GROUPS - 1) // 2, sh3=0, sh2=0, z1=1, n=last + EC)
            step3(GROUPS, 0, GROUPS // 2, sh3=0, sh2=0, z1=0, now=1, n=last + 2 * EC)


_INS = ["x", "L0_tok_W", "L0_tok_b", "L0_tok_class_token", "L0_tok_pos_embed", "L0_attn_W_c", "L0_ffn_ln_in_g",
        "L0_ffn_ln_in_b", "L0_ffn_router_w", "L0_ffn_router_b", "L0_ffn_ew1", "L0_ffn_eb1", "L0_ffn_ew2", "L0_ffn_eb2",
        "L0_ffn_sw1", "L0_ffn_sb1", "L0_ffn_sw2", "L0_ffn_sb2", "L0_ffn_ff_ln_g", "L0_ffn_ff_ln_b", "L0_ffn_ff_w1",
        "L0_ffn_ff_b1", "L0_ffn_ff_w2", "L0_ffn_ff_b2"]


def kernel(**inputs):
    import numpy as _np
    import concourse.bacc as _bacc
    from concourse import mybir as _mybir
    from concourse.bass_utils import run_bass_kernel_spmd as _run

    nc = _bacc.Bacc("TRN2", target_bir_lowering=False, num_devices=1)
    arrays, args = {"consts": constants()}, []
    for name in _INS:
        arrays[f"in_{name}"] = _np.ascontiguousarray(inputs[name])
    for name, a in arrays.items():
        args.append(nc.dram_tensor(name, a.shape, _mybir.dt.from_np(a.dtype), kind="ExternalInput").ap())
    out = nc.dram_tensor("out_0", (BATCH, SEQ + 1, D), _mybir.dt.float32, kind="ExternalOutput").ap()
    build(nc, *args, out)
    r = _run(nc, [arrays], core_ids=[0])
    return r.results[0]["out_0"]
```

```python
from contextlib import ExitStack

import numpy as np

import concourse.bass as bass
from concourse import mybir

F32 = mybir.dt.float32
F32R = mybir.dt.float32r
BF16 = mybir.dt.bfloat16
U32 = mybir.dt.uint32
I32 = mybir.dt.int32
ALU = mybir.AluOpType
ACT = mybir.ActivationFunctionType
AX = mybir.AxisListType

P = 128
D = 128
BATCH, CH, IMG, PATCH = 128, 3, 224, 28
NP = IMG // PATCH
SEQ = NP * NP
KROWS = CH * PATCH
PATCH_TILES = BATCH * SEQ // P
TILES = PATCH_TILES + 1
GT = 4
GTOK = GT * P
GIMG = GTOK // SEQ
GROUPS = PATCH_TILES // GT
TOKENS = TILES * P
E, DH, DS = 16, 512, 256
EC, SC = DH // P, DS // P
TOPK = 2
TEMP = 0.7
SHARED = 0.25
EPS = 1e-5
EROWS = 256
EH = EROWS // P
CAP = -(-TOKENS // EROWS) * EROWS + EROWS
EXPERT_TILES = (TOKENS * TOPK + E * (EROWS - 1)) // EROWS
SPARE_TILES = EXPERT_TILES - TOKENS * TOPK // EROWS
ZROWS = E * CAP + SPARE_TILES * EROWS
XLOADS = GIMG * CH
XS, XR = 10, 5
PX_ORDER = [*range(XR), *range(XS, XS + 8), *range(XR, XS), *range(XS + 8, PATCH)]
N_LOADS = 18

C_ID, C_MASK, C_CLS, C_KEEP, C_IOTA, C_PREF, C_BASE, C_TILE = 0, 128, 192, 193, 194, 210, 338, 354
C_END = C_TILE + 1

V_EB1, V_EB2 = 0, E * EC
V_SB1 = V_EB2 + E
V_SB2 = V_SB1 + SC
V_FB1 = V_SB2 + 1
V_FB2 = V_FB1 + EC
V_LG, V_LB, V_FG, V_FB, V_TB = V_FB2 + 1, V_FB2 + 2, V_FB2 + 3, V_FB2 + 4, V_FB2 + 5
V_END = V_TB + 1


def constants():
    c = np.zeros((P, C_END), np.float32)
    c[:, C_ID:C_ID + P] = np.eye(P)
    row = np.arange(P) % SEQ
    c[:, C_MASK:C_MASK + SEQ] = np.arange(SEQ)[None] < row[:, None]
    c[:, C_MASK + SEQ - 1] = 1
    c[:, C_CLS] = row == SEQ - 1
    c[:, C_KEEP] = row != SEQ - 1
    c[:, C_IOTA:C_IOTA + E] = np.arange(E)
    c[:, C_PREF:C_PREF + P] = np.arange(P)[:, None] < np.arange(P)[None]
    c[:, C_BASE:C_BASE + E] = np.arange(E) * CAP
    c[:, C_TILE] = np.arange(P)
    return c


def build(nc, consts, x, tok_w, tok_b, cls_tok, pos, w_c, ln_g, ln_b, r_w, r_b, ew1, eb1, ew2, eb2,
          sw1, sb1, sw2, sb2, f_g, f_b, fw1, fb1, fw2, fb2, out):
    with ExitStack() as ctx:
        def sb(name, shape, dt=F32):
            return ctx.enter_context(nc.sbuf_tensor(name, shape, dt))

        def sem(name):
            return ctx.enter_context(nc.semaphore(name))

        def dram(name, shape, dt=F32):
            return nc.dram_tensor(name, shape, dt, kind="Internal").ap()

        z_rows = dram("z_rows", [ZROWS, D])
        y_rows = dram("y_rows", [EXPERT_TILES * EROWS, D])
        r_dram = dram("r_dram", [P, TILES, D])
        ht_dram = dram("ht_dram", [P, TILES, P])

        cst = sb("cst", [P, C_END])
        ident = cst[:, C_ID:C_ID + P]
        mask = cst[:, C_MASK:C_MASK + SEQ]
        iota = cst[:, C_IOTA:C_IOTA + E]
        pref = sb("pref", [P, P], BF16)
        ones = sb("ones", [P, P], BF16)
        neghalf = sb("neghalf", [P, 2 * GT])
        spare = sb("spare", [P, 1])
        vecs = sb("vecs", [V_END, D])
        cols = sb("cols", [P, V_END])
        sb2q = sb("sb2q", [P, 1])
        pos_t = sb("pos_t", [P, D])
        wp = sb("wp", [P, PATCH, D])
        wc = sb("wc", [P, 2, D])
        rw = sb("rw", [P, E])
        rb = sb("rb", [P, E])
        hcls = sb("hcls", [P, D])
        pos0 = sb("pos0", [P, D])
        xcls = sb("xcls", [P, D])
        xclsT = sb("xclsT", [P, P])
        vcls = sb("vcls", [P, D])
        pos_all = sb("pos_all", [P, TILES * TOPK])
        w_all = sb("w_all", [P, TILES * TOPK])
        shift = sb("shift", [P, TILES * TOPK])
        base = sb("base", [P, E])

        XCOLS = GIMG * NP * IMG
        XZ = XCOLS // 4
        region = sb("region", [P, 2 * XCOLS])
        xb = [region[:, u * XCOLS:(u + 1) * XCOLS] for u in range(2)]
        wnat = region[:, XCOLS:XCOLS + CH * PATCH * PATCH].rearrange("h (c y x) -> h c y x", c=CH, y=PATCH)
        carved = [0]

        def carve(n):
            carved[0] += n
            assert carved[0] <= 2 * XCOLS
            return region[:, carved[0] - n:carved[0]]

        W = EC * P
        w1b = [carve(W) for _ in range(4)]
        w2b = [carve(W).rearrange("p (c d) -> p c d", c=EC) for _ in range(4)]
        zin = [carve(EH * D).rearrange("p (h d) -> p h d", h=EH) for _ in range(4)]
        h2T = [carve(EROWS) for _ in range(2)]
        ehT = [carve(EC * EROWS).rearrange("p (c r) -> p c r", c=EC) for _ in range(2)]
        eyT = [carve(EROWS) for _ in range(2)]
        yout = [carve(EH * D).rearrange("p (h d) -> p h d", h=EH) for _ in range(2)]
        sw1_t = carve(DS)
        sw2_t = carve(SC * D).rearrange("p (c d) -> p c d", c=SC)
        fw1_t = carve(DH)
        fw2_t = carve(EC * D).rearrange("p (c d) -> p c d", c=EC)
        gat = [carve(GT * TOPK * D).rearrange("p (t k d) -> p t k d", t=GT, k=TOPK) for _ in range(2)]
        shs = carve(SC * GTOK).rearrange("p (c r) -> p c r", c=SC)
        shF = carve(GTOK)
        moe = carve(GT * D).rearrange("p (t d) -> p t d", t=GT)
        z4 = carve(GT * D).rearrange("p (t d) -> p t d", t=GT)
        h4T = carve(GTOK)
        ffs = carve(EC * GTOK).rearrange("p (c r) -> p c r", c=EC)
        oF = carve(GTOK)
        ht3 = [carve(GTOK) for _ in range(2)]
        r_res = carve(TILES * D)

        parts = sb("parts", [P, 2 * XR * GTOK], F32R)
        w1h, w1l = ([parts[:, (2 * c + u) * W:(2 * c + u + 1) * W] for u in range(2)] for c in range(2))
        h2h, h2l = ([parts[:, 4 * W + (2 * c + u) * EROWS:4 * W + (2 * c + u + 1) * EROWS] for u in range(2)] for c in range(2))
        xhi, xlo = ([parts[:, (2 * u + c) * GTOK:(2 * u + c + 1) * GTOK] for u in range(XR)] for c in range(2))
        wparts = sb("wparts", [P, 2 * XS * D], F32R)
        wph, wpl = (wparts[:, c * XS * D:(c + 1) * XS * D].rearrange("p (x h) -> p x h", x=XS) for c in range(2))
        h4h, h4l, hth, htl = (parts[:, i * GTOK:(i + 1) * GTOK] for i in range(4))
        fw1h, fw1l = (wparts[:, i * DH:(i + 1) * DH] for i in range(2))
        sw1h, sw1l = (wparts[:, 2 * DH + i * DS:2 * DH + (i + 1) * DS] for i in range(2))

        def tm(name):
            return sb(name, [P, GT, D])

        h = [tm(f"h{u}") for u in range(2)]
        xh = tm("xh")
        vp = tm("vp")
        fm = sb("fm", [P, 5 * GTOK])
        xT, aT, cT, th, hF = (fm[:, i * GTOK:(i + 1) * GTOK] for i in range(5))
        xs = sb("xs", [P, GIMG, SEQ])
        past = fm[:, 0:TILES * TOPK * E].rearrange("p (s e) -> p s e", e=E)
        s_t = sb("s_t", [P, GT, SEQ])
        e_t = sb("e_t", [P, GT, SEQ])
        a_bd = tm("a_bd")
        h2 = tm("h2")
        z = [tm(f"z{u}") for u in range(2)]
        rr = [tm(f"rr{u}") for u in range(2)]
        hT = [sb(f"hT{u}", [P, GTOK]) for u in range(2)]
        st = sb("st", [P, GT, 6])
        mv = sb("mv", [P, GT, 2])
        var1 = sb("var1", [P, GT])
        rstd1 = sb("rstd1", [P, GT])
        var2 = sb("var2", [P, 2 * GT])
        rstd2 = sb("rstd2", [P, 2 * GT])
        rs1 = sb("rs1", [P, GT])
        rs2 = sb("rs2", [P, GT])
        mx = sb("mx", [P, GT])
        sm = sb("sm", [P, GT])
        rsm = sb("rsm", [P, GT])
        st2 = sb("st2", [P, GT, 6])
        mv2 = sb("mv2", [P, GT, 2])
        gsm = sb("gsm", [P, GT])
        rgsm = sb("rgsm", [P, GT])
        lg = sb("lg", [P, GT, E])
        m8 = sb("m8", [P, GT, 8])
        i8 = sb("i8", [P, GT, 8], U32)
        i2 = sb("i2", [P, GT * TOPK])
        d18 = sb("d18", [P, GT, E + TOPK])
        oh = sb("oh", [P, GT * TOPK, E])
        m2 = sb("m2", [P, GT, E], BF16)
        pp = sb("pp", [P, GT, TOPK, E])
        posf = sb("posf", [P, GT * TOPK])
        posg = [sb(f"posg{u}", [P, GT * TOPK], U32) for u in range(2)]
        gidx = [sb(f"gidx{u}", [P, GT * TOPK], U32) for u in range(2)]
        cnt = sb("cnt", [P, E])
        cnti = sb("cnti", [P, E], I32)
        nt = sb("nt", [P, E])
        nti = sb("nti", [P, E], I32)
        dsh = sb("dsh", [P, E])
        one_e = sb("one_e", [P, E])
        cum = sb("cum", [P, E])
        cmp = sb("cmp", [P, E])
        ejt = sb("ejt", [P, 2])
        tj = sb("tj", [P, 1])
        ejc = sb("ejc", [1, EXPERT_TILES], I32)
        rowj = sb("rowj", [1, EXPERT_TILES], I32)
        tail = sb("tail", [1, E], I32)
        zeros = sb("zeros", [P, EH * D])
        zsrc = zeros[:, :].rearrange("p (h d) -> p h d", h=EH)

        bank = [ctx.enter_context(nc.psum_tensor(f"bank{i}", [P, 512], F32)) for i in range(8)]

        def tiles_of(b, w=D):
            return bank[b][:, 0:GT * w].rearrange("p (t d) -> p t d", t=GT)

        pa = bank[0]
        t1, t2, s_ps, t3 = tiles_of(2), bank[3], tiles_of(4), bank[5]
        c_ps, w_ps, t4, t5 = bank[2], bank[3], tiles_of(4), bank[5]
        l_ps = bank[6][:, 0:GT * E].rearrange("p (t e) -> p t e", t=GT)
        p_ps = bank[7][:, 0:(GT + 1) * E].rearrange("p (t e) -> p t e", t=GT + 1)

        x_zeroed, x_zeroed_act, wp_zeroed = sem("x_zeroed"), sem("x_zeroed_act"), sem("wp_zeroed") 
        ld_id, ld_const, ld_w = sem("ld_id"), sem("ld_const"), sem("ld_w")
        memset_done, dve_setup = sem("memset_done"), sem("dve_setup")
        cls_var, cls_rstd, xcls_ready = sem("cls_var"), sem("cls_rstd"), sem("xcls_ready")
        setup_t, wp_t = sem("setup_t"), sem("wp_t")
        cols_ready, xclsT_ready, wp_ready = sem("cols_ready"), sem("xclsT_ready"), sem("wp_ready")
        xhi_ready, xlo_ready, xparts_used = sem("xhi_ready"), sem("xlo_ready"), sem("xparts_used")
        wph_ready, wpl_ready = sem("wph_ready"), sem("wpl_ready")
        x_loaded = [sem(f"x_loaded{u}") for u in range(2)]
        patch_done, hF_ready, t1_done, h_ready = sem("patch_done"), sem("hF_ready"), sem("t1_done"), sem("h_ready")
        var1_ready, rstd1_ready, xh_ready, vp_ready = sem("var1_ready"), sem("rstd1_ready"), sem("xh_ready"), sem("vp_ready")
        t2_done, xT_ready, s_done, smax_ready = sem("t2_done"), sem("xT_ready"), sem("s_done"), sem("smax_ready")
        e_ready, a_ready, t3_done, aT_ready = sem("e_ready"), sem("a_ready"), sem("t3_done"), sem("aT_ready")
        c_done, cT_ready, w_done, th_ready = sem("c_done"), sem("cT_ready"), sem("w_done"), sem("th_ready")
        t4_done, var2_ready, rstd2_ready, z_ready = sem("t4_done"), sem("var2_ready"), sem("rstd2_ready"), sem("z_ready")
        r_ready, t5_done, hT_ready, l_done = sem("r_ready"), sem("t5_done"), sem("hT_ready"), sem("l_done")
        rs_ready = sem("rs_ready")
        gate_ready, gexp_ready, m2_ready, p_done, pos_ready = (
            sem("gate_ready"), sem("gexp_ready"), sem("m2_ready"), sem("p_done"), sem("pos_ready"))
        dve_step = sem("dve_step")
        r_free = [sem(f"r_free{u}") for u in range(2)]
        hT_free = [sem(f"hT_free{u}") for u in range(2)]
        z_free = [sem(f"z_free{u}") for u in range(2)]
        tab_step, tab_ready, spare_zeroed, tails_zeroed = sem("tab_step"), sem("tab_ready"), sem("spare_zeroed"), sem("tails_zeroed")
        tail_ready, past_ready, shift_ready, ejt_ready, tej_done = (
            sem("tail_ready"), sem("past_ready"), sem("shift_ready"), sem("ejt_ready"), sem("tej_done"))
        w1_loaded = [sem(f"w1_loaded{u}") for u in range(4)]
        w2_loaded = [sem(f"w2_loaded{u}") for u in range(4)]
        zin_loaded = [sem(f"zin_loaded{u}") for u in range(4)]
        tin_done, h2T_ready, up_done, eh_ready = sem("tin_done"), sem("h2T_ready"), sem("up_done"), sem("eh_ready")
        w1h_ready, w1l_ready, h2h_ready, h2l_ready = sem("w1h_ready"), sem("w1l_ready"), sem("h2h_ready"), sem("h2l_ready")
        down_done, eyT_ready, tout_done, yout_ready = sem("down_done"), sem("eyT_ready"), sem("tout_done"), sem("yout_ready")
        y_free = [sem(f"y_free{u}") for u in range(2)]
        w3_loaded, r_loaded = sem("w3_loaded"), sem("r_loaded")
        ht_loaded = [sem(f"ht_loaded{u}") for u in range(2)]
        idx_ready, sb2q_ready = sem("idx_ready"), sem("sb2q_ready")
        gathered = [[sem(f"gathered{s}{u}") for u in range(2)] for s in range(TOPK)]
        fw_parts, h4l_ready, mix0_done = sem("fw_parts"), sem("h4l_ready"), sem("mix0_done")
        hth_ready, htl_ready = sem("hth_ready"), sem("htl_ready")
        u_done, u_used = sem("u_done"), sem("u_used")
        shd_done, shF_ready, tsh_done, mix_done = sem("shd_done"), sem("shF_ready"), sem("tsh_done"), sem("mix_done")
        var4_ready, rstd4_ready, z4_ready, tz_done, h4T_ready = (
            sem("var4_ready"), sem("rstd4_ready"), sem("z4_ready"), sem("tz_done"), sem("h4T_ready"))
        ffd_done, oF_ready, tout3_done, out_ready, out_stored = (
            sem("ffd_done"), sem("oF_ready"), sem("tout3_done"), sem("out_ready"), sem("out_stored"))
        wait_carried = sem("wait_carried")
        dve_step3 = sem("dve_step3")
        A_STEPS, R_STEPS = 7, 16
        FF_BANK = (0, 5, 1, 2)
        DVE_STEPS, DVE_STEPS3 = A_STEPS + R_STEPS, 3

        def bc(ap, shape):
            return ap.to_broadcast(shape)

        def groups(eng, first, last, body):
            assert (last - first) % 2 == 0
            with eng.Fori(0, (last - first) // 2) as i:
                for j in range(first, first + 2):
                    body(i * 2 + j, j % 2, i + j // 2)

        def one(body, g):
            body(g, g % 2, g // 2)

        def plain(eng):
            eng.sem_inc(wait_carried, 1)

        def col(n):
            return cols[:, n:n + 1]

        def pixels(k, px):
            return xb[k].rearrange("p (t x) -> p t x", x=PATCH)[:, :, px]

        def zero_tails(eng, first):
            eng.wait_ge(tail_ready, 1)
            with eng.Fori(0, E // 8) as e:
                rows = [eng.value_load(tail[0:1, bass.ds(e * 4 + (first + n), 1)], min_val=0, max_val=ZROWS - EROWS)
                        for n in range(4)]
                for row in rows:
                    eng.dma_start(z_rows[bass.ds(row, EROWS)].rearrange("(h p) d -> p h d", p=P), zsrc)\
                       .then_inc(tails_zeroed, 16)

        block = ctx.enter_context(nc.Block())

        @block.sync
        def _(sp):
            loads = [(vecs[V_EB1:V_EB2], eb1.rearrange("e (c p) -> (e c) p", p=P)),
                     (vecs[V_EB2:V_SB1], eb2), (vecs[V_SB1:V_SB2], sb1.rearrange("(c p) -> c p", p=P)),
                     (vecs[V_SB2:V_FB1], sb2.unsqueeze(0)), (vecs[V_FB1:V_FB2], fb1.rearrange("(c p) -> c p", p=P)),
                     (vecs[V_FB2:V_LG], fb2.unsqueeze(0)), (vecs[V_LG:V_LB], ln_g.unsqueeze(0)),
                     (vecs[V_LB:V_FG], ln_b.unsqueeze(0)), (vecs[V_FG:V_FB], f_g.unsqueeze(0)),
                     (vecs[V_FB:V_TB], f_b.unsqueeze(0)), (vecs[V_TB:V_END], tok_b.unsqueeze(0)),
                     (pos_t[0:SEQ], pos[1:SEQ + 1]), (pos_t[SEQ:P], pos[1:SEQ + 1]),
                     (hcls[:, :], cls_tok[0].partition_broadcast(P)), (pos0[:, :], pos[0].partition_broadcast(P)),
                     (wc[:, :, :], w_c.rearrange("(k f) o -> f k o", k=2)), (rw[:, :], r_w),
                     (rb[:, :], r_b.partition_broadcast(P))]
            assert len(loads) == N_LOADS

            def load_x(g, k, h):
                dst = xb[k].rearrange("p (b n w) -> p b n w", b=GIMG, n=NP)
                for c in range(CH):
                    if isinstance(g, int) and g < 2 and c == CH - 1:
                        sp.wait_ge(x_zeroed, g + 1)
                        sp.wait_ge(x_zeroed_act, 1)
                    for b in range(GIMG):
                        src = x[bass.ds(g * GIMG + b, 1), c].rearrange("o (n y) w -> y (o n) w", y=PATCH)
                        sp.dma_start(dst[c * PATCH:(c + 1) * PATCH, b], src).then_inc(x_loaded[k], 16)

            def reload_x(g, k, h):
                sp.wait_ge(patch_done, g - 1)
                load_x(g, k, h)

            def stores(r, k, h, nt=GT):
                tile = r * GT - GT if nt == GT else PATCH_TILES
                sp.wait_ge(hT_ready, r + 1)
                sp.dma_start(ht_dram[:, bass.ds(tile, nt)],
                             hT[k][:, 0:nt * P].rearrange("p (t c) -> p t c", t=nt)).then_inc(hT_free[k], 16)
                sp.wait_ge(r_ready, r + 1)
                sp.dma_start(r_dram[:, bass.ds(tile, nt)], rr[k][:, 0:nt]).then_inc(r_free[k], 16)

            sp.dma_start(cst[:, :], consts).then_inc(ld_id, 16)
            sp.dma_start(wnat, tok_w.rearrange("h (c y x) -> h c y x", c=CH, y=PATCH)).then_inc(ld_w, 16)
            load_x(0, 0, 0)
            for dst, src in loads:
                sp.dma_start(dst, src).then_inc(ld_const, 16)
            sp.wait_ge(wp_t, PATCH // 4)
            load_x(1, 1, 0)
            for k in range(2):
                sp.sem_inc(r_free[k], 16)
                sp.sem_inc(hT_free[k], 16)
            sp.wait_ge(memset_done, 2)
            for s in range(2, SPARE_TILES):
                at = E * CAP + s * EROWS
                sp.dma_start(z_rows[at:at + EROWS].rearrange("(h p) d -> p h d", p=P), zsrc).then_inc(spare_zeroed, 16)

            def step(g, k, h):
                reload_x(g + 2, k, h + 1)
                stores(g, k, h)

            reload_x(2, 0, 1)
            stores(0, 0, 0, 1)
            groups(sp, 1, GROUPS - 3, step)
            one(step, GROUPS - 3)
            one(stores, GROUPS - 2)
            one(stores, GROUPS - 1)

            one(stores, GROUPS)
            zero_tails(sp, 0)

            def expert_weights(j, n):
                ex = sp.value_load(ejc[0:1, bass.ds(j, 1)], min_val=0, max_val=E - 1)
                sp.wait_ge(w1l_ready, j - 3) if n >= 4 else None
                sp.dma_start(w1b[n % 4], ew1[bass.ds(ex, 1)].rearrange("o d h -> d (o h)")).then_inc(w1_loaded[n % 4], 16)
                sp.wait_ge(down_done, j - 3) if n >= 4 else None
                sp.dma_start(w2b[n % 4], ew2[bass.ds(ex, 1)].rearrange("o (c p) d -> p (o c) d", p=P))\
                  .then_inc(w2_loaded[n % 4], 16)

            def first_row(j):
                return sp.value_load(rowj[0:1, bass.ds(j, 1)], min_val=0, max_val=ZROWS - EROWS)

            def expert_rows(j, n, row=None):
                row = first_row(j) if row is None else row
                sp.wait_ge(tin_done, j - 3) if n >= 4 else None
                sp.dma_start(zin[n % 4], z_rows[bass.ds(row, EROWS)].rearrange("(h p) d -> p h d", p=P))\
                  .then_inc(zin_loaded[n % 4], 16)

            def expert_loads(j, n):
                expert_rows(j, n)
                expert_weights(j, n)

            sp.wait_ge(patch_done, GROUPS)
            sp.wait_ge(tab_ready, 1)
            expert_weights(0, 0)
            rows = [first_row(j) for j in range(4)]
            sp.wait_ge(tails_zeroed, 16 * E)
            sp.wait_ge(z_free[0], 16 + 16 * TOPK + 16 * TOPK * GT * GROUPS // 2)
            sp.wait_ge(z_free[1], 16 + 16 * TOPK * GT * GROUPS // 2)
            sp.wait_ge(spare_zeroed, 16 * (SPARE_TILES - 2))
            expert_rows(0, 0, rows[0])
            for j in range(1, 4):
                expert_rows(j, j, rows[j])
                expert_weights(j, j)
            for k in range(2):
                sp.wait_ge(r_free[k], 16 + 16 * (GROUPS // 2 + 1 - k))
                sp.wait_ge(hT_free[k], 16 + 16 * (GROUPS // 2 + 1 - k))
            for dst, src in ((sw1_t, sw1), (sw2_t, sw2.rearrange("(c p) d -> p c d", p=P)), (fw1_t, fw1),
                             (fw2_t, fw2.rearrange("(c p) d -> p c d", p=P))):
                sp.dma_start(dst, src).then_inc(w3_loaded, 16)
            for q in range(2):
                sp.dma_start(ht3[q], ht_dram[:, q * GT:(q + 1) * GT].rearrange("p t c -> p (t c)")).then_inc(ht_loaded[q], 16)
            with sp.Fori(1, 1 + GROUPS) as i:
                for n in range(4):
                    expert_loads(i * 4 + n, 4 + n)
                sp.dma_start(r_res[:, bass.ds(i * GTOK - GTOK, GTOK)].rearrange("p (t d) -> p t d", t=GT),
                             r_dram[:, bass.ds(i * GT - GT, GT)]).then_inc(r_loaded, 16)
            sp.dma_start(r_res[:, PATCH_TILES * D:], r_dram[:, PATCH_TILES]).then_inc(r_loaded, 16)
            with sp.Fori(1 + GROUPS, EXPERT_TILES // 4) as i:
                for n in range(4):
                    expert_loads(i * 4 + n, 4 + n)

            def load_ht(q, k, n, nt=GT):
                sp.wait_ge(u_done, n)
                sp.dma_start(ht3[k][:, 0:nt * P].rearrange("p (t c) -> p t c", t=nt),
                             ht_dram[:, bass.ds(q * GT, nt)]).then_inc(ht_loaded[k], 16)

            def store_out(q, nt=GT):
                sp.wait_ge(out_ready, q + 2)
                res = r_res.rearrange("p (t d) -> p t d", d=D)
                for t in range(nt):
                    if nt == GT:
                        dst = out[bass.ds(q * GIMG + 2 * t, 2), 1:SEQ + 1]
                    else:
                        dst = out[:, 0]
                    sp.dma_start(dst, res[:, bass.ds(q * GT + t, 1)].rearrange("p o d -> p (o d)"))\
                      .then_inc(out_stored, 16)

            def step3(q, k, h):
                store_out(q)
                load_ht(q + 5, (k + 5) % 2, q * 6 + 12)

            for q in range(2, 5):
                load_ht(q, q % 2, SC * (q - 1))
            groups(sp, 0, GROUPS - 6, step3)
            one(step3, GROUPS - 6)
            store_out(GROUPS - 5)
            load_ht(GROUPS, 0, (GROUPS - 5) * 6 + 12, 1)
            for q in range(GROUPS - 4, GROUPS):
                store_out(q)
            store_out(GROUPS, 1)
            sp.wait_ge(out_stored, 16 * TILES)

        @block.scalar
        def _(act):
            act.wait_ge(memset_done, 2)
            act.activation(xb[0][64:P, XZ:], zeros[64:P, 0:1].to_broadcast([P - 64, XCOLS - XZ]), ACT.Copy)\
               .then_inc(x_zeroed_act, 1)
            act.wait_ge(wp_zeroed, 2)
            for b in range(PATCH // 4):
                act.wait_ge(wp_t, b + 1)
                act.activation(wp[0:KROWS, 4 * b:4 * b + 4].rearrange("p x h -> p (x h)"), bank[b][0:KROWS, :], ACT.Copy)\
                   .then_inc(wp_ready, 1)
                if 4 * b < XS:
                    n = min(4, XS - 4 * b)
                    act.activation(wph[0:KROWS, 4 * b:4 * b + n].rearrange("p x h -> p (x h)"), bank[b][0:KROWS, 0:n * P],
                                   ACT.Copy).then_inc(wph_ready, 1)
            act.wait_ge(setup_t, 1)
            act.activation(cols[:, :], bank[7][:, 0:V_END], ACT.Copy).then_inc(cols_ready, 1)
            act.wait_ge(setup_t, 2)
            act.activation(xclsT[:, :], bank[7][:, P:2 * P], ACT.Copy).then_inc(xclsT_ready, 1)
            act.activation(xs[:, :, SEQ - 1], bank[7][:, P:P + GIMG], ACT.Copy)
            act.wait_ge(cols_ready, 1)

            def x_high(g, k, h, lo):
                act.wait_ge(x_loaded[k], h * (16 * XLOADS) + 16 * XLOADS)
                for px in range(lo, lo + XR):
                    n = (g - 1) * XS + px
                    if not (isinstance(n, int) and n < XR):
                        act.wait_ge(xparts_used, n + (1 - XR))
                    act.activation(xhi[px % XR], pixels(k, px), ACT.Copy).then_inc(xhi_ready, 1)

            def take_patch(g):
                act.wait_ge(patch_done, g + 1)
                act.activation(hF[:, :], pa[:, :], ACT.Identity, bias=col(V_TB)).then_inc(hF_ready, 1)

            def take_x(g):
                act.wait_ge(t2_done, g + 1)
                act.activation(xT, t2[:, :], ACT.Copy)
                act.activation(xs[:, :, 0:SEQ - 1], t2[:, :].rearrange("p (i s) -> p i s", s=SEQ)[:, :, 0:SEQ - 1],
                               ACT.Copy).then_inc(xT_ready, 1)

            def route_a(g, k, h, nt=GT):
                act.wait_ge(hT_free[k], h * 16 + 16)
                act.wait_ge(t5_done, g + 1)
                act.activation(hT[k][:, 0:nt * P], t5[:, 0:nt * P], ACT.Identity, scale=col(V_LG), bias=col(V_LB))\
                   .then_inc(hT_ready, 1)
                act.wait_ge(r_free[k], h * 16 + 16)
                act.wait_ge(rs_ready, g + 1)
                for t in range(nt):
                    ins = act.activation(rr[k][:, t], h2[:, t], ACT.Identity, scale=rs1[:, t:t + 1], bias=rs2[:, t:t + 1])
                ins.then_inc(r_ready, 1)

            def take_s(g):
                act.wait_ge(smax_ready, g + 1)
                act.activation(e_t[:, :, :], s_t[:, :, :], ACT.Exp).then_inc(e_ready, 1)

            def route_b(g, nt=GT):
                act.wait_ge(gate_ready, g + 1)
                act.activation(d18[:, 0:nt], d18[:, 0:nt], ACT.Exp, scale=1.0 / TEMP).then_inc(gexp_ready, 1)

            def take_a(g):
                act.wait_ge(t3_done, g + 1)
                act.activation(aT[:, :], t3[:, :], ACT.Copy).then_inc(aT_ready, 1)

            def take_c(g):
                act.wait_ge(c_done, g + 1)
                act.activation(cT[:, :], c_ps[:, :], ACT.Copy).then_inc(cT_ready, 1)

            def take_w(g, nt=GT):
                act.wait_ge(w_done, g + 1)
                act.activation(th[:, 0:nt * P], w_ps[:, 0:nt * P], ACT.Tanh, scale=0.5).then_inc(th_ready, 1)

            def body(g, k, h, ahead=2, nt=GT):
                if ahead:
                    x_high(g + 1, 1 - k, h + k, XR)
                take_x(g)
                route_a(g, k, h, nt)
                take_s(g)
                route_b(g, nt)
                if ahead > 1:
                    x_high(g + 2, k, h + 1, 0)
                take_a(g)
                if ahead:
                    take_patch(g + 1)
                take_c(g)
                take_w(g + 1)

            take_w(0, 1)
            take_patch(0)
            x_high(1, 1, 0, 0)
            body(0, 0, 0, nt=1)
            groups(act, 1, GROUPS - 3, body)
            one(body, GROUPS - 3)
            body(GROUPS - 2, 0, GROUPS // 2 - 1, ahead=1)
            body(GROUPS - 1, 1, GROUPS // 2 - 1, ahead=0)
            one(route_a, GROUPS)
            route_b(GROUPS)
            zero_tails(act, E // 2)

            def take_in(j, n):
                act.wait_ge(h2l_ready, j - 1) if n > 1 else None
                act.wait_ge(tin_done, j + 1)
                act.activation(h2T[n % 2], bank[0][:, 0:EROWS], ACT.Identity, scale=col(V_LG), bias=col(V_LB))\
                   .then_inc(h2T_ready, 1)

            def silus(j, n, ahead=True):
                ex = act.value_load(ejc[0:1, bass.ds(j, 1)], min_val=0, max_val=E - 1)
                bias = [cols[:, bass.ds(ex * EC + c, 1)] for c in range(EC)]
                for c in range(EC):
                    if c == 2 and ahead:
                        take_in(j + 1, n + 1)
                    act.wait_ge(up_done, j * EC + c + 1)
                    act.activation(ehT[n % 2][:, c], bank[1 + c][:, 0:EROWS], ACT.Silu, bias=bias[c])\
                       .then_inc(eh_ready, 1)

            act.wait_ge(tab_ready, 1)
            act.wait_ge(memset_done, 2)
            act.activation(spare[:, :], neghalf[:, 0:1], ACT.Silu)
            take_in(0, 0)
            for j in range(4):
                silus(j, j)
            with act.Fori(1, EXPERT_TILES // 4 - 1) as i:
                act.activation(spare[:, :], neghalf[:, 0:1], ACT.Silu)
                for n in range(4):
                    silus(i * 4 + n, 4 + n)
            for j in range(EXPERT_TILES - 4, EXPERT_TILES):
                silus(j, j, ahead=j + 1 < EXPERT_TILES)

            def silu3(n, b, dst, bias, w):
                act.wait_ge(u_done, n + 1)
                act.activation(dst[:, 0:w], bank[b][:, 0:w], ACT.Silu, bias=bias).then_inc(u_used, 1)

            def sh_silu(q, n, nt=GT):
                for c in range(SC):
                    silu3(n + c, (4 + c) % 3, shs[:, c], col(V_SB1 + c), nt * P)

            def sh_out(q, nt=GT):
                act.wait_ge(shd_done, q + 1)
                act.activation(shF[:, 0:nt * P], bank[3][:, 0:nt * P], ACT.Identity, scale=SHARED, bias=sb2q[:, 0:1])\
                   .then_inc(shF_ready, 1)

            def z_in(q, nt=GT):
                act.wait_ge(tz_done, q + 1)
                act.activation(h4T[:, 0:nt * P], bank[5][:, 0:nt * P], ACT.Identity, scale=col(V_FG), bias=col(V_FB))
                act.activation(h4h[:, 0:nt * P], bank[5][:, 0:nt * P], ACT.Identity, scale=col(V_FG), bias=col(V_FB))\
                   .then_inc(h4T_ready, 1)

            def ff_silu(q, n, nt=GT):
                for c in range(EC):
                    silu3(n + c, FF_BANK[c], ffs[:, c], col(V_FB1 + c), nt * P)

            def ff_out(q, nt=GT):
                act.wait_ge(ffd_done, q + 1)
                act.activation(oF[:, 0:nt * P], bank[4][:, 0:nt * P], ACT.Identity, bias=col(V_FB2)).then_inc(oF_ready, 1)

            def ht_high(q, k, h, nt=GT):
                act.wait_ge(ht_loaded[k], h * 16 + 16)
                act.activation(hth[:, 0:nt * P], ht3[k][:, 0:nt * P], ACT.Copy).then_inc(hth_ready, 1)

            act.wait_ge(sb2q_ready, 1)
            for q in range(3):
                ht_high(q, q % 2, q // 2)
                sh_silu(q, 2 * q)
                if q < 2:
                    sh_out(q)
            z_in(0)

            def step3(q, k, h, sh3=GT, sh2=GT, z1=GT, now=GT, n=None):
                n = q * 6 + 6 if n is None else n
                if sh3:
                    ht_high(q + 3, 1 - k, h + (k + 3) // 2, sh3)
                ff_silu(q, n, now)
                if sh2:
                    sh_out(q + 2, sh2)
                if z1:
                    z_in(q + 1, z1)
                ff_out(q, now)
                if sh3:
                    sh_silu(q + 3, n + 4, sh3)

            groups(act, 0, GROUPS - 4, step3)
            one(step3, GROUPS - 4)
            step3(GROUPS - 3, 1, GROUPS // 2 - 2, sh3=1)
            last = (GROUPS - 3) * 6 + 12
            step3(GROUPS - 2, 0, GROUPS // 2 - 1, sh3=0, sh2=1, n=last)
            step3(GROUPS - 1, 1, GROUPS // 2 - 1, sh3=0, sh2=0, z1=1, n=last + EC)
            step3(GROUPS, 0, GROUPS // 2, sh3=0, sh2=0, z1=0, now=1, n=last + 2 * EC)

        @block.gpsimd
        def _(pool):
            pool.memset(neghalf[:, :], -0.5).then_inc(memset_done, 1)
            def rstd(var_ready, n, dst, var, ready):
                pool.wait_ge(var_ready, n)
                pool.tensor_tensor(dst, var, neghalf[:, 0:var.shape[1]], ALU.pow).then_inc(ready, 1)

            pool.wait_ge(memset_done, 2)
            for u in range(2):
                at = E * CAP + u * EROWS
                pool.dma_start(z_rows[at:at + EROWS].rearrange("(h p) d -> p h d", p=P), zsrc).then_inc(z_free[u], 16)
            rstd(cls_var, 1, rstd1[:, 0:1], var1[:, 0:1], cls_rstd)

            def scatter(r, k, nt=GT):
                pool.wait_ge(z_ready, r + 1)
                pool.wait_ge(pos_ready, r + 1)
                plain(pool)
                for t in range(nt):
                    for s in range(TOPK):
                        n = t * TOPK + s
                        pool.indirect_dma_start(z_rows, bass.IndirectOffsetOnAxis(posg[k][:, n:n + 1], 0),
                                                z[k][:, t], None).then_inc(z_free[k], 16)

            def norms(g):
                rstd(var1_ready, g + 1, rstd1[:, :], var1[:, :], rstd1_ready)
                rstd(var2_ready, g + 1, rstd2[:, :], var2[:, :], rstd2_ready)

            def step(g, k, h):
                norms(g)
                scatter(g - 1, 1 - k)

            norms(0)
            norms(1)
            scatter(0, 0, 1)
            groups(pool, 2, GROUPS, step)
            rstd(var2_ready, GROUPS + 1, rstd2[:, :], var2[:, :], rstd2_ready)
            scatter(GROUPS - 1, 1)
            scatter(GROUPS, 0)

            pool.wait_ge(past_ready, 1)
            pool.tensor_tensor(past, past, bc(dsh[:, :].unsqueeze(1), [P, TILES * TOPK, E]), ALU.mult)\
                .then_inc(shift_ready, 1)


            def store_y(j, n):
                pool.wait_ge(yout_ready, j + 1)
                plain(pool)
                pool.dma_start(y_rows[bass.ds(j * EROWS, EROWS)].rearrange("(h p) d -> p h d", p=P), yout[n % 2])\
                    .then_inc(y_free[n % 2], 16)

            store_y(0, 0)
            store_y(1, 1)
            with pool.Fori(1, EXPERT_TILES // 2) as i:
                for n in range(2):
                    store_y(i * 2 + n, n)
            for k in range(2):
                pool.wait_ge(y_free[k], 16 * (EXPERT_TILES // 2))

            def gather(q, k, s, nt=GT):
                if s == 0:
                    pool.wait_ge(idx_ready, q + 1)
                if not (isinstance(q, int) and q < 2):
                    pool.wait_ge((mix0_done, mix_done)[s], q - 1)
                plain(pool)
                for t in range(nt):
                    n = t * TOPK + s
                    pool.indirect_dma_start(gat[k][:, t, s], None, y_rows,
                                            bass.IndirectOffsetOnAxis(gidx[k][:, n:n + 1], 0)).then_inc(gathered[s][k], 16)

            def norms3(q):
                rstd(var4_ready, q + 1, rstd1[:, :], var1[:, :], rstd4_ready)

            def step3(q, k, h, b=GT, a=GT):
                if b:
                    gather(q + 2, k, 1, b)
                norms3(q + 1)
                if a:
                    gather(q + 3, 1 - k, 0, a)

            gather(0, 0, 0)
            gather(0, 0, 1)
            gather(1, 1, 0)
            norms3(0)
            gather(1, 1, 1)
            gather(2, 0, 0)
            step3(0, 0, 0)
            groups(pool, 1, GROUPS - 3, step3)
            step3(GROUPS - 3, 1, GROUPS // 2 - 2, a=1)
            step3(GROUPS - 2, 0, GROUPS // 2 - 1, b=1, a=0)
            step3(GROUPS - 1, 1, GROUPS // 2 - 1, b=0, a=0)

        @block.vector
        def _(dve):
            dve.memset(ones[:, :], 1.0)
            dve.memset(a_bd[:, :, :], 0.0)
            dve.memset(zeros[:, :], 0.0)
            dve.memset(one_e[:, :], 1.0)
            for buf in (var1, var2):
                dve.memset(buf[:, :], 1.0)
            dve.memset(rstd2[:, :], 1.0).then_inc(memset_done, 1)
            dve.memset(xb[0][64:P, 0:XZ], 0.0).then_inc(x_zeroed, 1)
            dve.memset(wp[64:P, :, :], 0.0).then_inc(wp_zeroed, 1)
            dve.wait_ge(wp_zeroed, 1)
            dve.tensor_copy(wph[64:P, :, :], wp[64:P, 0:XS]).then_inc(wp_zeroed, 1)
            dve.wait_ge(wp_t, PATCH // 4)
            dve.memset(xb[1][64:P], 0.0).then_inc(x_zeroed, 1)
            dve.wait_ge(wph_ready, -(-XS // 4))
            dve.wait_ge(wp_ready, PATCH // 4)
            dve.tensor_tensor(wpl, wp[:, 0:XS], wph, ALU.subtract).then_inc(wpl_ready, 1)
            dve.wait_ge(ld_id, 16)
            dve.wait_ge(ld_const, 16 * N_LOADS)
            n = [0]

            def link(ins):
                n[0] += 1
                ins.then_inc(dve_setup, 1)

            def settle():
                dve.wait_ge(dve_setup, n[0])

            link(dve.tensor_copy(pref[:, :], cst[:, C_PREF:C_PREF + P]))
            link(dve.tensor_copy(base[:, :], cst[:, C_BASE:C_BASE + E]))
            link(dve.tensor_tensor(hcls[:, :], hcls[:, :], pos0[:, :], ALU.mult))
            settle()
            link(dve.bn_stats(st[:, 0], hcls[:, :]))
            settle()
            link(dve.bn_aggr(mv[:, 0], st[:, 0]))
            settle()
            dve.tensor_scalar(var1[:, 0:1], mv[:, 0, 1:2], EPS, None, ALU.add).then_inc(cls_var, 1)
            dve.wait_ge(cls_rstd, 1)
            dve.tensor_scalar(xcls[:, :], hcls[:, :], mv[:, 0, 0:1], rstd1[:, 0:1], ALU.subtract, ALU.mult)\
               .then_inc(xcls_ready, 1)
            dve.wait_ge(xcls_ready, 1)
            link(dve.tensor_scalar(vcls[:, :], xcls[:, :], cst[:, C_CLS:C_CLS + 1], None, ALU.mult))
            dve.wait_ge(cols_ready, 1)
            dve.tensor_scalar(sb2q[:, :], col(V_SB2), SHARED, None, ALU.mult).then_inc(sb2q_ready, 1)
            settle()

            def stats(src, nt, st, mv, link, settle):
                for t in range(nt):
                    ins = dve.bn_stats(st[:, t], src(t))
                settle(link(ins))
                plain(dve)
                for t in range(nt):
                    ins = dve.bn_aggr(mv[:, t], st[:, t])
                settle(link(ins))

            def normalise(dst, src, mv, scale, nt):
                for t in range(nt):
                    ins = dve.tensor_scalar(dst[:, t], src[:, t], mv[:, t, 0:1], scale[:, t:t + 1],
                                            ALU.subtract, ALU.mult)
                return ins

            mask3 = bc(mask.unsqueeze(1), [P, GT, SEQ])

            def attend_norm(g, k, link, settle):
                dve.wait_ge(h_ready, g + 1)
                stats(lambda t: h[k][:, t], GT, st, mv, link, settle)
                dve.tensor_scalar(var1[:, :], mv[:, :, 1], EPS, None, ALU.add).then_inc(var1_ready, 1)

            def x_low(g, k, lo):
                for px in range(lo, lo + XR):
                    dve.wait_ge(xhi_ready, (g - 1) * XS + (px + 1))
                    dve.tensor_tensor(xlo[px % XR], pixels(k, px), xhi[px % XR], ALU.subtract).then_inc(xlo_ready, 1)

            def body(r, k, h_, nt=GT, attn=True, ahead=2):
                m = [0]
                nk = nt * TOPK
                slot = r * nk - nk if nt == GT else PATCH_TILES * TOPK

                def link(ins):
                    m[0] += 1
                    ins.then_inc(dve_step, 1)
                    return m[0]

                def settle(n):
                    dve.wait_ge(dve_step, r * DVE_STEPS + n)

                if attn:
                    dve.wait_ge(t1_done, r + 1)
                    dve.tensor_tensor(h[k][:, :, :], t1, bc(pos_t[:, :].unsqueeze(1), [P, GT, D]), ALU.mult)\
                       .then_inc(h_ready, 1)
                dve.wait_ge(t4_done, r + 1)
                if not (isinstance(r, int) and r == 0):
                    dve.wait_ge(r_ready, r)
                src = h[1 - k][:, 0:nt] if nt == GT else hcls[:, :].unsqueeze(1)
                h2_step = link(dve.scalar_tensor_tensor(out=h2[:, 0:nt], in0=t4[:, 0:nt], scalar=0.5, in1=src,
                                                        op0=ALU.mult, op1=ALU.add))
                if attn:
                    attend_norm(r, k, link, settle)
                settle(h2_step)
                stats(lambda t: h2[:, t], nt, st2, mv2, link, settle)
                dve.tensor_scalar(var2[:, 0:nt], mv2[:, 0:nt, 1], EPS, None, ALU.add)
                dve.tensor_scalar(var2[:, GT:GT + nt], mv2[:, 0:nt, 1], 1.0 + EPS, EPS * EPS, ALU.mult, ALU.add)\
                   .then_inc(var2_ready, 1)
                if attn:
                    dve.wait_ge(rstd1_ready, r + 1)
                    normalise(xh, h[k], mv, rstd1, GT).then_inc(xh_ready, 1)
                dve.wait_ge(rstd2_ready, r + 1)
                dve.wait_ge(z_free[k], h_ * (16 * TOPK * GT) + 16 - (0 if k == 1 or nt == 1 else 16 * TOPK * (GT - 1)))
                normalise(z[k], h2, mv2, rstd2[:, GT:2 * GT], nt).then_inc(z_ready, 1)
                link(dve.tensor_scalar(rs1[:, 0:nt], rstd2[:, 0:nt], 1.0, None, ALU.add))
                settle(link(dve.tensor_tensor(rs2[:, 0:nt], mv2[:, 0:nt, 0], rstd2[:, 0:nt], ALU.mult)))
                dve.tensor_scalar(rs2[:, 0:nt], rs2[:, 0:nt], -1.0, 0.5, ALU.mult, ALU.add).then_inc(rs_ready, 1)
                if attn:
                    dve.wait_ge(xh_ready, r + 1)
                    dve.scalar_tensor_tensor(out=vp[:, :, :], in0=xh[:, :, :], scalar=cst[:, C_KEEP:C_KEEP + 1],
                                             in1=bc(vcls[:, :].unsqueeze(1), [P, GT, D]), op0=ALU.mult,
                                             op1=ALU.add).then_inc(vp_ready, 1)
                    if ahead:
                        x_low(r + 1, 1 - k, XR)
                    dve.wait_ge(s_done, r + 1)
                    for i in range(2):
                        q = slice(i * SEQ, (i + 1) * SEQ)
                        ins = dve.tensor_tensor(s_t[q], s_ps[q, :, q], mask3[q], ALU.mult)
                    s_step = link(ins)
                dve.wait_ge(l_done, r + 1)
                lg_step = link(dve.tensor_tensor(lg[:, 0:nt], l_ps[:, 0:nt], bc(rb[:, :].unsqueeze(1), [P, nt, E]), ALU.add))
                if attn:
                    settle(s_step)
                    s_step = link(dve.tensor_reduce(mx[:, :], s_t[:, :, :], AX.X, ALU.max))
                settle(lg_step)
                plain(dve)
                for t in range(nt):
                    ins = dve.max(m8[:, t], lg[:, t])
                m8_step = link(ins)
                if attn:
                    settle(s_step)
                    dve.tensor_tensor(s_t[:, :, :], s_t[:, :, :], bc(mx[:, :].unsqueeze(2), [P, GT, SEQ]),
                                      ALU.subtract).then_inc(smax_ready, 1)
                settle(m8_step)
                plain(dve)
                for t in range(nt):
                    ins = dve.max_index(i8[:, t], m8[:, t], lg[:, t])
                i8_step = link(ins)
                top = m8[:, 0:nt, 0:1]
                dve.tensor_tensor(d18[:, 0:nt, 0:E], lg[:, 0:nt], bc(top, [P, nt, E]), ALU.subtract)
                dve.tensor_tensor(d18[:, 0:nt, E:E + TOPK], m8[:, 0:nt, 0:TOPK], bc(top, [P, nt, TOPK]),
                                  ALU.subtract).then_inc(gate_ready, 1)
                settle(i8_step)
                settle(link(dve.tensor_copy(i2[:, 0:nk].rearrange("p (t k) -> p t k", k=TOPK), i8[:, 0:nt, 0:TOPK])))
                settle(link(dve.tensor_tensor(oh[:, 0:nk], bc(iota.unsqueeze(1), [P, nk, E]),
                                              bc(i2[:, 0:nk].unsqueeze(2), [P, nk, E]), ALU.is_equal)))
                oh4 = oh[:, 0:nk].rearrange("p (t k) e -> p t k e", k=TOPK)
                dve.tensor_tensor(m2[:, 0:nt], oh4[:, :, 0], oh4[:, :, 1], ALU.add).then_inc(m2_ready, 1)
                if attn:
                    dve.wait_ge(e_ready, r + 1)
                    sm_step = link(dve.tensor_reduce(sm[:, :], e_t[:, :, :], AX.X, ALU.add))
                    e_step = link(dve.tensor_tensor(s_t[:, :, :], e_t[:, :, :], mask3, ALU.mult))
                    settle(sm_step)
                    settle(link(dve.reciprocal(rsm[:, :], sm[:, :])))
                    settle(e_step)
                    for i in range(2):
                        q = slice(i * SEQ, (i + 1) * SEQ)
                        ins = dve.tensor_tensor(a_bd[q, :, q], s_t[q], bc(rsm[q, :].unsqueeze(2), [SEQ, GT, SEQ]), ALU.mult)
                    ins.then_inc(a_ready, 1)
                    if ahead > 1:
                        x_low(r + 2, k, 0)
                dve.wait_ge(gexp_ready, r + 1)
                gsm_step = link(dve.tensor_reduce(gsm[:, 0:nt], d18[:, 0:nt, 0:E], AX.X, ALU.add))
                dve.wait_ge(p_done, r + 1)
                base4 = bc(base[:, :].unsqueeze(1), [P, nt, E])
                for s in range(TOPK):
                    ins = dve.tensor_tensor(pp[:, 0:nt, s], p_ps[:, 0:nt], base4, ALU.add)
                pp_step = link(ins)
                settle(gsm_step)
                gsm_step = link(dve.reciprocal(rgsm[:, 0:nt], gsm[:, 0:nt]))
                settle(pp_step)
                link(dve.tensor_tensor(base[:, :], base[:, :], p_ps[:, nt], ALU.add))
                pk = pp[:, 0:nt].rearrange("p t k e -> p (t k) e")
                pp_step = link(dve.tensor_tensor(pk, pk, oh[:, 0:nk], ALU.mult))
                settle(gsm_step)
                w_out = w_all[:, bass.ds(slot, nk)].rearrange("p (t k) -> p t k", k=TOPK)
                dve.tensor_tensor(w_out, d18[:, 0:nt, E:E + TOPK], bc(rgsm[:, 0:nt].unsqueeze(2), [P, nt, TOPK]), ALU.mult)
                settle(pp_step)
                settle(link(dve.tensor_reduce(posf[:, 0:nk], pk, AX.X, ALU.add)))
                dve.tensor_copy(pos_all[:, bass.ds(slot, nk)], posf[:, 0:nk])
                dve.tensor_copy(posg[k][:, 0:nk], posf[:, 0:nk]).then_inc(pos_ready, 1)
                assert m[0] == A_STEPS * attn + R_STEPS, m[0]

            x_low(1, 1, 0)
            body(0, 0, 0, nt=1)
            groups(dve, 1, GROUPS - 3, body)
            one(body, GROUPS - 3)
            body(GROUPS - 2, 0, GROUPS // 2 - 1, ahead=1)
            body(GROUPS - 1, 1, GROUPS // 2 - 1, ahead=0)
            body(GROUPS, 0, GROUPS // 2, attn=False)
            dve.wait_ge(dve_step, GROUPS * DVE_STEPS + R_STEPS)
            dve.tensor_copy(tail[:, :], base[0:1, :]).then_inc(tail_ready, 1)
            n[0] = 0

            def tlink(ins):
                n[0] += 1
                ins.then_inc(tab_step, 1)
                dve.wait_ge(tab_step, n[0])

            ebase = cst[:, C_BASE:C_BASE + E]
            tlink(dve.tensor_tensor(cnt[:, :], base[:, :], ebase, ALU.subtract))
            tlink(dve.tensor_scalar(cnti[:, :], cnt[:, :], float(EROWS - 1), None, ALU.add))
            tlink(dve.tensor_scalar(nti[:, :], cnti[:, :], EROWS.bit_length() - 1, None, ALU.arith_shift_right))
            tlink(dve.tensor_copy(nt[:, :], nti[:, :]))
            tlink(dve.memset(dsh[:, :], 0.0))
            tlink(dve.tensor_scalar(dsh[:, 1:E], nt[:, 0:E - 1], float(EROWS), float(-CAP), ALU.mult, ALU.add))
            tlink(dve.tensor_tensor_scan(cum[:, :], one_e[:, :], nt[:, :], 0.0, ALU.mult, ALU.add))
            tlink(dve.tensor_scalar(cmp[:, :], cum[:, :], cst[:, C_TILE:C_TILE + 1], None, ALU.is_le))
            tlink(dve.tensor_reduce(ejt[:, 0:1], cmp[:, :], AX.X, ALU.add))
            tlink(dve.tensor_tensor(cmp[:, :], cmp[:, :], nt[:, :], ALU.mult))
            tlink(dve.tensor_reduce(tj[:, :], cmp[:, :], AX.X, ALU.add))
            tlink(dve.tensor_scalar(tj[:, :], tj[:, :], cst[:, C_TILE:C_TILE + 1], float(-EROWS), ALU.subtract, ALU.mult))
            dve.scalar_tensor_tensor(out=ejt[:, 1:2], in0=ejt[:, 0:1], scalar=float(CAP), in1=tj[:, :], op0=ALU.mult,
                                     op1=ALU.add).then_inc(ejt_ready, 1)
            dve.wait_ge(tej_done, 1)
            tlink(dve.tensor_scalar(ejc[:, :], bank[6][0:1, 0:EXPERT_TILES], float(E - 1), None, ALU.min))
            dve.tensor_copy(rowj[:, :], bank[6][0:1, P:P + EXPERT_TILES]).then_inc(tab_ready, 1)
            grid = [P, TILES * TOPK, E]
            dve.tensor_tensor(past, bc(pos_all[:, :].unsqueeze(2), grid), bc(ebase.unsqueeze(1), grid), ALU.is_ge)\
               .then_inc(past_ready, 1)

            dve.wait_ge(tab_ready, 1)

            def down_bias(j, n):
                ex = dve.value_load(ejc[0:1, bass.ds(j, 1)], min_val=0, max_val=E - 1)
                bias = cols[:, bass.ds(ex + V_EB2, 1)]
                dve.wait_ge(down_done, j + 1)
                dve.tensor_scalar(eyT[n % 2], bank[5 + n % 2][:, 0:EROWS], bias, None, ALU.add).then_inc(eyT_ready, 1)

            def rows_out(j, n, h_):
                if n > 1:
                    dve.wait_ge(y_free[n % 2], h_ * 16)
                dve.wait_ge(tout_done, j + 1)
                dve.tensor_copy(yout[n % 2], bank[7][:, 0:EROWS].rearrange("p (h d) -> p h d", h=EH)).then_inc(yout_ready, 1)

            def split_w1(j, n, h):
                dve.wait_ge(up_done, j * EC - EC) if n > 1 else None
                dve.wait_ge(w1_loaded[n % 4], h * 16 + 16)
                dve.tensor_copy(w1h[n % 2], w1b[n % 4]).then_inc(w1h_ready, 1)
                dve.wait_ge(w1h_ready, j + 1)
                dve.tensor_tensor(w1l[n % 2], w1b[n % 4], w1h[n % 2], ALU.subtract).then_inc(w1l_ready, 1)

            def split_rows(j, n):
                dve.wait_ge(up_done, j * EC - EC) if n > 1 else None
                dve.wait_ge(h2T_ready, j + 1)
                dve.tensor_copy(h2h[n % 2], h2T[n % 2]).then_inc(h2h_ready, 1)
                dve.wait_ge(h2h_ready, j + 1)
                dve.tensor_tensor(h2l[n % 2], h2T[n % 2], h2h[n % 2], ALU.subtract).then_inc(h2l_ready, 1)

            def step2(j, n, q=0):
                static = isinstance(j, int)
                if not static or j + 1 < EXPERT_TILES:
                    split_rows(j + 1, n + 1)
                if n >= 2:
                    rows_out(j - 2, n - 2, q * 2 + (n - 2) // 2)
                if not static or j + 2 < EXPERT_TILES:
                    split_w1(j + 2, n + 2, q + (n + 2) // 4)
                if n >= 1 and not (static and j > EXPERT_TILES):
                    down_bias(j - 1, n - 1)

            split_rows(0, 0)
            split_w1(0, 0, 0)
            split_w1(1, 1, 0)
            for j in range(4):
                step2(j, j)
            dve.wait_ge(shift_ready, 1)
            tlink(dve.tensor_reduce(shift[:, :], past, AX.X, ALU.add))
            tlink(dve.tensor_tensor(pos_all[:, :], pos_all[:, :], shift[:, :], ALU.add))
            dve.wait_ge(w3_loaded, 64)
            for w, high, low in ((fw1_t, fw1h, fw1l), (sw1_t, sw1h, sw1l)):
                tlink(dve.tensor_copy(high, w))
                dve.tensor_tensor(low, w, high, ALU.subtract).then_inc(fw_parts, 1)
            with dve.Fori(1, EXPERT_TILES // 4 - 1) as i:
                for n in range(4):
                    step2(i * 4 + n, 4 + n, i - 1)
            for j in range(EXPERT_TILES - 4, EXPERT_TILES + 2):
                step2(j, j)

            def copy_idx(q, k, nt=GT):
                dve.tensor_copy(gidx[k][:, 0:nt * TOPK], pos_all[:, bass.ds(q * (GT * TOPK), nt * TOPK)]).then_inc(idx_ready, 1)

            tsh = tiles_of(6)

            def add_rows(q, k, s, nt, done):
                for t in range(nt):
                    w = w_all[:, bass.ds(q * (GT * TOPK) + (t * TOPK + s), 1)]
                    ins = dve.scalar_tensor_tensor(out=moe[:, t], in0=gat[k][:, t, s], scalar=w,
                                                   in1=tsh[:, t] if s == 0 else moe[:, t], op0=ALU.mult, op1=ALU.add)
                ins.then_inc(done, 1)

            def mix0(q, k, h_, nt=GT):
                dve.wait_ge(gathered[0][k], h_ * (16 * GT) + 16 * nt)
                dve.wait_ge(tsh_done, q + 1)
                if not (isinstance(q, int) and q == 0):
                    dve.wait_ge(z4_ready, q)
                add_rows(q, k, 0, nt, mix0_done)

            def step_of(q, at):
                dve.wait_ge(dve_step3, q * DVE_STEPS3 + at)

            def mix1(q, k, h_, nt=GT):
                dve.wait_ge(gathered[1][k], h_ * (16 * GT) + 16 * nt)
                dve.wait_ge(mix0_done, q + 1)
                add_rows(q, k, 1, nt, mix_done)

            def mix_stats(q, nt=GT):
                dve.wait_ge(mix_done, q + 1)
                for t in range(nt):
                    ins = dve.bn_stats(st[:, t], moe[:, t])
                ins.then_inc(dve_step3, 1)

            def norm(q, nt=GT):
                step_of(q, 1)
                plain(dve)
                for t in range(nt):
                    ins = dve.bn_aggr(mv[:, t], st[:, t])
                ins.then_inc(dve_step3, 1)
                step_of(q, 2)
                dve.tensor_scalar(var1[:, 0:nt], mv[:, 0:nt, 1], EPS, None, ALU.add).then_inc(var4_ready, 1)
                res = r_res[:, bass.ds(q * GTOK, nt * D)].rearrange("p (t d) -> p t d", t=nt)
                dve.tensor_tensor(res, res, moe[:, 0:nt], ALU.add).then_inc(dve_step3, 1)

            def h4_low(q, nt=GT):
                dve.wait_ge(h4T_ready, q + 1)
                dve.tensor_tensor(h4l[:, 0:nt * P], h4T[:, 0:nt * P], h4h[:, 0:nt * P], ALU.subtract).then_inc(h4l_ready, 1)

            def z_out(q, nt=GT):
                dve.wait_ge(rstd4_ready, q + 1)
                if not (isinstance(q, int) and q == 0):
                    dve.wait_ge(tz_done, q)
                normalise(z4, moe, mv, rstd1, nt).then_inc(z4_ready, 1)
                step_of(q, 3)

            def out3(q, nt=GT):
                dve.wait_ge(tout3_done, q + 1)
                res = r_res[:, bass.ds(q * GTOK, nt * D)].rearrange("p (t d) -> p t d", t=nt)
                dve.tensor_tensor(res, tiles_of(7)[:, 0:nt], res, ALU.add).then_inc(out_ready, 1)

            def ht_low(q, k, nt=GT):
                dve.wait_ge(hth_ready, q + 1)
                dve.tensor_tensor(htl[:, 0:nt * P], ht3[k][:, 0:nt * P], hth[:, 0:nt * P], ALU.subtract).then_inc(htl_ready, 1)

            def step3(q, k, h_, out=GT, m1=GT, m2=GT, m3=GT, sh3=GT):
                if m1:
                    norm(q + 1, m1)
                if out:
                    out3(q - 1, out)
                if m1:
                    z_out(q + 1, m1)
                if m3:
                    copy_idx(q + 3, 1 - k, m3)
                if sh3:
                    ht_low(q + 3, 1 - k, sh3)
                if m2:
                    mix0(q + 2, k, h_ + 1, m2)
                    mix1(q + 2, k, h_ + 1, m2)
                if m1:
                    h4_low(q + 1, m1)
                if m2:
                    mix_stats(q + 2, m2)

            dve.sem_inc(out_ready, 1)
            copy_idx(0, 0)
            copy_idx(1, 1)
            dve.wait_ge(r_loaded, 16 * (GROUPS + 1))
            ht_low(0, 0)
            ht_low(1, 1)
            mix0(0, 0, 0)
            ht_low(2, 0)
            mix1(0, 0, 0)
            mix_stats(0)
            norm(0)
            z_out(0)
            copy_idx(2, 0)
            h4_low(0)
            mix0(1, 1, 0)
            mix1(1, 1, 0)
            mix_stats(1)
            step3(0, 0, 0, out=0)
            groups(dve, 1, GROUPS - 3, step3)
            step3(GROUPS - 3, 1, GROUPS // 2 - 2, m3=1, sh3=1)
            step3(GROUPS - 2, 0, GROUPS // 2 - 1, m2=1, m3=0, sh3=0)
            step3(GROUPS - 1, 1, GROUPS // 2 - 1, m1=1, m2=0, m3=0, sh3=0)
            step3(GROUPS, 0, GROUPS // 2, m1=0, m2=0, m3=0, sh3=0)
            out3(GROUPS, 1)

        @block.tensor
        def _(pe):
            pe.wait_ge(ld_id, 16)
            pe.wait_ge(memset_done, 2)
            pe.wait_ge(ld_w, 16)
            for px in range(PATCH):
                ins = pe.transpose(bank[px // 4][0:KROWS, (px % 4) * P:(px % 4 + 1) * P],
                                   wnat[:, :, :, px].rearrange("h c y -> h (c y)"), ident)
                if px % 4 == 3:
                    ins.then_inc(wp_t, 1)
            pe.wait_ge(wp_ready, PATCH // 4)
            WARM = 3

            def patch(g, k, h, lo, hi):
                if lo == 0:
                    pe.wait_ge(x_loaded[k], h * (16 * XLOADS) + 16 * XLOADS)
                for n in range(lo, hi):
                    px = PX_ORDER[n]
                    if px >= XS or (isinstance(g, int) and g == 0):
                        ins = pe.matmul(pa[:, :], wp[:, px], pixels(k, px), start=n == 0, stop=n == PATCH - 1)
                        continue
                    pe.wait_ge(xlo_ready, (g - 1) * XS + (px + 1))
                    u = px % XR
                    pe.matmul(pa[:, :], wph[:, px], xhi[u], start=n == 0, stop=False)
                    pe.matmul(pa[:, :], wph[:, px], xlo[u], start=False, stop=False)
                    pe.matmul(pa[:, :], wpl[:, px], xhi[u], start=False, stop=False).then_inc(xparts_used, 1)
                if hi == PATCH:
                    ins.then_inc(patch_done, 1)

            def transposes(dst, src, nt, done):
                for t in range(nt):
                    ins = pe.transpose(dst(t), src(t), ident)
                ins.then_inc(done, 1)

            def scores(g):
                pe.wait_ge(xT_ready, g + 1)
                for t in range(GT):
                    ins = pe.matmul(s_ps[:, t], xT[:, t * P:(t + 1) * P],
                                    xs[:, 2 * t:2 * t + 2].rearrange("p i s -> p (i s)"), start=True, stop=True)
                ins.then_inc(s_done, 1)

            def context(g):
                pe.wait_ge(vp_ready, g + 1)
                pe.wait_ge(aT_ready, g + 1)
                for t in range(GT):
                    ins = pe.matmul(c_ps[:, t * P:(t + 1) * P], vp[:, t], aT[:, t * P:(t + 1) * P], start=True, stop=True)
                ins.then_inc(c_done, 1)

            def t_th(g, nt=GT):
                pe.wait_ge(th_ready, g + 1)
                transposes(lambda t: t4[:, t], lambda t: th[:, t * P:(t + 1) * P], nt, t4_done)

            def t_zz(g, k, nt=GT):
                pe.wait_ge(z_ready, g + 1)
                transposes(lambda t: t5[:, t * P:(t + 1) * P], lambda t: z[k][:, t], nt, t5_done)

            def gates(g, k, nt=GT):
                pe.wait_ge(hT_ready, g + 1)
                for t in range(nt):
                    ins = pe.matmul(l_ps[:, t], hT[k][:, t * P:(t + 1) * P], rw[:, :], start=True, stop=True)
                ins.then_inc(l_done, 1)

            def ranks(g, nt=GT):
                pe.wait_ge(m2_ready, g + 1)
                pe.matmul(p_ps[:, 0:nt], pref[:, :], m2[:, 0:nt], start=True, stop=False)
                ins = pe.matmul(p_ps[:, nt], ones[:, :], m2[:, nt - 1], start=False, stop=nt == 1)
                for s in range(nt - 1):
                    if s == 0:
                        pe.matmul(p_ps[:, 1:nt], ones[:, :], m2[:, 0:nt - 1], start=False, stop=False)
                    else:
                        pe.matmul(p_ps[:, 1 + s:nt + 1], ones[:, :], m2[:, 0:nt - s], start=False, stop=False)
                if nt > 1:
                    ins = pe.matmul(p_ps[:, nt], ones[:, :], m2[:, 0], start=False, stop=True)
                ins.then_inc(p_done, 1)

            CUT = [1, 12, 14, 24, PATCH]

            def body(g, k, h, ahead=True, nt=GT):
                slot = [0, 0]

                def patches():
                    if ahead:
                        patch(g + 1, 1 - k, h + k, slot[1], CUT[slot[0]])
                    slot[:] = slot[0] + 1, CUT[slot[0]]

                pe.wait_ge(hF_ready, g + 1)
                transposes(lambda t: t1[:, t], lambda t: hF[:, t * P:(t + 1) * P], GT, t1_done)
                patches()
                t_th(g, nt)
                patches()
                pe.wait_ge(xh_ready, g + 1)
                transposes(lambda t: t2[:, t * P:(t + 1) * P], lambda t: xh[:, t], GT, t2_done)
                t_zz(g, k, nt)
                patches()
                scores(g)
                gates(g, k, nt)
                patches()
                ranks(g, nt)
                pe.wait_ge(a_ready, g + 1)
                transposes(lambda t: t3[:, t * P:(t + 1) * P], lambda t: a_bd[:, t], GT, t3_done)
                patches()
                context(g)
                pe.matmul(w_ps[:, :], wc[:, 1], xT[:, :], start=True, stop=False)
                pe.wait_ge(cT_ready, g + 1)
                pe.matmul(w_ps[:, :], wc[:, 0], cT[:, :], start=False, stop=True).then_inc(w_done, 1)

            for _ in range(WARM):
                pe.matmul(bank[1][:, :], a_bd[:, 0], a_bd[:, :].rearrange("p t d -> p (t d)"), start=True, stop=True)
            patch(0, 0, 0, 0, 20)
            pe.wait_ge(ld_const, 16 * N_LOADS)
            pe.transpose(bank[7][:, 0:V_END], vecs[:, :], ident[0:V_END, 0:V_END]).then_inc(setup_t, 1)
            patch(0, 0, 0, 20, 23)
            pe.wait_ge(cols_ready, 1)
            pe.wait_ge(xcls_ready, 1)
            pe.transpose(bank[7][:, P:2 * P], xcls[:, :], ident).then_inc(setup_t, 1)
            patch(0, 0, 0, 23, 26)
            pe.wait_ge(xclsT_ready, 1)
            pe.matmul(w_ps[:, 0:P], wc[:, 1], xclsT[:, :], start=True, stop=True).then_inc(w_done, 1)
            patch(0, 0, 0, 26, PATCH)
            pe.wait_ge(wpl_ready, 1)
            body(0, 0, 0, nt=1)
            groups(pe, 1, GROUPS - 1, body)
            body(GROUPS - 1, 1, GROUPS // 2 - 1, ahead=False)
            t_th(GROUPS)
            t_zz(GROUPS, 0)
            gates(GROUPS, 0)
            ranks(GROUPS)
            pe.wait_ge(ejt_ready, 1)
            for c in range(2):
                ins = pe.transpose(bank[6][0:1, c * P:(c + 1) * P], ejt[:, c:c + 1], ident)
            ins.then_inc(tej_done, 1)


            def t_in(j, n, h):
                pe.wait_ge(zin_loaded[n % 4], h * 16 + 16)
                if n > 0:
                    pe.wait_ge(h2T_ready, j)
                for i in range(EH):
                    ins = pe.transpose(bank[0][:, i * P:(i + 1) * P], zin[n % 4][:, i], ident)
                ins.then_inc(tin_done, 1)

            def t_out(j, n):
                pe.wait_ge(eyT_ready, j + 1)
                if n > 0:
                    pe.wait_ge(yout_ready, j)
                for i in range(EH):
                    ins = pe.transpose(bank[7][:, i * P:(i + 1) * P], eyT[n % 2][:, i * P:(i + 1) * P], ident)
                ins.then_inc(tout_done, 1)

            def up(j, n, h):
                pe.wait_ge(h2l_ready, j + 1)
                pe.wait_ge(w1l_ready, j + 1)
                terms = ((w1h, h2h), (w1h, h2l), (w1l, h2h))
                for c in range(EC):
                    if n > 0:
                        pe.wait_ge(eh_ready, j * EC + (c + 1 - EC))
                    for i, (w, v) in enumerate(terms):
                        ins = pe.matmul(bank[1 + c][:, 0:EROWS], w[n % 2][:, c * P:(c + 1) * P], v[n % 2],
                                        start=i == 0, stop=i == len(terms) - 1)
                    ins.then_inc(up_done, 1)

            def down(j, n, h):
                pe.wait_ge(w2_loaded[n % 4], h * 16 + 16)
                for c in range(EC):
                    pe.wait_ge(eh_ready, j * EC + c + 1)
                    ins = pe.matmul(bank[5 + n % 2][:, 0:EROWS], w2b[n % 4][:, c], ehT[n % 2][:, c],
                                    start=c == 0, stop=c == EC - 1)
                ins.then_inc(down_done, 1)

            def step2(j, n, h, first=0):
                if not (isinstance(j, int) and j + 1 >= EXPERT_TILES):
                    t_in(j + 1, n + 1, h + (n % 4 + 1) // 4)
                if not (isinstance(j, int) and j >= EXPERT_TILES):
                    up(j, n, h)
                if n - 2 >= first:
                    t_out(j - 2, n - 2)
                if n - 1 >= first and not (isinstance(j, int) and j > EXPERT_TILES):
                    down(j - 1, n - 1, h - (n % 4 == 0))

            t_in(0, 0, 0)
            for j in range(4):
                step2(j, j, 0)
            with pe.Fori(1, EXPERT_TILES // 4 - 1) as i:
                for n in range(4):
                    step2(i * 4 + n, 4 + n, i)
            for j in range(EXPERT_TILES - 4, EXPERT_TILES + 2):
                step2(j, j, j // 4)


            def in_parts(dst, c, terms, nt):
                for i, (w, v) in enumerate(terms):
                    ins = pe.matmul(dst, w[:, c * P:(c + 1) * P], v[:, 0:nt * P], start=i == 0, stop=i == len(terms) - 1)
                ins.then_inc(u_done, 1)

            def sh_up(q, n, nt=GT):
                pe.wait_ge(htl_ready, q + 1)
                for c in range(SC):
                    if not (isinstance(n, int) and n + c < 3):
                        pe.wait_ge(u_used, n + c - 2)
                    in_parts(bank[(4 + c) % 3][:, 0:nt * P], c, ((sw1h, hth), (sw1h, htl), (sw1l, hth)), nt)

            def sh_down(q, n, nt=GT):
                pe.wait_ge(u_used, n)
                for c in range(SC):
                    ins = pe.matmul(bank[3][:, 0:nt * P], sw2_t[:, c], shs[:, c, 0:nt * P], start=c == 0, stop=c == SC - 1)
                ins.then_inc(shd_done, 1)

            def t_sh(q, nt=GT):
                pe.wait_ge(shF_ready, q + 1)
                transposes(lambda t: bank[6][:, t * P:(t + 1) * P], lambda t: shF[:, t * P:(t + 1) * P], nt, tsh_done)

            def t_z(q, nt=GT):
                pe.wait_ge(z4_ready, q + 1)
                transposes(lambda t: bank[5][:, t * P:(t + 1) * P], lambda t: z4[:, t], nt, tz_done)

            def ff_up(q, n, nt=GT):
                pe.wait_ge(h4l_ready, q + 1)
                for c in range(EC):
                    if c > 1:
                        pe.wait_ge(u_used, n + (c - 3))
                    in_parts(bank[FF_BANK[c]][:, 0:nt * P], c, ((fw1h, h4h), (fw1h, h4l), (fw1l, h4h)), nt)

            def ff_down(q, n, nt, sh2, z1):
                for c in range(EC):
                    pe.wait_ge(u_used, n + c + 1)
                    ins = pe.matmul(bank[4][:, 0:nt * P], fw2_t[:, c], ffs[:, c, 0:nt * P], start=c == 0, stop=c == EC - 1)
                    if c == 0 and sh2:
                        pe.wait_ge(mix0_done, q + 2)
                        t_sh(q + 2, sh2)
                    if c == 1 and z1:
                        t_z(q + 1, z1)
                ins.then_inc(ffd_done, 1)

            def t_out3(q, nt=GT):
                pe.wait_ge(oF_ready, q + 1)
                pe.wait_ge(out_ready, q + 1)
                transposes(lambda t: bank[7][:, t * P:(t + 1) * P], lambda t: oF[:, t * P:(t + 1) * P], nt, tout3_done)

            pe.wait_ge(w3_loaded, 64)
            pe.wait_ge(fw_parts, 2)
            for q in range(3):
                if q > 0:
                    pe.wait_ge(u_used, SC * q)
                sh_up(q, SC * q if q == 0 else SC * q + 1)
                if q < 2:
                    sh_down(q, SC * (q + 1))
                    if q == 1:
                        pe.wait_ge(mix0_done, 1)
                    t_sh(q)
            t_z(0)

            def step3(q, k, h, sh3=GT, sh2=GT, z1=GT, now=GT, n=None):
                n = q * 6 + 6 if n is None else n
                ff_up(q, n, now)
                if sh2:
                    sh_down(q + 2, n, sh2)
                ff_down(q, n, now, sh2, z1)
                if sh3:
                    sh_up(q + 3, n + 4, sh3)
                t_out3(q, now)

            groups(pe, 0, GROUPS - 4, step3)
            one(step3, GROUPS - 4)
            step3(GROUPS - 3, 1, (GROUPS - 3) // 2, sh3=1)
            last = (GROUPS - 3) * 6 + 12
            step3(GROUPS - 2, 0, (GROUPS - 2) // 2, sh3=0, sh2=1, n=last)
            step3(GROUPS - 1, 1, (GROUPS - 1) // 2, sh3=0, sh2=0, z1=1, n=last + EC)
            step3(GROUPS, 0, GROUPS // 2, sh3=0, sh2=0, z1=0, now=1, n=last + 2 * EC)


_INS = ["x", "L0_tok_W", "L0_tok_b", "L0_tok_class_token", "L0_tok_pos_embed", "L0_attn_W_c", "L0_ffn_ln_in_g",
        "L0_ffn_ln_in_b", "L0_ffn_router_w", "L0_ffn_router_b", "L0_ffn_ew1", "L0_ffn_eb1", "L0_ffn_ew2", "L0_ffn_eb2",
        "L0_ffn_sw1", "L0_ffn_sb1", "L0_ffn_sw2", "L0_ffn_sb2", "L0_ffn_ff_ln_g", "L0_ffn_ff_ln_b", "L0_ffn_ff_w1",
        "L0_ffn_ff_b1", "L0_ffn_ff_w2", "L0_ffn_ff_b2"]


def kernel(**inputs):
    import numpy as _np
    import concourse.bacc as _bacc
    from concourse import mybir as _mybir
    from concourse.bass_utils import run_bass_kernel_spmd as _run

    nc = _bacc.Bacc("TRN2", target_bir_lowering=False, num_devices=1)
    arrays, args = {"consts": constants()}, []
    for name in _INS:
        arrays[f"in_{name}"] = _np.ascontiguousarray(inputs[name])
    for name, a in arrays.items():
        args.append(nc.dram_tensor(name, a.shape, _mybir.dt.from_np(a.dtype), kind="ExternalInput").ap())
    out = nc.dram_tensor("out_0", (BATCH, SEQ + 1, D), _mybir.dt.float32, kind="ExternalOutput").ap()
    build(nc, *args, out)
    r = _run(nc, [arrays], core_ids=[0])
    return r.results[0]["out_0"]
```
